# Optimizing a Trainium2 kernel written in Bass

```python
import numpy as np
import jax
import jax.numpy as jnp

def _softmax(x, axis=-1):
    return jax.nn.softmax(x, axis=axis)

def _gelu(x):
    return jax.nn.gelu(x, approximate=True)

def _silu(x):
    return jax.nn.silu(x)

def _sigmoid(x):
    return jax.nn.sigmoid(x)

def _layernorm(x, axis=-1, eps=1e-05):
    m = jnp.mean(x, axis=axis, keepdims=True)
    v = jnp.var(x, axis=axis, keepdims=True)
    return (x - m) / jnp.sqrt(v + eps)

def _scatter_add(tgt, idx, src, axis=0):
    return tgt.at[idx].add(src)

def _segment_sum(src, seg, n):
    return jax.ops.segment_sum(src, seg, n)
kernel_name = 'mk_gps_d1_gnn_r8_e74e28'

def setup_inputs(seed: int=0):
    np.random.seed(seed)
    _w = jnp.asarray

    def _rec_inputs():
        import jax
        import jax.numpy as jnp
        _gk = jax.random.key(seed)
        x = -0.0003713 + 1 * jax.random.normal(jax.random.fold_in(_gk, 1), (6250, 256), jnp.float32)
        _s = jax.random.randint(jax.random.fold_in(_gk, 2), (50000,), 0, 6250, jnp.int32)
        _d = jax.random.randint(jax.random.fold_in(_gk, 3), (50000,), 0, 6250, jnp.int32)
        _loop = jnp.arange(6250, dtype=jnp.int32)
        src = jnp.concatenate([_s, _d, _loop])
        dst = jnp.concatenate([_d, _s, _loop])
        _o = jnp.argsort(dst, stable=True)
        src = src[_o]
        dst = dst[_o]
        edge_attr_16 = 0.000196303 + 1.00016 * jax.random.normal(jax.random.fold_in(_gk, 11), (106250, 16), jnp.float32)
        return (x, src, dst, edge_attr_16)
    x, src, dst, edge_attr_16 = _rec_inputs()

    def _L0_gnn_setup():
        import jax, jax.numpy as jnp
        import numpy as np
        N_NODES = 6250
        key = jax.random.key(seed)
        ks = jax.random.split(key, 6)
        d_in, d_out = (256, 256)
        n_edges = 200000
        x = jax.random.normal(ks[0], (N_NODES, d_in), dtype=jnp.float32)
        edge_index = jax.random.randint(ks[1], (2, n_edges), 0, N_NODES, dtype=jnp.int64)
        edge_attr = jax.random.normal(ks[2], (n_edges, 16), dtype=jnp.float32)
        W1 = jax.random.normal(ks[3], (d_in, d_out), dtype=jnp.float32) * (1.0 / np.sqrt(d_in))
        b1 = jnp.zeros((d_out,), dtype=jnp.float32)
        W2 = jax.random.normal(ks[4], (d_out, d_out), dtype=jnp.float32) * (1.0 / np.sqrt(d_out))
        b2 = jnp.zeros((d_out,), dtype=jnp.float32)
        eps = jnp.zeros((1,), dtype=jnp.float32)
        return {'x': x, 'edge_index': edge_index, 'edge_attr': edge_attr, 'W1': W1, 'b1': b1, 'W2': W2, 'b2': b2, 'eps': eps}
    _L0_gnn_all = _L0_gnn_setup()
    _L0_gnn_in = {k: v for k, v in _L0_gnn_all.items() if k in ('W1', 'b1', 'W2', 'b2', 'eps')}
    del _L0_gnn_all

    def _L0_mix_setup():
        import jax, jax.numpy as jnp
        import numpy as np
        D_MODEL = 256
        NUM_HEADS = 8
        DEPTH = D_MODEL // NUM_HEADS
        B, L = (32, 512)

        def _feature_map(x):
            return jax.nn.elu(x) + 1.0
        key = jax.random.key(seed)
        ks = jax.random.split(key, 9)
        sc = 1.0 / np.sqrt(D_MODEL)
        return {'x': jax.random.normal(ks[0], (B, L, D_MODEL), dtype=jnp.float32), 'wq': jax.random.normal(ks[1], (D_MODEL, D_MODEL), dtype=jnp.float32) * sc, 'bq': jnp.zeros((D_MODEL,), dtype=jnp.float32), 'wk': jax.random.normal(ks[2], (D_MODEL, D_MODEL), dtype=jnp.float32) * sc, 'bk': jnp.zeros((D_MODEL,), dtype=jnp.float32), 'wv': jax.random.normal(ks[3], (D_MODEL, D_MODEL), dtype=jnp.float32) * sc, 'bv': jnp.zeros((D_MODEL,), dtype=jnp.float32), 'wo': jax.random.normal(ks[4], (D_MODEL, D_MODEL), dtype=jnp.float32) * sc, 'bo': jnp.zeros((D_MODEL,), dtype=jnp.float32)}
    _L0_mix_all = _L0_mix_setup()
    _L0_mix_in = {k: v for k, v in _L0_mix_all.items() if k in ('wq', 'bq', 'wk', 'bk', 'wv', 'bv', 'wo', 'bo')}
    del _L0_mix_all

    def _L0_ffn_setup():
        import jax, jax.numpy as jnp
        import numpy as np
        NUM_EXPERTS = 8
        TOP_K = 2
        B, S, D = (8, 1024, 256)

        def _moe(tokens, router_w, w1, b1, w2, b2):
            N = tokens.shape[0]
            E = router_w.shape[0]
            logits = tokens.astype(jnp.float32) @ router_w.astype(jnp.float32).T
            probs = jax.nn.softmax(logits, axis=-1)
            rw, re = jax.lax.top_k(probs, TOP_K)
            if TOP_K > 1:
                rw = rw / jnp.maximum(rw.sum(-1, keepdims=True), 1e-12)
            rw = rw.astype(tokens.dtype)
            combine = jnp.zeros((N, E), tokens.dtype).at[jnp.arange(N)[:, None], re].set(rw)
            out = tokens
            for e in range(E):
                h = jax.nn.gelu(tokens @ w1[e] + b1[e], approximate=False)
                y = h @ w2[e] + b2[e]
                out = out + combine[:, e:e + 1] * y
            return out
        key = jax.random.key(seed)
        ks = jax.random.split(key, 4)
        scale = 1.0 / np.sqrt(D).astype(np.float32)
        return {'input_embeddings': jax.random.normal(ks[0], (B, S, D), jnp.float32), 'router_w': jax.random.normal(ks[1], (NUM_EXPERTS, D), jnp.float32) * scale, 'w1': jax.random.normal(ks[2], (NUM_EXPERTS, D, D), jnp.float32) * scale, 'b1': jnp.zeros((NUM_EXPERTS, D), jnp.float32), 'w2': jax.random.normal(ks[3], (NUM_EXPERTS, D, D), jnp.float32) * scale, 'b2': jnp.zeros((NUM_EXPERTS, D), jnp.float32)}
    _L0_ffn_all = _L0_ffn_setup()
    _L0_ffn_in = {k: v for k, v in _L0_ffn_all.items() if k in ('router_w', 'w1', 'b1', 'w2', 'b2')}
    del _L0_ffn_all
    return {'x': x, 'src': src, 'dst': dst, 'edge_attr_16': edge_attr_16, 'L0_gnn_W1': _L0_gnn_in['W1'], 'L0_gnn_b1': _L0_gnn_in['b1'], 'L0_gnn_W2': _L0_gnn_in['W2'], 'L0_gnn_b2': _L0_gnn_in['b2'], 'L0_gnn_eps': _L0_gnn_in['eps'], 'L0_mix_wq': _L0_mix_in['wq'], 'L0_mix_bq': _L0_mix_in['bq'], 'L0_mix_wk': _L0_mix_in['wk'], 'L0_mix_bk': _L0_mix_in['bk'], 'L0_mix_wv': _L0_mix_in['wv'], 'L0_mix_bv': _L0_mix_in['bv'], 'L0_mix_wo': _L0_mix_in['wo'], 'L0_mix_bo': _L0_mix_in['bo'], 'L0_ffn_router_w': _L0_ffn_in['router_w'], 'L0_ffn_w1': _L0_ffn_in['w1'], 'L0_ffn_b1': _L0_ffn_in['b1'], 'L0_ffn_w2': _L0_ffn_in['w2'], 'L0_ffn_b2': _L0_ffn_in['b2']}

def reference(x, src, dst, edge_attr_16, L0_gnn_W1, L0_gnn_b1, L0_gnn_W2, L0_gnn_b2, L0_gnn_eps, L0_mix_wq, L0_mix_bq, L0_mix_wk, L0_mix_bk, L0_mix_wv, L0_mix_bv, L0_mix_wo, L0_mix_bo, L0_ffn_router_w, L0_ffn_w1, L0_ffn_b1, L0_ffn_w2, L0_ffn_b2):
    import jax
    import jax.numpy as jnp

    def _L0_gnn_ref(x, edge_index, edge_attr, W1, b1, W2, b2, eps):
        import jax, jax.numpy as jnp
        import numpy as np
        N_NODES = 6250
        src, dst = (edge_index[0], edge_index[1])
        agg = jax.ops.segment_sum(x[src], dst, num_segments=N_NODES)
        h = (1.0 + eps[0]) * x + agg
        h = jax.nn.relu(h @ W1 + b1)
        out = h @ W2 + b2
        return out

    def _L0_mix_ref(x, wq, bq, wk, bk, wv, bv, wo, bo):
        import jax, jax.numpy as jnp
        import numpy as np
        D_MODEL = 256
        NUM_HEADS = 8
        DEPTH = D_MODEL // NUM_HEADS
        B, L = (32, 512)

        def _feature_map(x):
            return jax.nn.elu(x) + 1.0
        b, l, _ = x.shape
        q = (x @ wq + bq).reshape(b, l, NUM_HEADS, DEPTH)
        k = (x @ wk + bk).reshape(b, l, NUM_HEADS, DEPTH)
        v = (x @ wv + bv).reshape(b, l, NUM_HEADS, DEPTH)
        q = _feature_map(q)
        k = _feature_map(k)
        kv = jnp.einsum('blhd,blhe->bhde', k, v)
        k_sum = jnp.sum(k, axis=1)
        qkv = jnp.einsum('blhd,bhde->blhe', q, kv)
        normalizer = jnp.einsum('blhd,bhd->blh', q, k_sum) + 1e-06
        out = qkv / normalizer[..., None]
        out = out.reshape(b, l, D_MODEL)
        return out @ wo + bo

    def _L0_ffn_ref(input_embeddings, router_w, w1, b1, w2, b2):
        import jax, jax.numpy as jnp
        import numpy as np
        NUM_EXPERTS = 8
        TOP_K = 2
        B, S, D = (8, 1024, 256)

        def _moe(tokens, router_w, w1, b1, w2, b2):
            N = tokens.shape[0]
            E = router_w.shape[0]
            logits = tokens.astype(jnp.float32) @ router_w.astype(jnp.float32).T
            probs = jax.nn.softmax(logits, axis=-1)
            rw, re = jax.lax.top_k(probs, TOP_K)
            if TOP_K > 1:
                rw = rw / jnp.maximum(rw.sum(-1, keepdims=True), 1e-12)
            rw = rw.astype(tokens.dtype)
            combine = jnp.zeros((N, E), tokens.dtype).at[jnp.arange(N)[:, None], re].set(rw)
            out = tokens
            for e in range(E):
                h = jax.nn.gelu(tokens @ w1[e] + b1[e], approximate=False)
                y = h @ w2[e] + b2[e]
                out = out + combine[:, e:e + 1] * y
            return out
        b, s, d = input_embeddings.shape
        tokens = input_embeddings.reshape(b * s, d)
        return _moe(tokens, router_w, w1, b1, w2, b2).reshape(b, s, d)
    edge_index = jnp.stack([src, dst])
    xn = _layernorm(x, axis=-1)
    x = x + _L0_gnn_ref(xn, edge_index, edge_attr_16, L0_gnn_W1, L0_gnn_b1, L0_gnn_W2, L0_gnn_b2, L0_gnn_eps) + _L0_mix_ref(xn[None], L0_mix_wq, L0_mix_bq, L0_mix_wk, L0_mix_bk, L0_mix_wv, L0_mix_bv, L0_mix_wo, L0_mix_bo)[0]
    x = x + _L0_ffn_ref(_layernorm(x, axis=-1)[None], L0_ffn_router_w, L0_ffn_w1, L0_ffn_b1, L0_ffn_w2, L0_ffn_b2)[0]
    return x

_drawn_inputs = setup_inputs


def setup_inputs(seed=0):
    import zlib

    import numpy as np

    out = dict(_drawn_inputs(seed))
    spreads = {'L0_gnn_b1': (0.0, 0.296),
     'L0_gnn_b2': (0.0, 0.1),
     'L0_mix_bq': (0.0, 0.8),
     'L0_mix_bk': (0.0, 0.8),
     'L0_mix_bv': (0.0, 0.1),
     'L0_mix_bo': (0.0, 0.1),
     'L0_ffn_b1': (0.0, 0.684),
     'L0_ffn_b2': (0.0, 0.469)}
    factors = {'L0_mix_wq': 8.0, 'L0_mix_wk': 8.0, 'L0_mix_wv': 7.991}
    for name, (base, spread) in spreads.items():
        noise = np.random.default_rng([zlib.crc32(name.encode()), seed]).standard_normal(out[name].shape)
        drawn = base * np.exp(spread * noise) if base else spread * noise
        out[name] = jnp.asarray(drawn.astype(out[name].dtype))
    for name, factor in factors.items():
        out[name] = (out[name] * factor).astype(out[name].dtype)
    return out
```

```python
from contextlib import ExitStack

import concourse.bass as bass
from concourse import mybir

F32 = mybir.dt.float32
F32R = mybir.dt.float32r
F16 = mybir.dt.float16
I32 = mybir.dt.int32
U32 = mybir.dt.uint32
ALU = mybir.AluOpType
ACT = mybir.ActivationFunctionType
AX_X = mybir.AxisListType.X

P = 128
D = 256
KH = D // P
N = 6250
NE = 8
HD = 32
TILES = -(-N // P)
LAST_ROWS = N - (TILES - 1) * P
SUPER = 2
STEPS = -(-TILES // SUPER)
E = 106250
GROUP = 16
RING = 32
CHUNKS = -(-E // (P * RING)) * RING
GROUPS = CHUNKS // GROUP
ROUNDS = CHUNKS // RING
ROUNDS_ANY = TILES * ROUNDS + 1
NO_NODE = TILES * P
TABLE_SCALE = 2048.0
LN_EPS = 1e-5
NORM_EPS = 1e-6
LB = 4
LBATCHES = (TILES - 1) // LB
MAGIC = 0x5F3759DF
G_CHAIN = 31
PASSES = ((0, 0), (0, 1), (1, 0))


class Count:

    def __init__(self, sem, per):
        self.sem, self.per = sem, per

    def wait(self, eng, step, k):
        value = step * self.per + k
        if isinstance(value, int) and value <= 0:
            return
        eng.wait_ge(self.sem, value)


class Chain:

    def __init__(self, sem, per):
        self.sem, self.per, self.step, self.k = sem, per, 0, 0

    def begin(self, step):
        self.step, self.k = step, 0

    def inc(self, ins):
        ins.then_inc(self.sem, 1)
        self.k += 1

    def wait(self, eng):
        eng.wait_ge(self.sem, self.step * self.per + self.k)


def rows_of(tile):
    return LAST_ROWS if isinstance(tile, int) and tile == TILES - 1 else P


def tiles_of(step):
    return TILES - SUPER * step if isinstance(step, int) and step == STEPS - 1 else SUPER


def gps_layer(nc, x_d, src_d, dstc_d, dstf_d, w, out_d):
    with ExitStack() as ctx:
        def sb(name, shape, dt=F32):
            return ctx.enter_context(nc.sbuf_tensor(name, shape, dt))

        def sem(name):
            return ctx.enter_context(nc.semaphore(name))

        xn_d = nc.dram_tensor("xn_scratch", [N, D], F32).ap()
        table_d = nc.dram_tensor("table_scratch", [N, 2 * D], F16).ap()
        ctl_d = nc.dram_tensor("control_scratch", [TILES + 1, 3], I32).ap()

        wkv = sb("wkv", [P, 2, KH, 2 * D], F32R)
        wq = sb("wq", [P, 2, KH, D], F32R)
        wg1 = sb("wg1", [P, 2, KH, D], F32R)
        wg2 = sb("wg2", [P, 2, KH, D], F32R)
        kvwo = sb("kvwo", [P, 2, KH, D], F32R)
        we1 = sb("we1", [P, 2, NE, KH, D], F32R)
        we2 = sb("we2", [P, 2, NE, KH, D], F32R)
        wr = sb("wr", [P, 2, KH, NE], F32R)
        wo = sb("wo", [P, KH, D])
        stage_w = sb("stage_w", [P, 2, 2 * KH, D])
        bkv = sb("bkv", [P, 2, D])
        bout = sb("bout", [P, D])
        bout2 = sb("bout2", [P, D])
        bq = sb("bq", [P, KH])
        nbq = sb("nbq", [P, KH])
        bq1 = sb("bq1", [P, KH])
        bg1 = sb("bg1", [P, KH])
        be1 = sb("be1", [P, NE, KH])
        be2 = sb("be2", [NE, D])
        eps1 = sb("eps1", [P, 1])

        ring = sb("ring", [P, RING, 2 * D], F16)
        onehot = sb("onehot", [P, RING, P], F16)
        onehot1 = sb("onehot1", [P, SUPER, P], F16)
        idx_stage = sb("idx_stage", [P, 2, GROUP], I32)
        dst_f = sb("dst_f", [P, CHUNKS + 1])
        iota_t = sb("iota_t", [P, P])
        iota8 = sb("iota8", [P, NE])
        ident = sb("ident", [P, P])
        zeros16 = sb("zeros16", [P, P], F16)
        headmask = sb("headmask", [P, P])
        ones = sb("ones", [P, P])
        control = sb("control", [1, TILES + 1, 3], I32)

        area = sb("area", [P, 7168])
        lx = area[:, 0:2048].rearrange("p (b t c) -> p b t c", b=2, t=LB)
        lxn = area[:, 2048:4096].rearrange("p (b t c) -> p b t c", b=2, t=LB)
        ltab = area[:, 4096:6144].bitcast(F16).rearrange("p (b t h c) -> p b t h c", b=2, t=LB, h=2)

        def two(n, k=512):
            return area[:, n:n + k]

        def view(n):
            return two(n).rearrange("p (t c) -> p t c", t=2)

        xs, xn2, xe, h = view(0), view(512), view(1024), view(1536)
        rT, ex, qf, nrm = view(2048), view(2560), view(3072), view(3584)
        qs, tok = view(4096), view(4608)
        acc = two(5120, 1024).rearrange("p (u t c) -> p u t c", u=2, t=2)
        gact = two(6144, 1024).rearrange("p (u t c) -> p u t c", u=2, t=2)
        mxn = two(0).rearrange("p (u c) -> p u c", u=2)
        kb = two(512).rearrange("p (u c) -> p u c", u=2)
        kr = two(1024).rearrange("p (u c) -> p u c", u=2)
        kf = two(1536).rearrange("p (u c) -> p u c", u=2)
        kvm = two(2048, KH * P).rearrange("p (k c) -> p k c", k=KH)
        kvmT = two(2304, KH * P).rearrange("p (k c) -> p k c", k=KH)
        vf = two(6144, 2 * KH * (P + 2)).rearrange("p (u k c) -> p u k c", u=2, k=KH)
        ring32 = ring[:, :, :].rearrange("p s c -> p (s c)").bitcast(F32)
        d_cur = ring32[:, 0:CHUNKS].bitcast(I32)
        d_next = ring32[:, CHUNKS:2 * CHUNKS].bitcast(I32)
        d_bad = ring32[:, 2 * CHUNKS:3 * CHUNKS]
        dst_i = ring32[:, 4 * CHUNKS:5 * CHUNKS + 1].bitcast(I32)
        d_last = ring32[0:TILES + 1, 3 * CHUNKS:4 * CHUNKS].bitcast(I32)

        lstat = sb("lstat", [P, LB, 6])
        lmv = sb("lmv", [P, LB, 2])
        lv = sb("lv", [P, LB])
        ly = sb("ly", [P, LB])
        lt = sb("lt", [P, LB])
        lrs = sb("lrs", [P, 2, LB])
        lnm = sb("lnm", [P, 2, LB])
        cs = sb("cs", [P, 16])
        ctl_i = sb("ctl_i", [P, 3], I32)

        ksm = sb("ksm", [P, KH, P])
        ksum = sb("ksum", [P, KH])

        xT = sb("xT", [P, 2, KH, 2 * P], F32R)
        mxT = xT[:, :, :, :].rearrange("p a k c -> p (a k c)").rearrange("p (u a k c) -> p u a k c", u=2, a=2, k=KH)
        hT = sb("hT", [P, 2, KH, 2 * P], F32R)
        rTs = sb("rTs", [P, 2, KH, 2 * P], F32R)
        qTs = sb("qTs", [P, 2, KH, 2 * P], F32R)
        tokT = sb("tokT", [P, 2, 2, KH, 2 * P], F32R)
        gT = wkv[:, :, :, :].rearrange("p a k c -> p (a k c)").rearrange("p (u a k c) -> p u a k c", u=2, a=2, k=KH)
        gstat = sb("gstat", [P, SUPER, 6])
        gmv = sb("gmv", [P, SUPER, 2])
        gv = sb("gv", [P, SUPER])
        gy = sb("gy", [P, SUPER])
        gt = sb("gt", [P, SUPER])
        gnm = sb("gnm", [P, SUPER])
        top = sb("top", [P, SUPER, 8])
        topi = sb("topi", [P, SUPER, 8], U32)
        topf = sb("topf", [P, SUPER, 2])
        ntop = sb("ntop", [P, SUPER])
        etop = sb("etop", [P, SUPER, 8])
        esum = sb("esum", [P, SUPER])
        erec = sb("erec", [P, SUPER])
        prob = sb("prob", [P, SUPER, 2])
        pden = sb("pden", [P, SUPER])
        prec = sb("prec", [P, SUPER])
        wtop = sb("wtop", [P, SUPER, 2])
        pick0 = sb("pick0", [P, SUPER, NE])
        pick1 = sb("pick1", [P, SUPER, NE])
        wr_f = sb("wr_f", [P, KH, NE])
        comb = sb("comb", [P, 2, SUPER, NE])
        combT = sb("combT", [NE, 2 * P])

        bank = [ctx.enter_context(nc.psum_tensor(f"bank{i}", [P, 512], F32)) for i in range(8)]
        ps_l1, ps_l2, ps_agg, ps_g = bank[0:2], bank[2:4], bank[4], bank[5:8]
        ps_kvp, ps_kva, ps_mt = bank[0:2], bank[2:4], bank[5:7]

        s_bias, s_wload, s_wo = sem("bias_loaded"), [sem("weights_loaded0"), sem("weights_loaded1")], sem("wo_loaded")
        s_whi, s_wlo = sem("weight_hi"), sem("weight_lo")
        s_const, s_bprep = sem("constants"), sem("biases_prepared")
        s_dst, s_ctlchain, s_viol = sem("dst_loaded"), sem("control_chain"), sem("violations_summed")
        s_ctlo, s_ctl = sem("control_stored"), sem("control_loaded")
        s_lx = [sem("ln_x_loaded0"), sem("ln_x_loaded1")]
        s_lchain, s_lxn, s_lhi, s_llo = sem("ln_chain"), sem("ln_xn"), sem("ln_table_hi"), sem("ln_table_lo")
        s_lrs = sem("ln_scales")
        s_lout = [sem("ln_stored0"), sem("ln_stored1")]
        s_mxn = [sem("mix_xn_loaded0"), sem("mix_xn_loaded1")]
        s_mt, s_mhi, s_mlo = sem("mix_transposed"), sem("mix_hi"), sem("mix_lo")
        s_kvp, s_kb, s_kr, s_ke = sem("kv_projected"), sem("kv_biased"), sem("k_negative_part"), sem("k_exp")
        s_kf, s_kva, s_kv1 = sem("k_features"), sem("kv_accumulated"), sem("v_ones")
        s_kvx, s_kvy = sem("kvwo_vector"), sem("kvwo_tensor")
        s_kvz = sem("kvwo_scalar")
        s_idx, s_slot = [sem("indices0"), sem("indices1")], [sem(f"slot{k}_landed") for k in range(RING)]
        s_landed, s_free, s_grant = sem("chunks_landed"), sem("slots_free"), sem("slot_granted")
        s_table = sem("table_complete")
        s_hot, s_iota = sem("onehot_ready"), sem("tile_iota")
        s_wrs = sem("router_weights_split")
        s_gate = sem("gate_passed")

        def count(name, per):
            return Count(sem(name), per)

        c_hot1 = count("last_onehot_ready", 2)
        c_xs, c_xn2 = count("x_loaded", 16), count("xn_loaded", 16)
        c_xe, c_agg, c_h = count("xn_scaled", 1), count("segment_summed", 2), count("h_ready", 2)
        c_hp = count("h_first_part", 2)
        c_tx, c_th = count("xT_in_psum", 1), count("hT_in_psum", 1)
        c_xhi, c_xlo = count("xT_hi", 1), count("xT_lo", 1)
        c_hhi, c_hlo = count("hT_hi", 1), count("hT_lo", 1)
        c_q, c_qneg, c_qexp, c_qf = count("q_product", 1), count("q_negative", 1), count("q_exp", 1), count("q_features", 1)
        c_w1, c_r, c_rhi, c_rlo = count("gin1_product", 1), count("gin1_relu", 1), count("gin1_hi", 1), count("gin1_lo", 1)
        c_n, c_ne, c_nr, c_qs = count("norm_product", 1), count("norm_eps", 1), count("norm_reciprocal", 1), count("q_normed", 1)
        c_qhi, c_qlo = count("q_hi", 1), count("q_lo", 1)
        c_o, c_xb, c_x1 = count("layer_product", 1), count("x_plus_bias", 1), count("residual1", 1)
        c_ln, c_tok, c_acc = count("ln2_scales", 1), count("tokens_normed", 1), count("acc_started", 1)
        c_tk, c_khi, c_klo = count("tokT_in_psum", 1), count("tokT_hi", 1), count("tokT_lo", 1)
        c_lg, c_top, c_et, c_comb = count("logits", 1), count("top_logits", 1), count("top_exp", 1), count("combine_weights", 1)
        c_out = count("out_stored", 16)
        c_ct, c_ctc, c_b2, c_accb = count("combT_in_psum", 1), count("combT_copied", 1), count("bias2_product", 1), count("acc_with_bias", 1)
        c_l1, c_g, c_ghi, c_glo = count("expert_l1", NE), count("gelu", NE), count("gelu_hi", NE), count("gelu_lo", NE)
        c_l2, c_add = count("expert_l2", NE), count("expert_added", NE)
        s_gchain = sem("ln2_router_chain")

        def rows(s):
            return P if tiles_of(s) == SUPER else LAST_ROWS

        def super_rows(dram, s):
            if tiles_of(s) == 1:
                return dram[s * SUPER * P:N, :]
            return dram[bass.ds(s * (SUPER * P), SUPER * P), :].rearrange("(t p) c -> p t c", p=P)

        def super_buf(buf, s):
            return buf[0:LAST_ROWS, 0, :] if tiles_of(s) == 1 else buf

        def cut(buf, s):
            return buf[0:rows(s), 0:tiles_of(s)]

        def tokens(buf, s):
            return buf[:, :, 0:(SUPER * P if tiles_of(s) == SUPER else LAST_ROWS)]

        def halves(b):
            return b[:, :].rearrange("p (t c) -> p t c", t=2)

        ORDER = ["hot 0", "l1 0", "combT", "l1 1", "store", "bias2", "trans", "loadxn", "l1 2", "l2 0",
                 "q", "l1 3", "l2 1", "gin1", "l1 4", "l2 2", "norm", "hot 1", "agg 0", "l1 5", "l2 3",
                 "out", "l1 6", "l2 4", "agg 1", "l1 7", "l2 5", "tokT", "l2 6", "router", "l2 7"]
        STAGE = {"hot": "a", "agg": "a", "loadxn": "a", "l1": "m", "l2": "m", "combT": "m", "bias2": "m",
                 "store": "m", "trans": "g", "q": "g", "gin1": "g", "norm": "g", "out": "g", "tokT": "g",
                 "router": "g"}
        LOOP_FROM = 2
        TURNS = (STEPS - 1 - 2 - LOOP_FROM) // 2

        def main_program(eng, stage_fn):
            def step(a, g, m, u):
                for name in ORDER:
                    key, *arg = name.split()
                    s = {"a": a, "g": g, "m": m}[STAGE[key]]
                    if s is not None:
                        stage_fn(key, s, int(arg[0]) if arg else None, 1 - u if STAGE[key] == "g" else u)

            def alone(n):
                step(*(n - k if 0 <= n - k < STEPS else None for k in range(3)), n % 2)

            for n in range(LOOP_FROM + 2):
                alone(n)
            with eng.Fori(0, TURNS) as turn:
                for b in range(2):
                    step(*(turn * 2 + (LOOP_FROM + b + k) for k in (2, 1, 0)), b)
            for n in range(LOOP_FROM + 2 + 2 * TURNS, STEPS + 2):
                alone(n)

        MIX_AHEAD = 3
        MIX_TURNS = (TILES - 1 - MIX_AHEAD) // 2

        def mix_program(eng, tile_fn):
            tile_fn(0, 0)
            tile_fn(1, 1)
            with eng.Fori(1, MIX_TURNS) as turn:
                tile_fn(turn * 2, 0)
                tile_fn(turn * 2 + 1, 1)
            for j in range(2 * MIX_TURNS, TILES):
                tile_fn(j, j % 2)

        def beyond(j, k=TILES):
            return isinstance(j, int) and j >= k

        def wait_tile(eng, s, value):
            if not (isinstance(value, int) and value <= 0):
                eng.wait_ge(s, value)

        weights = [([w["wk"], w["wv"]], "kv"), ([w["wq"], w["wg1"]], "q1"), ([w["wg2"]], "g2")]
        weights += [([w["we1"][e], w["we2"][e]], e) for e in range(NE)]
        PIECES = [0]
        for sources, _ in weights:
            PIECES.append(PIECES[-1] + len(sources))

        def parts(n, part):
            key = weights[n][1]
            if key == "kv":
                dst = [wkv[:, part, :, 0:D], wkv[:, part, :, D:2 * D]]
            elif key == "q1":
                dst = [wq[:, part], wg1[:, part]]
            elif key == "g2":
                dst = [wg2[:, part]]
            else:
                dst = [we1[:, part, key], we2[:, part, key]]
            return [(d, stage_w[:, n % 2, i * KH:(i + 1) * KH, :]) for i, d in enumerate(dst)]

        def loaded_pieces(n):
            return sum(PIECES[i + 1] - PIECES[i] for i in range(n % 2, n + 1, 2))

        block = ctx.enter_context(nc.Block())

        @block.sync
        def _(sp):
            def batch(dram, b):
                if b == LBATCHES:
                    return dram[b * LB * P:N, :]
                return dram[b * LB * P:(b + 1) * LB * P, :].rearrange("(t p) c -> p t c", p=P)

            def load_x(b):
                if b >= 2:
                    sp.wait_ge(s_lxn, b - 1)
                to = lx[:, b % 2] if b < LBATCHES else lx[0:LAST_ROWS, b % 2, 0, :]
                sp.dma_start(to, batch(x_d, b)).then_inc(s_lx[b % 2], 16)

            def load_w(n):
                if n >= 2:
                    sp.wait_ge(s_wlo, PIECES[n - 1])
                for i, source in enumerate(weights[n][0]):
                    sp.dma_start(stage_w[:, n % 2, i * KH:(i + 1) * KH, :],
                                 source.rearrange("(k p) n -> p k n", p=P)).then_inc(s_wload[n % 2], 16)

            load_x(0)
            load_x(1)
            sp.dma_start(dst_i[:, :], dstc_d).then_inc(s_dst, 16)
            sp.dma_start(d_cur, dstf_d[0:P * CHUNKS].rearrange("(p c) -> p c", p=P)).then_inc(s_dst, 16)
            sp.dma_start(d_next, dstf_d[1:P * CHUNKS + 1].rearrange("(p c) -> p c", p=P)).then_inc(s_dst, 16)
            sp.dma_start(d_last, dstc_d[P - 1:P, 0:CHUNKS].broadcast_to([TILES + 1, CHUNKS])).then_inc(s_dst, 16)
            load_w(0)
            load_w(1)
            sp.dma_start(wo[:, :, :], w["wo"].rearrange("(k p) n -> p k n", p=P)).then_inc(s_wo, 16)
            for b in range(LBATCHES + 1):
                last = b == LBATCHES
                sp.wait_ge(s_lxn, b + 1)
                sp.dma_start(batch(xn_d, b), lxn[0:LAST_ROWS, b % 2, 0, :] if last else lxn[:, b % 2]
                             ).then_inc(s_lout[b % 2], 16)
                sp.wait_ge(s_llo, b + 1)
                rows16 = ltab[0:LAST_ROWS, b % 2, 0].rearrange("p h c -> p (h c)") if last else \
                    ltab[:, b % 2].rearrange("p t h c -> p t (h c)")
                sp.dma_start(batch(table_d, b), rows16).then_inc(s_lout[b % 2], 16)
                if b + 2 <= LBATCHES:
                    load_x(b + 2)
                if b + 2 < len(weights):
                    load_w(b + 2)
            sp.wait_ge(s_ctlchain, 12)
            sp.dma_start(ctl_d, ctl_i[0:TILES + 1, :]).then_inc(s_ctlo, 16)
            sp.wait_ge(s_ctlo, 16)
            sp.dma_start(control[:, :, :], ctl_d.rearrange("(o t) c -> o t c", o=1)).then_inc(s_ctl, 16)
            sp.wait_ge(s_ctl, 16)
            rounds = sp.value_load(control[0:1, 0, 2:3], min_val=ROUNDS, max_val=ROUNDS_ANY)
            for b in range(2):
                sp.wait_ge(s_lout[b], 32 * len(range(b, LBATCHES + 1, 2)))
            sp.sem_inc(s_table, 1)
            for b in range(2):
                sp.dma_start(idx_stage[:, b, :], src_d[b * P:(b + 1) * P, :]).then_inc(s_idx[b], 16)
            with sp.Fori(0, rounds) as r:
                for half in range(2):
                    for k in range(half * GROUP, (half + 1) * GROUP):
                        sp.wait_ge(s_slot[k], r * 16 + 16)
                        sp.sem_inc(s_landed, 1)
                    group = ((r + 1) % ROUNDS) * 2 + half
                    sp.dma_start(idx_stage[:, half, :], src_d[bass.ds(group * P, P), :]).then_inc(s_idx[half], 16)
            for b in range(2):
                sp.wait_ge(s_idx[b], rounds * 16 + 16)
            sp.sem_inc(s_gate, 1)

        @block.gpsimd
        def _(pool):
            for u in range(2):
                pool.memset(vf[:, u, :, P:P + 2], 1.0).then_inc(s_kv1, 1)
            pool.memset(ident[:, :], 0.0).then_inc(s_const, 1)
            pool.memset(headmask[:, :], 0.0).then_inc(s_const, 1)
            pool.memset(ones[:, :], 1.0).then_inc(s_const, 1)
            pool.memset(zeros16[:, :], 0.0).then_inc(s_const, 1)
            pool.iota(iota_t[:, :], [[1, P]], base=0, channel_multiplier=0,
                      allow_small_or_imprecise_dtypes=True).then_inc(s_const, 1)
            pool.iota(iota8[:, :], [[1, NE]], base=0, channel_multiplier=0,
                      allow_small_or_imprecise_dtypes=True).then_inc(s_const, 1)
            pool.iota(cs[:, 0:2], [[P, 2]], base=0, channel_multiplier=P,
                      allow_small_or_imprecise_dtypes=True).then_inc(s_const, 1)
            pool.iota(cs[:, 2:3], [[1, 1]], base=0, channel_multiplier=CHUNKS,
                      allow_small_or_imprecise_dtypes=True).then_inc(s_const, 1)
            pool.wait_ge(s_const, 8)
            pool.affine_select(out=ident[:, :], in_=ident[:, :], compare_op=ALU.not_equal, fill=1.0, base=0,
                               pattern=[[-1, P]], channel_multiplier=1).then_inc(s_const, 1)
            for b in range(P // HD):
                pool.wait_ge(s_const, 9 + b)
                pool.memset(headmask[b * HD:(b + 1) * HD, b * HD:(b + 1) * HD], 1.0).then_inc(s_const, 1)
            pool.wait_ge(s_const, 9 + P // HD)
            for n in range(len(weights)):
                pool.wait_ge(s_whi, PIECES[n + 1])
                for (lo, whole), (hi, _) in zip(parts(n, 1), parts(n, 0)):
                    pool.tensor_tensor(out=lo, in0=whole, in1=hi.bitcast(F32), op=ALU.subtract).then_inc(s_wlo, 1)
            pool.wait_ge(s_ctl, 16)
            rounds = pool.value_load(control[0:1, 0, 2:3], min_val=ROUNDS, max_val=ROUNDS_ANY)
            pool.wait_ge(s_table, 1)

            def gathers(r):
                for k in range(RING):
                    if k % GROUP == 0:
                        pool.wait_ge(s_idx[k // GROUP], r * 16 + 16)
                        pool.sem_inc(s_grant, 1)
                    pool.wait_ge(s_free, r * RING + k + 1)
                    pool.sem_inc(s_grant, 1)
                    pool.indirect_dma_start(
                        out=ring[:, k, :].bitcast(F32), out_offset=None, in_=table_d.bitcast(F32),
                        in_offset=bass.IndirectOffsetOnAxis(
                            ap=idx_stage[:, k // GROUP, k % GROUP:k % GROUP + 1].bitcast(U32), axis=0),
                        bounds_check=N - 1, oob_is_err=False).then_inc(s_slot[k], 16)

            with pool.Fori(0, rounds) as r:
                gathers(r)

        @block.scalar
        def _(act):
            act.dma_start(bkv[:, 0, :], w["bk"].broadcast_to([P, D])).then_inc(s_bias, 16)
            act.dma_start(bkv[:, 1, :], w["bv"].broadcast_to([P, D])).then_inc(s_bias, 16)
            act.dma_start(bout[:, :], w["bg2"].broadcast_to([P, D])).then_inc(s_bias, 16)
            act.dma_start(bout2[:, :], w["bo"].broadcast_to([P, D])).then_inc(s_bias, 16)
            act.dma_start(bq[:, :], w["bq"]).then_inc(s_bias, 16)
            act.dma_start(bg1[:, :], w["bg1"]).then_inc(s_bias, 16)
            act.dma_start(be1[:, :, :], w["be1"]).then_inc(s_bias, 16)
            act.dma_start(be2[:, :], w["be2"]).then_inc(s_bias, 16)
            act.dma_start(eps1[:, :], w["eps"].broadcast_to([P, 1])).then_inc(s_bias, 16)
            act.dma_start(wr_f[:, :, :], w["wr"]).then_inc(s_bias, 16)

            for b in range(LBATCHES + 1):
                nt = LB if b < LBATCHES else 1
                r = P if b < LBATCHES else LAST_ROWS
                act.wait_ge(s_lrs, b + 1)
                if b >= 2:
                    act.wait_ge(s_lout[b % 2], 32 * (b // 2))
                for t in range(nt):
                    last = act.activation(lxn[0:r, b % 2, t, :], lx[0:r, b % 2, t, :], ACT.Identity,
                                          bias=lnm[0:r, b % 2, t:t + 1], scale=lrs[0:r, b % 2, t:t + 1])
                last.then_inc(s_lxn, 1)
                act.wait_ge(s_lxn, b + 1)
                act.activation(ltab[0:r, b % 2, 0:nt, 0, :], lxn[0:r, b % 2, 0:nt, :], ACT.Copy,
                               scale=TABLE_SCALE).then_inc(s_lhi, 1)
                if b < len(weights):
                    act.wait_ge(s_wload[b % 2], 16 * loaded_pieces(b))
                    for hi, whole in parts(b, 0):
                        act.activation(hi, whole, ACT.Copy).then_inc(s_whi, 1)
                if b == 0:
                    act.wait_ge(s_bias, 160)
                    act.activation(wr[:, 0], wr_f[:, :, :], ACT.Copy).then_inc(s_wrs, 1)

            def load_mix(j, u):
                wait_tile(act, s_mt, j - 1)
                src = xn_d[j * P:j * P + rows_of(j), :] if isinstance(j, int) else xn_d[bass.ds(j * P, P), :]
                act.dma_start(mxn[0:rows_of(j), u, :], src).then_inc(s_mxn[u], 16)

            def split_mix(j, u):
                r = rows_of(j)
                act.wait_ge(s_mt, j + 1)
                wait_tile(act, s_kvp, j - 1)
                act.activation(mxT[:, u, 0, :, 0:r], halves(ps_mt[u])[:, :, 0:r], ACT.Copy).then_inc(s_mhi, 1)

            def mix_tile(j, u):
                if not beyond(j + 1):
                    split_mix(j + 1, 1 - u)
                    if not beyond(j + MIX_AHEAD):
                        load_mix(j + MIX_AHEAD, 1 - u)
                r = rows_of(j)
                act.wait_ge(s_kb, 2 * j + 1)
                wait_tile(act, s_kf, j - 1)
                act.activation(kr[0:r, u, :], kb[0:r, u, :], ACT.Relu, scale=-1.0).then_inc(s_kr, 1)
                act.wait_ge(s_kr, j + 1)
                act.activation(kr[0:r, u, :], kr[0:r, u, :], ACT.Exp, scale=-1.0).then_inc(s_ke, 1)

            act.wait_ge(s_table, 1)
            load_mix(0, 0)
            load_mix(1, 1)
            split_mix(0, 0)
            load_mix(2, 0)
            mix_program(act, mix_tile)
            act.wait_ge(s_kvy, 2)
            act.activation(kvwo[:, 0, :, :], halves(ps_g[1]), ACT.Copy).then_inc(s_kvz, 1)

            def stage(key, s, i, v):
                if key == "loadxn":
                    c_tx.wait(act, s, 0)
                    c_xe.wait(act, s, 0)
                    act.dma_start(super_buf(xn2, s), super_rows(xn_d, s)).then_inc(c_xn2.sem, 16)
                elif key == "l1":
                    c_l1.wait(act, s, i + 1)
                    c_glo.wait(act, s, i - 1)
                    for half in range(KH):
                        last = act.activation(tokens(gact[:, i % 2], s)[:, half], tokens(halves(ps_l1[i % 2]), s)[:, half],
                                              ACT.Gelu, bias=be1[:, i, half:half + 1])
                    last.then_inc(c_g.sem, 1)
                    c_g.wait(act, s, i + 1)
                    c_l2.wait(act, s, i - 1)
                    act.activation(tokens(gT[:, i % 2, 0], s), tokens(gact[:, i % 2], s), ACT.Copy).then_inc(c_ghi.sem, 1)
                elif key == "store" and not (isinstance(s, int) and s == 0):
                    c_add.wait(act, s, 0)
                    act.dma_start(super_rows(out_d, s - 1), super_buf(acc[:, 1 - v], s - 1)).then_inc(c_out.sem, 16)
                elif key == "combT":
                    c_ct.wait(act, s, 1)
                    n = SUPER * P if tiles_of(s) == SUPER else LAST_ROWS
                    act.activation(combT[:, 0:n], ps_g[2][0:NE, 0:n], ACT.Copy).then_inc(c_ctc.sem, 1)
                elif key == "trans":
                    c_x1.wait(act, s, 0)
                    act.dma_start(super_buf(xs, s), super_rows(x_d, s)).then_inc(c_xs.sem, 16)
                    c_tx.wait(act, s, 1)
                    c_q.wait(act, s, 0)
                    act.activation(tokens(xT[:, 0], s), tokens(halves(ps_g[0]), s), ACT.Copy).then_inc(c_xhi.sem, 1)
                    c_th.wait(act, s, 1)
                    c_w1.wait(act, s, 0)
                    act.activation(tokens(hT[:, 0], s), tokens(halves(ps_g[1]), s), ACT.Copy).then_inc(c_hhi.sem, 1)
                elif key == "q":
                    c_q.wait(act, s, 1)
                    c_qf.wait(act, s, 0)
                    for half in range(KH):
                        last = act.activation(tokens(ex, s)[:, half], tokens(halves(ps_g[2]), s)[:, half], ACT.Relu,
                                              bias=nbq[:, half:half + 1], scale=-1.0)
                    last.then_inc(c_qneg.sem, 1)
                    c_qneg.wait(act, s, 1)
                    act.activation(tokens(ex, s), tokens(ex, s), ACT.Exp, scale=-1.0).then_inc(c_qexp.sem, 1)
                elif key == "gin1":
                    c_w1.wait(act, s, 1)
                    c_rlo.wait(act, s, 0)
                    for half in range(KH):
                        last = act.activation(tokens(rT, s)[:, half], tokens(halves(ps_g[0]), s)[:, half], ACT.Relu,
                                              bias=bg1[:, half:half + 1])
                    last.then_inc(c_r.sem, 1)
                    c_r.wait(act, s, 1)
                    c_o.wait(act, s, 0)
                    act.activation(tokens(rTs[:, 0], s), tokens(rT, s), ACT.Copy).then_inc(c_rhi.sem, 1)
                elif key == "norm":
                    c_n.wait(act, s, 1)
                    c_qs.wait(act, s, 0)
                    act.activation(tokens(nrm, s), tokens(halves(ps_g[1]), s), ACT.Copy, bias=NORM_EPS).then_inc(c_ne.sem, 1)
                    c_qs.wait(act, s, 1)
                    act.activation(tokens(qTs[:, 0], s), tokens(qs, s), ACT.Copy).then_inc(c_qhi.sem, 1)
                elif key == "agg" and i == 0:
                    c_xn2.wait(act, s, 16)
                    c_h.wait(act, s, 0)
                    act.activation(cut(xe, s), cut(xn2, s), ACT.Copy, scale=eps1[0:rows(s), 0:1]).then_inc(c_xe.sem, 1)
                elif key == "tokT":
                    c_ln.wait(act, s, 1)
                    c_acc.wait(act, s, 0)
                    for t in range(tiles_of(s)):
                        last = act.activation(tok[0:rows(s), t, :], acc[0:rows(s), v, t, :], ACT.Identity,
                                              bias=gnm[0:rows(s), t:t + 1], scale=gy[0:rows(s), t:t + 1])
                    last.then_inc(c_tok.sem, 1)
                    c_tk.wait(act, s, 1)
                    c_l1.wait(act, s, -NE)
                    act.activation(tokens(tokT[:, v, 0], s), tokens(halves(ps_g[0]), s), ACT.Copy).then_inc(c_khi.sem, 1)
                elif key == "router":
                    c_top.wait(act, s, 1)
                    for t in range(tiles_of(s)):
                        last = act.activation(etop[0:rows(s), t, :], top[0:rows(s), t, :], ACT.Exp,
                                              bias=ntop[0:rows(s), t:t + 1], accum_out=esum[0:rows(s), t:t + 1])
                    last.then_inc(c_et.sem, 1)

            main_program(act, stage)
            last = STEPS - 1
            c_add.wait(act, last, NE)
            act.dma_start(super_rows(out_d, last), super_buf(acc[:, last % 2], last)).then_inc(c_out.sem, 16)
            act.wait_ge(c_out.sem, 16 * STEPS)

        @block.tensor
        def _(pe):
            pe.sem_inc(s_free, RING)
            pe.wait_ge(s_const, 9 + P // HD)
            pe.wait_ge(s_ctlchain, 2)
            pe.matmul(ps_g[2][0:TILES + 1, 0:1], ones[:, 0:TILES + 1], cs[:, 4:5], start=True, stop=True).then_inc(s_viol, 1)

            def transposes_mix(j, u):
                r = rows_of(j)
                if isinstance(j, int):
                    pe.wait_ge(s_mxn[u], 16 * (j // 2 + 1))
                else:
                    pe.wait_ge(s_mxn[u], j * 8 + (16 - 8 * u))
                wait_tile(pe, s_mlo, j - 1)
                for k in range(KH):
                    last = pe.transpose(halves(ps_mt[u])[:, k, 0:r], mxn[0:r, u, k * P:(k + 1) * P], ident[0:r, 0:r])
                last.then_inc(s_mt, 1)

            def project_mix(j, u):
                r = rows_of(j)
                pe.wait_ge(s_mhi, j + 1)
                pe.wait_ge(s_mlo, j + 1)
                wait_tile(pe, s_kb, 2 * (j - 1))
                n = 0
                for wp, ap in PASSES:
                    for k in range(KH):
                        last = pe.matmul(ps_kvp[u][0:r, :], mxT[:, u, ap, k, 0:r], wkv[:, wp, k, :],
                                         start=n == 0, stop=n == len(PASSES) * KH - 1)
                        n += 1
                last.then_inc(s_kvp, 1)

            def accumulate_mix(j, u):
                r = rows_of(j)
                pe.wait_ge(s_kf, j + 1)
                pe.wait_ge(s_kb, 2 * j + 2)
                for k in range(KH):
                    last = pe.matmul(ps_kva[k][:, 0:P + 1], kf[0:r, u, k * P:(k + 1) * P], vf[0:r, u, k, 0:P + 1],
                                     start=isinstance(j, int) and j == 0, stop=isinstance(j, int) and j == TILES - 1,
                                     skip_group_check=True)
                last.then_inc(s_kva, 1)

            def mix_tile(j, u):
                if not beyond(j + 1):
                    transposes_mix(j + 1, 1 - u)
                project_mix(j, u)
                if not (isinstance(j, int) and j == 0):
                    accumulate_mix(j - 1, 1 - u)

            pe.wait_ge(s_wlo, PIECES[1])
            pe.wait_ge(s_kv1, 2)
            transposes_mix(0, 0)
            mix_program(pe, mix_tile)
            accumulate_mix(TILES - 1, (TILES - 1) % 2)
            pe.wait_ge(s_kvx, 3)
            for k in range(KH):
                last = pe.transpose(ps_g[0][:, k * P:(k + 1) * P], kvm[:, k, :], ident[:, :])
            last.then_inc(s_kvy, 1)
            pe.wait_ge(s_kvx, 4)
            pe.wait_ge(s_wo, 16)
            for k in range(KH):
                last = pe.matmul(halves(ps_g[1])[:, k, :], kvmT[:, k, :], wo[:, k, :], start=True, stop=True)
            last.then_inc(s_kvy, 1)

            pe.wait_ge(s_wlo, PIECES[-1])
            pe.wait_ge(s_wrs, 2)
            pe.wait_ge(s_ctl, 16)

            def product_T(bank_, weight, act_parts, s):
                for half in range(KH):
                    n = 0
                    for wp, ap in PASSES:
                        for k in range(KH):
                            last = pe.matmul(tokens(halves(bank_), s)[:, half], weight[:, wp, k, half * P:(half + 1) * P],
                                             tokens(act_parts[:, ap], s)[:, k], start=n == 0,
                                             stop=n == len(PASSES) * KH - 1, skip_group_check=True)
                            n += 1
                return last

            def product(bank_, pairs, s, t):
                r = rows(s)
                n = 0
                for act_parts, weight in pairs:
                    for wp, ap in PASSES:
                        for k in range(KH):
                            last = pe.matmul(halves(bank_)[0:r, t, :], act_parts[:, ap, k, t * P:t * P + r],
                                             weight[:, wp, k, :], start=n == 0,
                                             stop=n == len(pairs) * len(PASSES) * KH - 1, skip_group_check=True)
                            n += 1
                return last

            def transposes(bank_, src, s):
                r = rows(s)
                for t in range(tiles_of(s)):
                    for k in range(KH):
                        last = pe.transpose(halves(bank_)[:, k, t * P:t * P + r], src[0:r, t, k * P:(k + 1) * P],
                                            ident[0:r, 0:r])
                return last

            def stage(key, s, i, v):
                if key == "l1":
                    if i == 0:
                        c_khi.wait(pe, s, 1)
                        c_klo.wait(pe, s, 1)
                    c_g.wait(pe, s, i - 1)
                    product_T(ps_l1[i % 2], we1[:, :, i], tokT[:, v], s).then_inc(c_l1.sem, 1)
                elif key == "l2":
                    c_ghi.wait(pe, s, i + 1)
                    c_glo.wait(pe, s, i + 1)
                    c_add.wait(pe, s, i - 1)
                    for t in range(tiles_of(s)):
                        last = product(ps_l2[i % 2], [(gT[:, i % 2], we2[:, :, i])], s, t)
                    last.then_inc(c_l2.sem, 1)
                elif key == "combT":
                    c_comb.wait(pe, s, 1)
                    r = rows(s)
                    for t in range(tiles_of(s)):
                        last = pe.transpose(ps_g[2][0:NE, t * P:t * P + r], comb[0:r, v, t, :], ident[0:r, 0:r])
                    last.then_inc(c_ct.sem, 1)
                elif key == "bias2":
                    c_ctc.wait(pe, s, 1)
                    r = rows(s)
                    for t in range(tiles_of(s)):
                        last = pe.matmul(halves(ps_g[2])[0:r, t, :], combT[:, t * P:t * P + r], be2[:, :],
                                         start=True, stop=True, skip_group_check=True)
                    last.then_inc(c_b2.sem, 1)
                elif key == "trans":
                    c_xn2.wait(pe, s, 16)
                    c_khi.wait(pe, s, 0)
                    c_klo.wait(pe, s, 0)
                    transposes(ps_g[0], xn2, s).then_inc(c_tx.sem, 1)
                    c_h.wait(pe, s, tiles_of(s))
                    c_top.wait(pe, s, 0)
                    transposes(ps_g[1], h, s).then_inc(c_th.sem, 1)
                elif key == "q":
                    c_xhi.wait(pe, s, 1)
                    c_xlo.wait(pe, s, 1)
                    c_accb.wait(pe, s, 0)
                    product_T(ps_g[2], wq, xT, s).then_inc(c_q.sem, 1)
                elif key == "gin1":
                    c_hhi.wait(pe, s, 1)
                    c_hlo.wait(pe, s, 1)
                    product_T(ps_g[0], wg1, hT, s).then_inc(c_w1.sem, 1)
                elif key == "norm":
                    c_qf.wait(pe, s, 1)
                    for k in range(KH):
                        last = pe.matmul(tokens(halves(ps_g[1]), s)[:, k], ksm[:, k, :], tokens(qf, s)[:, k],
                                         start=True, stop=True, skip_group_check=True)
                    last.then_inc(c_n.sem, 1)
                elif key == "out":
                    c_rhi.wait(pe, s, 1)
                    c_rlo.wait(pe, s, 1)
                    c_qhi.wait(pe, s, 1)
                    c_qlo.wait(pe, s, 1)
                    for t in range(tiles_of(s)):
                        last = product(ps_g[2], [(rTs, wg2), (qTs, kvwo)], s, t)
                    last.then_inc(c_o.sem, 1)
                elif key == "tokT":
                    c_tok.wait(pe, s, 1)
                    c_r.wait(pe, s, 1)
                    transposes(ps_g[0], tok, s).then_inc(c_tk.sem, 1)
                elif key == "router":
                    c_khi.wait(pe, s, 1)
                    c_klo.wait(pe, s, 1)
                    c_ne.wait(pe, s, 1)
                    r = rows(s)
                    for t in range(tiles_of(s)):
                        n = 0
                        for wp, ap in PASSES:
                            for k in range(KH):
                                last = pe.matmul(ps_g[1][0:r, t * NE:(t + 1) * NE], tokT[:, v, ap, k, t * P:t * P + r],
                                                 wr[:, wp, k, :], start=n == 0, stop=n == len(PASSES) * KH - 1,
                                                 skip_group_check=True)
                                n += 1
                    last.then_inc(c_lg.sem, 1)
                elif key == "agg" and i < tiles_of(s):
                    tile = s * SUPER + i
                    first = pe.value_load(control[0:1, tile, 0:1] if isinstance(tile, int) else control[0:1, bass.ds(tile, 1), 0],
                                          min_val=0, max_val=TILES * CHUNKS)
                    end = pe.value_load(control[0:1, tile + 1, 0:1] if isinstance(tile, int) else control[0:1, bass.ds(tile + 1, 1), 0],
                                        min_val=0, max_val=TILES * CHUNKS)
                    c_h.wait(pe, s, i)
                    pe.matmul(ps_agg[:, 0:2], zeros16[:, :], zeros16[:, 0:2], start=True, stop=False, skip_group_check=True)

                    with pe.If(first < end):
                        with pe.Fori(first, end) as q:
                            pe.wait_ge(s_hot, q + 1)
                            pe.wait_ge(s_landed, q + 1)
                            pe.matmul(ps_agg[:, :], onehot[:, q & (RING - 1), :], ring[:, q & (RING - 1), :],
                                      start=False, stop=False, skip_group_check=True).then_inc(s_free, 1)
                    c_hot1.wait(pe, s, i + 1)
                    pe.wait_ge(s_landed, end + 1)
                    pe.matmul(ps_agg[:, :], onehot1[:, i, :], ring[:, end & (RING - 1), :],
                              start=False, stop=True, skip_group_check=True).then_inc(c_agg.sem, 1)

            main_program(pe, stage)

        @block.vector
        def _(dve):
            dve.wait_ge(s_bias, 160)
            dve.tensor_tensor(bout[:, :], bout[:, :], bout2[:, :], ALU.add).then_inc(s_bprep, 1)
            dve.tensor_scalar(nbq[:, :], bq[:, :], -1.0, None, ALU.mult).then_inc(s_bprep, 1)
            dve.tensor_scalar(bq1[:, :], bq[:, :], 1.0, None, ALU.add).then_inc(s_bprep, 1)
            dve.tensor_scalar(eps1[:, :], eps1[:, :], 1.0, None, ALU.add).then_inc(s_bprep, 1)

            def rsqrt(v, y, t, inc, wait):
                inc(dve.tensor_scalar(y.bitcast(I32), v.bitcast(I32), 1, None, ALU.logical_shift_right))
                wait()
                inc(dve.tensor_scalar(y.bitcast(I32), y.bitcast(I32), -1.0, float(MAGIC), ALU.mult, ALU.add))
                for _ in range(3):
                    wait()
                    inc(dve.tensor_tensor(t, y, y, ALU.mult))
                    wait()
                    inc(dve.scalar_tensor_tensor(out=t, in0=t, scalar=-0.5, in1=v, op0=ALU.mult, op1=ALU.mult))
                    wait()
                    inc(dve.scalar_tensor_tensor(out=y, in0=t, scalar=1.5, in1=y, op0=ALU.add, op1=ALU.mult))
                wait()

            chain = [0]

            def l_inc(ins):
                ins.then_inc(s_lchain, 1)
                chain[0] += 1

            def l_wait():
                dve.wait_ge(s_lchain, chain[0])

            def control_table():
                T = TILES + 1
                dve.wait_ge(s_dst, 64)
                dve.wait_ge(s_const, 9 + P // HD)
                dve.tensor_tensor(d_bad, d_next, d_cur, ALU.is_lt).then_inc(s_ctlchain, 1)
                dve.wait_ge(s_ctlchain, 1)
                dve.tensor_reduce(cs[:, 4:5], d_bad, AX_X, ALU.add).then_inc(s_ctlchain, 1)
                dve.tensor_copy(dst_f[:, :], dst_i[:, :]).then_inc(s_bprep, 1)
                dve.wait_ge(s_ctlchain, 2)
                for n in range(2):
                    dve.tensor_scalar(d_bad[0:T, :], d_last, cs[0:T, n:n + 1], None, ALU.is_lt).then_inc(s_ctlchain, 1)
                    dve.wait_ge(s_ctlchain, 3 + 2 * n)
                    dve.tensor_reduce(cs[0:T, 5 + n:6 + n], d_bad[0:T, :], AX_X, ALU.add).then_inc(s_ctlchain, 1)
                    dve.wait_ge(s_ctlchain, 4 + 2 * n)
                dve.wait_ge(s_viol, 1)
                dve.tensor_scalar(cs[0:T, 7:8], ps_g[2][0:T, 0:1], 0.5, None, ALU.is_gt).then_inc(s_ctlchain, 1)
                dve.tensor_tensor(cs[0:T, 8:9], cs[0:T, 2:3], cs[0:T, 5:6], ALU.subtract).then_inc(s_ctlchain, 1)
                dve.tensor_scalar(cs[0:T, 9:10], cs[0:T, 6:7], -1.0, float(CHUNKS), ALU.mult, ALU.add).then_inc(s_ctlchain, 1)
                dve.wait_ge(s_ctlchain, 9)
                for n, count_ in enumerate((cs[0:T, 5:6], cs[0:T, 6:7])):
                    dve.scalar_tensor_tensor(out=ctl_i[0:T, n:n + 1], in0=cs[0:T, 8 + n:9 + n], scalar=cs[0:T, 7:8],
                                             in1=count_, op0=ALU.mult, op1=ALU.add).then_inc(s_ctlchain, 1)
                dve.tensor_scalar(ctl_i[0:T, 2:3], cs[0:T, 7:8], float(ROUNDS_ANY - ROUNDS), float(ROUNDS),
                                  ALU.mult, ALU.add).then_inc(s_ctlchain, 1)

            for b in range(LBATCHES + 1):
                nt = LB if b < LBATCHES else 1
                r = P if b < LBATCHES else LAST_ROWS
                dve.wait_ge(s_lx[b % 2], 16 * (b // 2 + 1))
                for t in range(nt):
                    l_inc(dve.bn_stats(lstat[0:r, t, :], lx[0:r, b % 2, t, :]))
                l_wait()
                for t in range(nt):
                    l_inc(dve.bn_aggr(lmv[0:r, t, :], lstat[0:r, t, :]))
                l_wait()
                l_inc(dve.tensor_scalar(lv[0:r, 0:nt], lmv[0:r, 0:nt, 1], LN_EPS, None, ALU.add))
                l_wait()
                rsqrt(lv[0:r, 0:nt], ly[0:r, 0:nt], lt[0:r, 0:nt], l_inc, l_wait)
                if b >= 2:
                    dve.wait_ge(s_lxn, b - 1)
                l_inc(dve.tensor_copy(lrs[0:r, b % 2, 0:nt], ly[0:r, 0:nt]))
                dve.scalar_tensor_tensor(out=lnm[0:r, b % 2, 0:nt], in0=lmv[0:r, 0:nt, 0], scalar=-1.0, in1=ly[0:r, 0:nt],
                                         op0=ALU.mult, op1=ALU.mult).then_inc(s_lrs, 1)
                if b == 0:
                    control_table()
                dve.wait_ge(s_lhi, b + 1)
                dve.scalar_tensor_tensor(out=ltab[0:r, b % 2, 0:nt, 1, :], in0=lxn[0:r, b % 2, 0:nt, :],
                                         scalar=TABLE_SCALE, in1=ltab[0:r, b % 2, 0:nt, 0, :],
                                         op0=ALU.mult, op1=ALU.subtract).then_inc(s_llo, 1)
            dve.wait_ge(s_wrs, 1)
            dve.tensor_tensor(wr[:, 1], wr_f[:, :, :], wr[:, 0].bitcast(F32), ALU.subtract).then_inc(s_wrs, 1)

            def split_mix(j, u):
                r = rows_of(j)
                dve.wait_ge(s_mhi, j + 1)
                dve.tensor_tensor(mxT[:, u, 1, :, 0:r], halves(ps_mt[u])[:, :, 0:r], mxT[:, u, 0, :, 0:r].bitcast(F32),
                                  ALU.subtract).then_inc(s_mlo, 1)

            def mix_tile(j, u):
                r = rows_of(j)
                if not beyond(j + 1):
                    split_mix(j + 1, 1 - u)
                dve.wait_ge(s_kvp, j + 1)
                wait_tile(dve, s_kva, j - 1)
                dve.tensor_tensor(kb[0:r, u, :], ps_kvp[u][0:r, 0:D], bkv[0:r, 0, :], ALU.add).then_inc(s_kb, 1)
                dve.tensor_tensor(vf[0:r, u, :, 0:P], halves(ps_kvp[u])[0:r, 1, :].rearrange("p (k c) -> p k c", k=KH),
                                  bkv[0:r, 1, :].rearrange("p (k c) -> p k c", k=KH), ALU.add).then_inc(s_kb, 1)
                dve.wait_ge(s_ke, j + 1)
                dve.scalar_tensor_tensor(out=kf[0:r, u, :], in0=kb[0:r, u, :], scalar=0.0, in1=kr[0:r, u, :],
                                         op0=ALU.max, op1=ALU.add).then_inc(s_kf, 1)

            split_mix(0, 0)
            mix_program(dve, mix_tile)
            dve.wait_ge(s_kva, TILES)
            for k in range(KH):
                dve.tensor_tensor(kvm[:, k, :], ps_kva[k][:, 0:P], headmask[:, :], ALU.mult)
                last = dve.tensor_copy(ksum[:, k:k + 1], ps_kva[k][:, P:P + 1])
            last.then_inc(s_kvx, 1)
            dve.wait_ge(s_kvx, 1)
            for k in range(KH):
                dve.tensor_scalar(ksm[:, k, :], headmask[:, :], ksum[:, k:k + 1], None, ALU.mult).then_inc(s_kvx, 1)
            dve.wait_ge(s_kvy, 1)
            dve.tensor_copy(kvmT[:, :, :], ps_g[0][:, 0:KH * P].rearrange("p (k c) -> p k c", k=KH)).then_inc(s_kvx, 1)
            dve.wait_ge(s_kvz, 1)
            dve.tensor_tensor(kvwo[:, 1, :, :], halves(ps_g[1]), kvwo[:, 0, :, :].bitcast(F32), ALU.subtract).then_inc(s_kvx, 1)

            gchain = Chain(s_gchain, G_CHAIN)

            def gate():
                dve.sem_inc(s_gate, 1)

            def lo_part(parts_, whole, s):
                return dve.tensor_tensor(tokens(parts_[:, 1], s), tokens(whole, s), tokens(parts_[:, 0], s).bitcast(F32), ALU.subtract)

            def stage(key, s, i, v):
                r, nt = rows(s), tiles_of(s)
                if key == "hot" and i < nt:
                    tile = s * SUPER + i
                    first = dve.value_load(control[0:1, tile, 0:1] if isinstance(tile, int) else control[0:1, bass.ds(tile, 1), 0],
                                           min_val=0, max_val=TILES * CHUNKS)
                    end = dve.value_load(control[0:1, tile + 1, 0:1] if isinstance(tile, int) else control[0:1, bass.ds(tile + 1, 1), 0],
                                         min_val=0, max_val=TILES * CHUNKS)
                    last_chunk = dve.value_load(control[0:1, tile, 1:2] if isinstance(tile, int) else control[0:1, bass.ds(tile, 1), 1],
                                                min_val=0, max_val=CHUNKS)
                    if not (isinstance(tile, int) and tile == 0):
                        dve.tensor_scalar(iota_t[:, :], iota_t[:, :], float(P), None, ALU.add).then_inc(s_iota, 1)
                        dve.wait_ge(s_iota, tile)
                        gate()
                    with dve.If(first < end):
                        with dve.Fori(first, end) as q:
                            dve.wait_ge(s_free, q + 1)
                            dve.tensor_scalar(onehot[:, q & (RING - 1), :], iota_t[:, :], dst_f[:, bass.ds(q % CHUNKS, 1)],
                                              None, ALU.is_equal).then_inc(s_hot, 1)
                    c_agg.wait(dve, s, i - 1)
                    dve.tensor_scalar(onehot1[:, i, :], iota_t[:, :], dst_f[:, bass.ds(last_chunk, 1)],
                                      None, ALU.is_equal).then_inc(c_hot1.sem, 1)
                elif key == "agg" and i < nt:
                    c_xe.wait(dve, s, 1)
                    c_th.wait(dve, s, 0)
                    c_agg.wait(dve, s, i + 1)
                    dve.scalar_tensor_tensor(out=h[0:r, i, :], in0=ps_agg[0:r, 0:D], scalar=1.0 / TABLE_SCALE, in1=xe[0:r, i, :],
                                             op0=ALU.mult, op1=ALU.add).then_inc(c_hp.sem, 1)
                    c_hp.wait(dve, s, i + 1)
                    dve.scalar_tensor_tensor(out=h[0:r, i, :], in0=ps_agg[0:r, D:2 * D], scalar=1.0 / TABLE_SCALE, in1=h[0:r, i, :],
                                             op0=ALU.mult, op1=ALU.add).then_inc(c_h.sem, 1)
                elif key == "l1":
                    c_ghi.wait(dve, s, i + 1)
                    lo_part(gT[:, i % 2], gact[:, i % 2], s).then_inc(c_glo.sem, 1)
                elif key == "l2":
                    c_l2.wait(dve, s, i + 1)
                    c_accb.wait(dve, s, 1) if i == 0 else c_add.wait(dve, s, i)
                    for t in range(nt):
                        last = dve.scalar_tensor_tensor(out=acc[0:r, v, t, :], in0=halves(ps_l2[i % 2])[0:r, t, :],
                                                        scalar=comb[0:r, v, t, i:i + 1], in1=acc[0:r, v, t, :],
                                                        op0=ALU.mult, op1=ALU.add)
                    last.then_inc(c_add.sem, 1)
                elif key == "bias2":
                    c_b2.wait(dve, s, 1)
                    c_acc.wait(dve, s, 1)
                    dve.tensor_tensor(cut(acc[:, v], s), cut(halves(ps_g[2]), s), cut(acc[:, v], s), ALU.add).then_inc(c_accb.sem, 1)
                elif key == "trans":
                    c_xhi.wait(dve, s, 1)
                    lo_part(xT, halves(ps_g[0]), s).then_inc(c_xlo.sem, 1)
                    c_hhi.wait(dve, s, 1)
                    lo_part(hT, halves(ps_g[1]), s).then_inc(c_hlo.sem, 1)
                elif key == "q":
                    c_qexp.wait(dve, s, 1)
                    for half in range(KH):
                        last = dve.scalar_tensor_tensor(out=tokens(qf, s)[:, half], in0=tokens(halves(ps_g[2]), s)[:, half],
                                                        scalar=bq1[:, half:half + 1], in1=tokens(ex, s)[:, half],
                                                        op0=ALU.add, op1=ALU.max)
                    last.then_inc(c_qf.sem, 1)
                elif key == "gin1":
                    c_rhi.wait(dve, s, 1)
                    lo_part(rTs, rT, s).then_inc(c_rlo.sem, 1)
                elif key == "norm":
                    c_ne.wait(dve, s, 1)
                    dve.reciprocal(tokens(nrm, s), tokens(nrm, s)).then_inc(c_nr.sem, 1)
                    c_nr.wait(dve, s, 1)
                    c_qhi.wait(dve, s, 0)
                    dve.tensor_tensor(tokens(qs, s), tokens(qf, s), tokens(nrm, s), ALU.mult).then_inc(c_qs.sem, 1)
                    c_qhi.wait(dve, s, 1)
                    lo_part(qTs, qs, s).then_inc(c_qlo.sem, 1)
                elif key == "out":
                    gchain.begin(s)
                    inc, wait = gchain.inc, lambda: gchain.wait(dve)
                    c_xs.wait(dve, s, 16)
                    dve.tensor_tensor(cut(xs, s), cut(xs, s), bout[0:r, :].rearrange("p (o c) -> p o c", o=1).broadcast_to([r, nt, D]),
                                      ALU.add).then_inc(c_xb.sem, 1)
                    c_xb.wait(dve, s, 1)
                    c_o.wait(dve, s, 1)
                    c_out.wait(dve, s, -16)
                    dve.tensor_tensor(cut(acc[:, v], s), cut(halves(ps_g[2]), s), cut(xs, s), ALU.add).then_inc(c_x1.sem, 1)
                    c_x1.wait(dve, s, 1)
                    for t in range(nt):
                        inc(dve.bn_stats(gstat[0:r, t, :], acc[0:r, v, t, :]))
                    wait()
                    gate()
                    for t in range(nt):
                        inc(dve.bn_aggr(gmv[0:r, t, :], gstat[0:r, t, :]))
                    wait()
                    inc(dve.tensor_scalar(gv[0:r, 0:nt], gmv[0:r, 0:nt, 1], LN_EPS, None, ALU.add))
                    wait()
                    c_tok.wait(dve, s, 0)
                    rsqrt(gv[0:r, 0:nt], gy[0:r, 0:nt], gt[0:r, 0:nt], inc, wait)
                    dve.scalar_tensor_tensor(out=gnm[0:r, 0:nt], in0=gmv[0:r, 0:nt, 0], scalar=-1.0, in1=gy[0:r, 0:nt],
                                             op0=ALU.mult, op1=ALU.mult).then_inc(c_ln.sem, 1)
                elif key == "tokT":
                    c_tok.wait(dve, s, 1)
                    dve.tensor_tensor(cut(acc[:, v], s), cut(acc[:, v], s), cut(tok, s), ALU.add).then_inc(c_acc.sem, 1)
                    c_khi.wait(dve, s, 1)
                    lo_part(tokT[:, v], halves(ps_g[0]), s).then_inc(c_klo.sem, 1)
                elif key == "router":
                    inc, wait = gchain.inc, lambda: gchain.wait(dve)
                    c_lg.wait(dve, s, 1)
                    gate()
                    for t in range(nt):
                        inc(dve.max(top[0:r, t, :], ps_g[1][0:r, t * NE:(t + 1) * NE]))
                    wait()
                    gate()
                    for t in range(nt):
                        inc(dve.max_index(topi[0:r, t, :], top[0:r, t, :], ps_g[1][0:r, t * NE:(t + 1) * NE]))
                    dve.tensor_scalar(ntop[0:r, 0:nt], top[0:r, 0:nt, 0], -1.0, None, ALU.mult).then_inc(c_top.sem, 1)
                    wait()
                    inc(dve.tensor_copy(topf[0:r, 0:nt, :], topi[0:r, 0:nt, 0:2]))
                    c_et.wait(dve, s, 1)
                    inc(dve.reciprocal(erec[0:r, 0:nt], esum[0:r, 0:nt]))
                    wait()

                    def over(ap, n):
                        return ap[0:r, 0:nt].rearrange("p (t o) -> p t o", o=1).broadcast_to([r, nt, n])

                    inc(dve.tensor_tensor(prob[0:r, 0:nt, :], etop[0:r, 0:nt, 0:2], over(erec, 2), ALU.mult))
                    wait()
                    inc(dve.tensor_tensor(pden[0:r, 0:nt], prob[0:r, 0:nt, 0], prob[0:r, 0:nt, 1], ALU.add))
                    wait()
                    inc(dve.tensor_scalar(pden[0:r, 0:nt], pden[0:r, 0:nt], 1e-12, None, ALU.max))
                    wait()
                    inc(dve.reciprocal(prec[0:r, 0:nt], pden[0:r, 0:nt]))
                    wait()
                    inc(dve.tensor_tensor(wtop[0:r, 0:nt, :], prob[0:r, 0:nt, :], over(prec, 2), ALU.mult))
                    for n, pick in enumerate((pick0, pick1)):
                        inc(dve.tensor_tensor(pick[0:r, 0:nt, :], iota8[0:r, :].rearrange("p (o c) -> p o c", o=1).broadcast_to([r, nt, NE]),
                                              topf[0:r, 0:nt, n:n + 1].broadcast_to([r, nt, NE]), ALU.is_equal))
                    wait()
                    for n, pick in enumerate((pick0, pick1)):
                        inc(dve.tensor_tensor(pick[0:r, 0:nt, :], pick[0:r, 0:nt, :],
                                              wtop[0:r, 0:nt, n:n + 1].broadcast_to([r, nt, NE]), ALU.mult))
                    wait()
                    c_ct.wait(dve, s, -1)
                    dve.tensor_tensor(comb[0:r, v, 0:nt, :], pick0[0:r, 0:nt, :], pick1[0:r, 0:nt, :], ALU.add).then_inc(c_comb.sem, 1)
                    assert nt < SUPER or gchain.k == G_CHAIN, gchain.k

            main_program(dve, stage)


def kernel(x, src, dst, edge_attr_16, L0_gnn_W1, L0_gnn_b1, L0_gnn_W2, L0_gnn_b2, L0_gnn_eps, L0_mix_wq, L0_mix_bq,
           L0_mix_wk, L0_mix_bk, L0_mix_wv, L0_mix_bv, L0_mix_wo, L0_mix_bo, L0_ffn_router_w, L0_ffn_w1, L0_ffn_b1,
           L0_ffn_w2, L0_ffn_b2):
    import numpy as np
    import concourse.bacc as bacc
    from concourse.bass_utils import run_bass_kernel_spmd

    def columns(v):
        return np.ascontiguousarray(np.asarray(v).reshape(-1, KH, P).transpose(2, 0, 1))

    slots = CHUNKS * P
    src_p = np.zeros(slots, np.int32)
    src_p[:E] = np.asarray(src)
    dst_p = np.full(slots + P, NO_NODE, np.int32)
    dst_p[:E] = np.asarray(dst)
    arrays = {
        "x": np.asarray(x),
        "src": np.ascontiguousarray(src_p.reshape(GROUPS, GROUP, P).transpose(0, 2, 1)).reshape(GROUPS * P, GROUP),
        "dst_columns": np.ascontiguousarray(dst_p.reshape(CHUNKS + 1, P).T),
        "dst_flat": dst_p,
        "wq": np.asarray(L0_mix_wq), "wk": np.asarray(L0_mix_wk), "wv": np.asarray(L0_mix_wv), "wo": np.asarray(L0_mix_wo),
        "wg1": np.asarray(L0_gnn_W1), "wg2": np.asarray(L0_gnn_W2), "we1": np.asarray(L0_ffn_w1), "we2": np.asarray(L0_ffn_w2),
        "bk": np.asarray(L0_mix_bk).reshape(1, D), "bv": np.asarray(L0_mix_bv).reshape(1, D),
        "bo": np.asarray(L0_mix_bo).reshape(1, D), "bg2": np.asarray(L0_gnn_b2).reshape(1, D),
        "eps": np.asarray(L0_gnn_eps).reshape(1, 1), "be2": np.asarray(L0_ffn_b2),
        "bq": columns(L0_mix_bq).reshape(P, KH), "bg1": columns(L0_gnn_b1).reshape(P, KH), "be1": columns(L0_ffn_b1),
        "wr": np.ascontiguousarray(np.asarray(L0_ffn_router_w).reshape(NE, KH, P).transpose(2, 1, 0)),
    }
    nc = bacc.Bacc("TRN2", target_bir_lowering=False, num_devices=1)
    aps = {k: nc.dram_tensor(f"in_{k}", list(a.shape), mybir.dt.from_np(a.dtype), kind="ExternalInput").ap()
           for k, a in arrays.items()}
    out = nc.dram_tensor("out", [N, D], F32, kind="ExternalOutput").ap()
    gps_layer(nc, aps["x"], aps["src"], aps["dst_columns"], aps["dst_flat"], aps, out)
    r = run_bass_kernel_spmd(nc, [{f"in_{k}": a for k, a in arrays.items()}], core_ids=[0])
    return r.results[0]["out"]
```

```python
from contextlib import ExitStack

import concourse.bass as bass
from concourse import mybir

F32 = mybir.dt.float32
F32R = mybir.dt.float32r
F16 = mybir.dt.float16
I32 = mybir.dt.int32
U32 = mybir.dt.uint32
ALU = mybir.AluOpType
ACT = mybir.ActivationFunctionType
AX_X = mybir.AxisListType.X

P = 128
D = 256
KH = D // P
N = 6250
NE = 8
HD = 32
TILES = -(-N // P)
LAST_ROWS = N - (TILES - 1) * P
SUPER = 2
STEPS = -(-TILES // SUPER)
E = 106250
J = 18
SEG = J * P
MAX_EXTRA = -(-E // SEG) - 1
CHUNKS = -(-E // (P * 32)) * 32
EDGES = CHUNKS * P + (MAX_EXTRA + 1) * SEG
NO_NODE = TILES * P
TABLE_SCALE = 2048.0
LN_EPS = 1e-5
NORM_EPS = 1e-6
LB = 4
LBATCHES = (TILES - 1) // LB
MAGIC = 0x5F3759DF
G_CHAIN = 31
CTL_CHUNKS = 7
CTL_CHAIN = CTL_CHUNKS + 12
PASSES = ((0, 0), (0, 1), (1, 0))


class Count:

    def __init__(self, sem, per):
        self.sem, self.per = sem, per

    def wait(self, eng, step, k):
        value = step * self.per + k
        if isinstance(value, int) and value <= 0:
            return
        eng.wait_ge(self.sem, value)


class Chain:

    def __init__(self, sem, per):
        self.sem, self.per, self.step, self.k = sem, per, 0, 0

    def begin(self, step):
        self.step, self.k = step, 0

    def inc(self, ins):
        ins.then_inc(self.sem, 1)
        self.k += 1

    def wait(self, eng):
        eng.wait_ge(self.sem, self.step * self.per + self.k)


def rows_of(tile):
    return LAST_ROWS if isinstance(tile, int) and tile == TILES - 1 else P


def tiles_of(step):
    return TILES - SUPER * step if isinstance(step, int) and step == STEPS - 1 else SUPER


def gps_layer(nc, x_d, src_d, dst_d, w, out_d):
    with ExitStack() as ctx:
        def sb(name, shape, dt=F32):
            return ctx.enter_context(nc.sbuf_tensor(name, shape, dt))

        def sem(name):
            return ctx.enter_context(nc.semaphore(name))

        xn_d = nc.dram_tensor("xn_scratch", [N, D], F32).ap()
        table_d = nc.dram_tensor("table_scratch", [N, 2 * D], F16).ap()
        ctl_d = nc.dram_tensor("control_scratch", [TILES, 2], I32).ap()
        rest_d = nc.dram_tensor("rest_scratch", [TILES * P, D], F32).ap()

        wkv = sb("wkv", [P, 2, KH, 2 * D], F32R)
        wq = sb("wq", [P, 2, KH, D], F32R)
        wg1 = sb("wg1", [P, 2, KH, D], F32R)
        wg2 = sb("wg2", [P, 2, KH, D], F32R)
        kvwo = sb("kvwo", [P, 2, KH, D], F32R)
        we1 = sb("we1", [P, 2, NE, KH, D], F32R)
        we2 = sb("we2", [P, 2, NE, KH, D], F32R)
        wr = sb("wr", [P, 2, KH, NE], F32R)
        wo = sb("wo", [P, KH, D])
        stage_w = sb("stage_w", [P, 2, 2 * KH, D])
        bkv = sb("bkv", [P, 2, D])
        bout = sb("bout", [P, D])
        bout2 = sb("bout2", [P, D])
        bq = sb("bq", [P, KH])
        nbq = sb("nbq", [P, KH])
        bq1 = sb("bq1", [P, KH])
        bg1 = sb("bg1", [P, KH])
        be1 = sb("be1", [P, NE, KH])
        be2 = sb("be2", [NE, D])
        eps1 = sb("eps1", [P, 1])

        ring = sb("ring", [P, 2, J, 2 * D], F16)
        onehot = sb("onehot", [P, 2, J, P], F16)
        idx_stage = sb("idx_stage", [P, 2, J], I32)
        dst_stage = sb("dst_stage", [P, 2, J], I32)
        dst_rel = sb("dst_rel", [P, 2, J], F16)
        tile_base = sb("tile_base", [P, TILES])
        iota_h = sb("iota_h", [P, P], F16)
        iota8 = sb("iota8", [P, NE])
        ident = sb("ident", [P, P])
        headmask = sb("headmask", [P, P])
        ones = sb("ones", [P, P])
        control = sb("control", [1, TILES, 2], I32)
        most = sb("most", [1, 1], I32)

        area = sb("area", [P, 7168])
        lx = area[:, 0:2048].rearrange("p (b t c) -> p b t c", b=2, t=LB)
        lxn = area[:, 2048:4096].rearrange("p (b t c) -> p b t c", b=2, t=LB)
        ltab = area[:, 4096:6144].bitcast(F16).rearrange("p (b t h c) -> p b t h c", b=2, t=LB, h=2)

        def two(n, k=512):
            return area[:, n:n + k]

        def view(n):
            return two(n).rearrange("p (t c) -> p t c", t=2)

        xs, xn2, xe, h = view(0), view(512), view(1024), view(1536)
        rT, ex, qf, nrm = view(2048), view(2560), view(3072), view(3584)
        qs, tok = view(4096), view(4608)
        acc = two(5120, 1024).rearrange("p (u t c) -> p u t c", u=2, t=2)
        gact = two(6144, 1024).rearrange("p (u t c) -> p u t c", u=2, t=2)
        mxn = two(0).rearrange("p (u c) -> p u c", u=2)
        kb = two(512).rearrange("p (u c) -> p u c", u=2)
        kr = two(1024).rearrange("p (u c) -> p u c", u=2)
        kf = two(1536).rearrange("p (u c) -> p u c", u=2)
        kvm = two(2048, KH * P).rearrange("p (k c) -> p k c", k=KH)
        kvmT = two(2304, KH * P).rearrange("p (k c) -> p k c", k=KH)
        vf = two(6144, 2 * KH * (P + 2)).rearrange("p (u k c) -> p u k c", u=2, k=KH)
        ring32 = ring[:, :, :, :].rearrange("p u s c -> p (u s c)").bitcast(F32)
        d_cur = ring32[:, 0:CHUNKS].bitcast(I32)
        d_next = ring32[:, CHUNKS:2 * CHUNKS].bitcast(I32)
        d_bad = ring32[:, 2 * CHUNKS:3 * CHUNKS]
        d_last = ring32[0:TILES, 3 * CHUNKS:4 * CHUNKS].bitcast(I32)
        d_row = ring32[0:TILES, 4 * CHUNKS:4 * CHUNKS + 2 * P].bitcast(I32).rearrange("p (n c) -> p n c", n=2)
        seg_ends = ring32[0:TILES, 4 * CHUNKS + 2 * P:4 * CHUNKS + 2 * P + MAX_EXTRA]

        lstat = sb("lstat", [P, LB, 6])
        lmv = sb("lmv", [P, LB, 2])
        lv = sb("lv", [P, LB])
        ly = sb("ly", [P, LB])
        lt = sb("lt", [P, LB])
        lrs = sb("lrs", [P, 2, LB])
        lnm = sb("lnm", [P, 2, LB])
        cs = sb("cs", [P, 16])
        ctl_i = sb("ctl_i", [P, 2], I32)
        row_i = sb("row_i", [P, 2], I32)

        ksm = sb("ksm", [P, KH, P])
        ksum = sb("ksum", [P, KH])

        xT = sb("xT", [P, 2, KH, 2 * P], F32R)
        mxT = xT[:, :, :, :].rearrange("p a k c -> p (a k c)").rearrange("p (u a k c) -> p u a k c", u=2, a=2, k=KH)
        hT = sb("hT", [P, 2, KH, 2 * P], F32R)
        rTs = sb("rTs", [P, 2, KH, 2 * P], F32R)
        qTs = sb("qTs", [P, 2, KH, 2 * P], F32R)
        tokT = sb("tokT", [P, 2, 2, KH, 2 * P], F32R)
        gT = wkv[:, :, :, :].rearrange("p a k c -> p (a k c)").rearrange("p (u a k c) -> p u a k c", u=2, a=2, k=KH)
        gstat = sb("gstat", [P, SUPER, 6])
        gmv = sb("gmv", [P, SUPER, 2])
        gv = sb("gv", [P, SUPER])
        gy = sb("gy", [P, SUPER])
        gt = sb("gt", [P, SUPER])
        gnm = sb("gnm", [P, SUPER])
        top = sb("top", [P, SUPER, 8])
        topi = sb("topi", [P, SUPER, 8], U32)
        topf = sb("topf", [P, SUPER, 2])
        ntop = sb("ntop", [P, SUPER])
        etop = sb("etop", [P, SUPER, 8])
        esum = sb("esum", [P, SUPER])
        erec = sb("erec", [P, SUPER])
        prob = sb("prob", [P, SUPER, 2])
        pden = sb("pden", [P, SUPER])
        prec = sb("prec", [P, SUPER])
        wtop = sb("wtop", [P, SUPER, 2])
        pick0 = sb("pick0", [P, SUPER, NE])
        pick1 = sb("pick1", [P, SUPER, NE])
        wr_f = sb("wr_f", [P, KH, NE])
        comb = sb("comb", [P, 2, SUPER, NE])
        combT = sb("combT", [NE, 2 * P])

        bank = [ctx.enter_context(nc.psum_tensor(f"bank{i}", [P, 512], F32)) for i in range(8)]
        ps_l1, ps_l2, ps_agg, ps_g = bank[0:2], bank[2:4], bank[4], bank[5:8]
        ps_kvp, ps_kva, ps_mt = bank[0:2], bank[2:4], bank[5:7]

        s_bias, s_wload, s_wo = sem("bias_loaded"), [sem("weights_loaded0"), sem("weights_loaded1")], sem("wo_loaded")
        s_whi, s_wlo = sem("weight_hi"), sem("weight_lo")
        s_const, s_bprep = sem("constants"), sem("biases_prepared")
        s_dst, s_ctlchain, s_viol = sem("dst_loaded"), sem("control_chain"), sem("violations_summed")
        s_ctlo, s_ctl, s_most = sem("control_stored"), sem("control_loaded"), sem("control_complete")
        s_row = [sem("chunk_rows0"), sem("chunk_rows1")]
        s_lx = [sem("ln_x_loaded0"), sem("ln_x_loaded1")]
        s_lchain, s_lxn, s_lhi, s_llo = sem("ln_chain"), sem("ln_xn"), sem("ln_table_hi"), sem("ln_table_lo")
        s_lrs = sem("ln_scales")
        s_lout = [sem("ln_stored0"), sem("ln_stored1")]
        s_mxn = [sem("mix_xn_loaded0"), sem("mix_xn_loaded1")]
        s_mt, s_mhi, s_mlo = sem("mix_transposed"), sem("mix_hi"), sem("mix_lo")
        s_kvp, s_kb, s_kr, s_ke = sem("kv_projected"), sem("kv_biased"), sem("k_negative_part"), sem("k_exp")
        s_kf, s_kva, s_kv1 = sem("k_features"), sem("kv_accumulated"), sem("v_ones")
        s_kvx, s_kvy = sem("kvwo_vector"), sem("kvwo_tensor")
        s_kvz = sem("kvwo_scalar")
        s_idx = [sem("indices_loaded0"), sem("indices_loaded1")]
        s_dstl = [sem("segment_dst_loaded0"), sem("segment_dst_loaded1")]
        s_gath = [sem("rows_gathered0"), sem("rows_gathered1")]
        s_grant = sem("gather_granted")
        s_table = sem("table_complete")
        s_xidx, s_xdst, s_xbase, s_xgath = sem("rest_indices"), sem("rest_dst"), sem("rest_loaded"), sem("rest_gathered")
        s_xhot, s_xsum, s_xadd, s_xout = sem("rest_onehot"), sem("rest_summed"), sem("rest_added"), sem("rest_stored")
        s_xchain = sem("rest_chain")
        s_wrs = sem("router_weights_split")
        s_gate = sem("gate_passed")

        def count(name, per):
            return Count(sem(name), per)

        c_rel, c_hot = count("dst_relative", 2), count("onehot_ready", 2)
        c_rest, c_xr = count("rest_reloaded", 16), count("rest_joined", 1)
        c_xs, c_xn2 = count("x_loaded", 16), count("xn_loaded", 16)
        c_xe, c_agg, c_h = count("xn_scaled", 1), count("segment_summed", 2), count("h_ready", 2)
        c_hp = count("h_first_part", 2)
        c_tx, c_th = count("xT_in_psum", 1), count("hT_in_psum", 1)
        c_xhi, c_xlo = count("xT_hi", 1), count("xT_lo", 1)
        c_hhi, c_hlo = count("hT_hi", 1), count("hT_lo", 1)
        c_q, c_qneg, c_qexp, c_qf = count("q_product", 1), count("q_negative", 1), count("q_exp", 1), count("q_features", 1)
        c_w1, c_r, c_rhi, c_rlo = count("gin1_product", 1), count("gin1_relu", 1), count("gin1_hi", 1), count("gin1_lo", 1)
        c_n, c_ne, c_nr, c_qs = count("norm_product", 1), count("norm_eps", 1), count("norm_reciprocal", 1), count("q_normed", 1)
        c_qhi, c_qlo = count("q_hi", 1), count("q_lo", 1)
        c_o, c_xb, c_x1 = count("layer_product", 1), count("x_plus_bias", 1), count("residual1", 1)
        c_ln, c_tok, c_acc = count("ln2_scales", 1), count("tokens_normed", 1), count("acc_started", 1)
        c_tk, c_khi, c_klo = count("tokT_in_psum", 1), count("tokT_hi", 1), count("tokT_lo", 1)
        c_lg, c_top, c_et, c_comb = count("logits", 1), count("top_logits", 1), count("top_exp", 1), count("combine_weights", 1)
        c_out = count("out_stored", 16)
        c_ct, c_ctc, c_b2, c_accb = count("combT_in_psum", 1), count("combT_copied", 1), count("bias2_product", 1), count("acc_with_bias", 1)
        c_l1, c_g, c_ghi, c_glo = count("expert_l1", NE), count("gelu", NE), count("gelu_hi", NE), count("gelu_lo", NE)
        c_l2, c_add = count("expert_l2", NE), count("expert_added", NE)
        s_gchain = sem("ln2_router_chain")

        def rows(s):
            return P if tiles_of(s) == SUPER else LAST_ROWS

        def super_rows(dram, s):
            if tiles_of(s) == 1:
                return dram[s * SUPER * P:N, :]
            return dram[bass.ds(s * (SUPER * P), SUPER * P), :].rearrange("(t p) c -> p t c", p=P)

        def super_buf(buf, s):
            return buf[0:LAST_ROWS, 0, :] if tiles_of(s) == 1 else buf

        def cut(buf, s):
            return buf[0:rows(s), 0:tiles_of(s)]

        def tokens(buf, s):
            return buf[:, :, 0:(SUPER * P if tiles_of(s) == SUPER else LAST_ROWS)]

        def halves(b):
            return b[:, :].rearrange("p (t c) -> p t c", t=2)

        ORDER = ["hot 0", "l1 0", "combT", "l1 1", "store", "bias2", "trans", "loadxn", "l1 2", "l2 0",
                 "q", "l1 3", "l2 1", "gin1", "l1 4", "l2 2", "norm", "hot 1", "agg 0", "l1 5", "l2 3",
                 "out", "l1 6", "l2 4", "agg 1", "l1 7", "l2 5", "tokT", "l2 6", "router", "l2 7"]
        STAGE = {"hot": "a", "agg": "a", "loadxn": "a", "l1": "m", "l2": "m", "combT": "m", "bias2": "m",
                 "store": "m", "trans": "g", "q": "g", "gin1": "g", "norm": "g", "out": "g", "tokT": "g",
                 "router": "g"}
        LOOP_FROM = 2
        TURNS = (STEPS - 1 - 2 - LOOP_FROM) // 2

        def main_program(eng, stage_fn):
            def step(a, g, m, u):
                for name in ORDER:
                    key, *arg = name.split()
                    s = {"a": a, "g": g, "m": m}[STAGE[key]]
                    if s is not None:
                        stage_fn(key, s, int(arg[0]) if arg else None, 1 - u if STAGE[key] == "g" else u)

            def alone(n):
                step(*(n - k if 0 <= n - k < STEPS else None for k in range(3)), n % 2)

            for n in range(LOOP_FROM + 2):
                alone(n)
            with eng.Fori(0, TURNS) as turn:
                for b in range(2):
                    step(*(turn * 2 + (LOOP_FROM + b + k) for k in (2, 1, 0)), b)
            for n in range(LOOP_FROM + 2 + 2 * TURNS, STEPS + 2):
                alone(n)

        MIX_AHEAD = 3
        MIX_TURNS = (TILES - 1 - MIX_AHEAD) // 2

        def mix_program(eng, tile_fn):
            tile_fn(0, 0)
            tile_fn(1, 1)
            with eng.Fori(1, MIX_TURNS) as turn:
                tile_fn(turn * 2, 0)
                tile_fn(turn * 2 + 1, 1)
            for j in range(2 * MIX_TURNS, TILES):
                tile_fn(j, j % 2)

        def pair_program(eng, tile_fn):
            for u in range(2):
                tile_fn(u, 0, u)
            with eng.Fori(1, TILES // 2) as r:
                for u in range(2):
                    tile_fn(r * 2 + u, r, u)
            for tile in range(TILES // 2 * 2, TILES):
                tile_fn(tile, tile // 2, tile % 2)

        def beyond(j, k=TILES):
            return isinstance(j, int) and j >= k

        def wait_tile(eng, s, value):
            if not (isinstance(value, int) and value <= 0):
                eng.wait_ge(s, value)

        weights = [([w["wk"], w["wv"]], "kv"), ([w["wq"], w["wg1"]], "q1"), ([w["wg2"]], "g2")]
        weights += [([w["we1"][e], w["we2"][e]], e) for e in range(NE)]
        PIECES = [0]
        for sources, _ in weights:
            PIECES.append(PIECES[-1] + len(sources))

        def parts(n, part):
            key = weights[n][1]
            if key == "kv":
                dst = [wkv[:, part, :, 0:D], wkv[:, part, :, D:2 * D]]
            elif key == "q1":
                dst = [wq[:, part], wg1[:, part]]
            elif key == "g2":
                dst = [wg2[:, part]]
            else:
                dst = [we1[:, part, key], we2[:, part, key]]
            return [(d, stage_w[:, n % 2, i * KH:(i + 1) * KH, :]) for i, d in enumerate(dst)]

        def loaded_pieces(n):
            return sum(PIECES[i + 1] - PIECES[i] for i in range(n % 2, n + 1, 2))

        block = ctx.enter_context(nc.Block())

        @block.sync
        def _(sp):
            def batch(dram, b):
                if b == LBATCHES:
                    return dram[b * LB * P:N, :]
                return dram[b * LB * P:(b + 1) * LB * P, :].rearrange("(t p) c -> p t c", p=P)

            def load_x(b):
                if b >= 2:
                    sp.wait_ge(s_lxn, b - 1)
                to = lx[:, b % 2] if b < LBATCHES else lx[0:LAST_ROWS, b % 2, 0, :]
                sp.dma_start(to, batch(x_d, b)).then_inc(s_lx[b % 2], 16)

            def load_w(n):
                if n >= 2:
                    sp.wait_ge(s_wlo, PIECES[n - 1])
                for i, source in enumerate(weights[n][0]):
                    sp.dma_start(stage_w[:, n % 2, i * KH:(i + 1) * KH, :],
                                 source.rearrange("(k p) n -> p k n", p=P)).then_inc(s_wload[n % 2], 16)

            load_x(0)
            load_x(1)
            sp.dma_start(d_cur, dst_d[0:P * CHUNKS].rearrange("(p c) -> p c", p=P)).then_inc(s_dst, 16)
            sp.dma_start(d_next, dst_d[1:P * CHUNKS + 1].rearrange("(p c) -> p c", p=P)).then_inc(s_dst, 16)
            sp.dma_start(d_last, w["last_dst"].broadcast_to([TILES, CHUNKS])).then_inc(s_dst, 16)
            load_w(0)
            load_w(1)
            sp.dma_start(wo[:, :, :], w["wo"].rearrange("(k p) n -> p k n", p=P)).then_inc(s_wo, 16)
            for b in range(LBATCHES + 1):
                last = b == LBATCHES
                sp.wait_ge(s_lxn, b + 1)
                sp.dma_start(batch(xn_d, b), lxn[0:LAST_ROWS, b % 2, 0, :] if last else lxn[:, b % 2]
                             ).then_inc(s_lout[b % 2], 16)
                sp.wait_ge(s_llo, b + 1)
                rows16 = ltab[0:LAST_ROWS, b % 2, 0].rearrange("p h c -> p (h c)") if last else \
                    ltab[:, b % 2].rearrange("p t h c -> p t (h c)")
                sp.dma_start(batch(table_d, b), rows16).then_inc(s_lout[b % 2], 16)
                if b + 2 <= LBATCHES:
                    load_x(b + 2)
                if b + 2 < len(weights):
                    load_w(b + 2)
                if b == 3:
                    sp.wait_ge(s_ctlchain, CTL_CHAIN)
                    sp.dma_start(ctl_d, ctl_i[0:TILES, :]).then_inc(s_ctlo, 16)
                    sp.wait_ge(s_ctlo, 16)
                    sp.dma_start(control[:, :, :], ctl_d.rearrange("(o t) c -> o t c", o=1)).then_inc(s_ctl, 16)
            for b in range(2):
                sp.wait_ge(s_lout[b], 32 * len(range(b, LBATCHES + 1, 2)))
            sp.sem_inc(s_table, 1)
            sp.wait_ge(s_most, 1)

            def start_of(tile):
                return sp.value_load(control[0:1, tile, 0:1] if isinstance(tile, int) else control[0:1, bass.ds(tile, 1), 0],
                                     min_val=0, max_val=E)

            def segment(dram, start):
                return dram[bass.ds(start, SEG)].rearrange("(p j) -> p j", p=P)

            extra = sp.value_load(most[0:1, 0:1], min_val=0, max_val=MAX_EXTRA)
            with sp.If(extra > 0):
                with sp.Fori(0, TILES) as tile:
                    sp.dma_start(rest_d[bass.ds(tile * P, P), :], bout2[:, :]).then_inc(s_xout, 16)
                    sp.wait_ge(s_xout, 16)
                    sp.sem_clear(s_xout)
                with sp.Fori(0, extra) as k:
                    with sp.Fori(0, TILES) as tile:
                        start = start_of(tile)
                        sp.dma_start(idx_stage[:, 0, :], segment(src_d, start + (k * SEG + SEG))).then_inc(s_xidx, 16)
                        sp.dma_start(dst_stage[:, 0, :], segment(dst_d, start + (k * SEG + SEG))).then_inc(s_xdst, 16)
                        sp.dma_start(xe[:, 0, :], rest_d[bass.ds(tile * P, P), :]).then_inc(s_xbase, 16)
                        sp.wait_ge(s_xadd, 1)
                        sp.sem_clear(s_xadd)
                        sp.dma_start(rest_d[bass.ds(tile * P, P), :], xe[:, 0, :]).then_inc(s_xout, 16)
                        sp.wait_ge(s_xout, 16)
                        sp.sem_clear(s_xout)

            def indices(tile, r, u):
                start = start_of(tile)
                if not (isinstance(r, int) and r == 0):
                    sp.wait_ge(s_gath[u], r * (16 * J))
                    sp.sem_inc(s_gate, 1)
                    sp.wait_ge(c_rel.sem, tile - 1)
                    sp.sem_inc(s_gate, 1)
                sp.dma_start(idx_stage[:, u, :], segment(src_d, start)).then_inc(s_idx[u], 16)
                sp.dma_start(dst_stage[:, u, :], segment(dst_d, start)).then_inc(s_dstl[u], 16)

            pair_program(sp, indices)

        @block.gpsimd
        def _(pool):
            for u in range(2):
                pool.memset(vf[:, u, :, P:P + 2], 1.0).then_inc(s_kv1, 1)
            pool.memset(ident[:, :], 0.0).then_inc(s_const, 1)
            pool.memset(headmask[:, :], 0.0).then_inc(s_const, 1)
            pool.memset(ones[:, :], 1.0).then_inc(s_const, 1)
            pool.iota(tile_base[:, :], [[P, TILES]], base=0, channel_multiplier=0,
                      allow_small_or_imprecise_dtypes=True).then_inc(s_const, 1)
            pool.iota(iota_h[:, :], [[1, P]], base=0, channel_multiplier=0,
                      allow_small_or_imprecise_dtypes=True).then_inc(s_const, 1)
            pool.iota(iota8[:, :], [[1, NE]], base=0, channel_multiplier=0,
                      allow_small_or_imprecise_dtypes=True).then_inc(s_const, 1)
            pool.iota(cs[:, 0:2], [[P, 2]], base=0, channel_multiplier=P,
                      allow_small_or_imprecise_dtypes=True).then_inc(s_const, 1)
            pool.iota(seg_ends, [[SEG, MAX_EXTRA]], base=SEG, channel_multiplier=0,
                      allow_small_or_imprecise_dtypes=True).then_inc(s_const, 1)
            pool.wait_ge(s_const, 8)
            pool.affine_select(out=ident[:, :], in_=ident[:, :], compare_op=ALU.not_equal, fill=1.0, base=0,
                               pattern=[[-1, P]], channel_multiplier=1).then_inc(s_const, 1)
            for b in range(P // HD):
                pool.wait_ge(s_const, 9 + b)
                pool.memset(headmask[b * HD:(b + 1) * HD, b * HD:(b + 1) * HD], 1.0).then_inc(s_const, 1)
            pool.wait_ge(s_const, 9 + P // HD)
            pool.wait_ge(s_ctlchain, CTL_CHUNKS)
            for n in range(2):
                pool.indirect_dma_start(
                    out=d_row[:, n, :], out_offset=None, in_=dst_d[0:(CHUNKS + 1) * P].rearrange("(c p) -> c p", p=P),
                    in_offset=bass.IndirectOffsetOnAxis(ap=row_i[0:TILES, n:n + 1].bitcast(U32), axis=0),
                    bounds_check=CHUNKS, oob_is_err=False).then_inc(s_row[n], 16)
            for n in range(len(weights)):
                pool.wait_ge(s_whi, PIECES[n + 1])
                for (lo, whole), (hi, _) in zip(parts(n, 1), parts(n, 0)):
                    pool.tensor_tensor(out=lo, in0=whole, in1=hi.bitcast(F32), op=ALU.subtract).then_inc(s_wlo, 1)
            def gather(u, j, landed):
                pool.indirect_dma_start(
                    out=ring[:, u, j, :].bitcast(F32), out_offset=None, in_=table_d.bitcast(F32),
                    in_offset=bass.IndirectOffsetOnAxis(ap=idx_stage[:, u, j:j + 1].bitcast(U32), axis=0),
                    bounds_check=N - 1, oob_is_err=False).then_inc(landed, 16)

            pool.wait_ge(s_table, 1)
            pool.wait_ge(s_most, 1)
            extra = pool.value_load(most[0:1, 0:1], min_val=0, max_val=MAX_EXTRA)
            with pool.If(extra > 0):
                with pool.Fori(0, extra):
                    with pool.Fori(0, TILES):
                        pool.wait_ge(s_xidx, 16)
                        pool.sem_clear(s_xidx)
                        for j in range(J):
                            gather(0, j, s_xgath)

            def gathers(tile, r, u):
                pool.wait_ge(s_idx[u], r * 16 + 16)
                if not isinstance(r, int):
                    pool.sem_inc(s_grant, 1)
                if not (isinstance(r, int) and r == 0):
                    pool.wait_ge(c_agg.sem, tile - 1)
                    if not isinstance(r, int):
                        pool.sem_inc(s_grant, 1)
                for j in range(J):
                    gather(u, j, s_gath[u])

            pair_program(pool, gathers)

        @block.scalar
        def _(act):
            act.dma_start(bkv[:, 0, :], w["bk"].broadcast_to([P, D])).then_inc(s_bias, 16)
            act.dma_start(bkv[:, 1, :], w["bv"].broadcast_to([P, D])).then_inc(s_bias, 16)
            act.dma_start(bout[:, :], w["bg2"].broadcast_to([P, D])).then_inc(s_bias, 16)
            act.dma_start(bout2[:, :], w["bo"].broadcast_to([P, D])).then_inc(s_bias, 16)
            act.dma_start(bq[:, :], w["bq"]).then_inc(s_bias, 16)
            act.dma_start(bg1[:, :], w["bg1"]).then_inc(s_bias, 16)
            act.dma_start(be1[:, :, :], w["be1"]).then_inc(s_bias, 16)
            act.dma_start(be2[:, :], w["be2"]).then_inc(s_bias, 16)
            act.dma_start(eps1[:, :], w["eps"].broadcast_to([P, 1])).then_inc(s_bias, 16)
            act.dma_start(wr_f[:, :, :], w["wr"]).then_inc(s_bias, 16)

            for b in range(LBATCHES + 1):
                nt = LB if b < LBATCHES else 1
                r = P if b < LBATCHES else LAST_ROWS
                act.wait_ge(s_lrs, b + 1)
                if b >= 2:
                    act.wait_ge(s_lout[b % 2], 32 * (b // 2))
                for t in range(nt):
                    last = act.activation(lxn[0:r, b % 2, t, :], lx[0:r, b % 2, t, :], ACT.Identity,
                                          bias=lnm[0:r, b % 2, t:t + 1], scale=lrs[0:r, b % 2, t:t + 1])
                last.then_inc(s_lxn, 1)
                act.wait_ge(s_lxn, b + 1)
                act.activation(ltab[0:r, b % 2, 0:nt, 0, :], lxn[0:r, b % 2, 0:nt, :], ACT.Copy,
                               scale=TABLE_SCALE).then_inc(s_lhi, 1)
                if b < len(weights):
                    act.wait_ge(s_wload[b % 2], 16 * loaded_pieces(b))
                    for hi, whole in parts(b, 0):
                        act.activation(hi, whole, ACT.Copy).then_inc(s_whi, 1)
                if b == 0:
                    act.wait_ge(s_bias, 160)
                    act.activation(wr[:, 0], wr_f[:, :, :], ACT.Copy).then_inc(s_wrs, 1)

            def load_mix(j, u):
                wait_tile(act, s_mt, j - 1)
                src = xn_d[j * P:j * P + rows_of(j), :] if isinstance(j, int) else xn_d[bass.ds(j * P, P), :]
                act.dma_start(mxn[0:rows_of(j), u, :], src).then_inc(s_mxn[u], 16)

            def split_mix(j, u):
                r = rows_of(j)
                act.wait_ge(s_mt, j + 1)
                wait_tile(act, s_kvp, j - 1)
                act.activation(mxT[:, u, 0, :, 0:r], halves(ps_mt[u])[:, :, 0:r], ACT.Copy).then_inc(s_mhi, 1)

            def mix_tile(j, u):
                if not beyond(j + 1):
                    split_mix(j + 1, 1 - u)
                    if not beyond(j + MIX_AHEAD):
                        load_mix(j + MIX_AHEAD, 1 - u)
                r = rows_of(j)
                act.wait_ge(s_kb, 2 * j + 1)
                wait_tile(act, s_kf, j - 1)
                act.activation(kr[0:r, u, :], kb[0:r, u, :], ACT.Relu, scale=-1.0).then_inc(s_kr, 1)
                act.wait_ge(s_kr, j + 1)
                act.activation(kr[0:r, u, :], kr[0:r, u, :], ACT.Exp, scale=-1.0).then_inc(s_ke, 1)

            act.wait_ge(s_table, 1)
            act.wait_ge(s_most, 1)
            act_extra = act.value_load(most[0:1, 0:1], min_val=0, max_val=MAX_EXTRA)
            load_mix(0, 0)
            load_mix(1, 1)
            split_mix(0, 0)
            load_mix(2, 0)
            mix_program(act, mix_tile)
            act.wait_ge(s_kvy, 2)
            act.activation(kvwo[:, 0, :, :], halves(ps_g[1]), ACT.Copy).then_inc(s_kvz, 1)

            def stage(key, s, i, v):
                if key == "loadxn":
                    c_tx.wait(act, s, 0)
                    c_xe.wait(act, s, 0)
                    act.dma_start(super_buf(xn2, s), super_rows(xn_d, s)).then_inc(c_xn2.sem, 16)
                elif key == "l1":
                    c_l1.wait(act, s, i + 1)
                    c_glo.wait(act, s, i - 1)
                    for half in range(KH):
                        last = act.activation(tokens(gact[:, i % 2], s)[:, half], tokens(halves(ps_l1[i % 2]), s)[:, half],
                                              ACT.Gelu, bias=be1[:, i, half:half + 1])
                    last.then_inc(c_g.sem, 1)
                    c_g.wait(act, s, i + 1)
                    c_l2.wait(act, s, i - 1)
                    act.activation(tokens(gT[:, i % 2, 0], s), tokens(gact[:, i % 2], s), ACT.Copy).then_inc(c_ghi.sem, 1)
                elif key == "store" and not (isinstance(s, int) and s == 0):
                    c_add.wait(act, s, 0)
                    act.dma_start(super_rows(out_d, s - 1), super_buf(acc[:, 1 - v], s - 1)).then_inc(c_out.sem, 16)
                elif key == "combT":
                    c_ct.wait(act, s, 1)
                    n = SUPER * P if tiles_of(s) == SUPER else LAST_ROWS
                    act.activation(combT[:, 0:n], ps_g[2][0:NE, 0:n], ACT.Copy).then_inc(c_ctc.sem, 1)
                elif key == "trans":
                    c_x1.wait(act, s, 0)
                    act.dma_start(super_buf(xs, s), super_rows(x_d, s)).then_inc(c_xs.sem, 16)
                    c_tx.wait(act, s, 1)
                    c_q.wait(act, s, 0)
                    act.activation(tokens(xT[:, 0], s), tokens(halves(ps_g[0]), s), ACT.Copy).then_inc(c_xhi.sem, 1)
                    c_th.wait(act, s, 1)
                    c_w1.wait(act, s, 0)
                    act.activation(tokens(hT[:, 0], s), tokens(halves(ps_g[1]), s), ACT.Copy).then_inc(c_hhi.sem, 1)
                elif key == "q":
                    c_q.wait(act, s, 1)
                    c_qf.wait(act, s, 0)
                    for half in range(KH):
                        last = act.activation(tokens(ex, s)[:, half], tokens(halves(ps_g[2]), s)[:, half], ACT.Relu,
                                              bias=nbq[:, half:half + 1], scale=-1.0)
                    last.then_inc(c_qneg.sem, 1)
                    c_qneg.wait(act, s, 1)
                    act.activation(tokens(ex, s), tokens(ex, s), ACT.Exp, scale=-1.0).then_inc(c_qexp.sem, 1)
                elif key == "gin1":
                    c_w1.wait(act, s, 1)
                    c_rlo.wait(act, s, 0)
                    for half in range(KH):
                        last = act.activation(tokens(rT, s)[:, half], tokens(halves(ps_g[0]), s)[:, half], ACT.Relu,
                                              bias=bg1[:, half:half + 1])
                    last.then_inc(c_r.sem, 1)
                    c_r.wait(act, s, 1)
                    c_o.wait(act, s, 0)
                    act.activation(tokens(rTs[:, 0], s), tokens(rT, s), ACT.Copy).then_inc(c_rhi.sem, 1)
                elif key == "norm":
                    c_n.wait(act, s, 1)
                    c_qs.wait(act, s, 0)
                    act.activation(tokens(nrm, s), tokens(halves(ps_g[1]), s), ACT.Copy, bias=NORM_EPS).then_inc(c_ne.sem, 1)
                    c_qs.wait(act, s, 1)
                    act.activation(tokens(qTs[:, 0], s), tokens(qs, s), ACT.Copy).then_inc(c_qhi.sem, 1)
                elif key == "agg" and i == 0:
                    c_xn2.wait(act, s, 16)
                    c_h.wait(act, s, 0)
                    act.activation(cut(xe, s), cut(xn2, s), ACT.Copy, scale=eps1[0:rows(s), 0:1]).then_inc(c_xe.sem, 1)
                    with act.If(act_extra > 0):
                        c_th.wait(act, s, 0)
                        act.dma_start(super_buf(h, s), super_rows(rest_d, s)).then_inc(c_rest.sem, 16)
                elif key == "tokT":
                    c_ln.wait(act, s, 1)
                    c_acc.wait(act, s, 0)
                    for t in range(tiles_of(s)):
                        last = act.activation(tok[0:rows(s), t, :], acc[0:rows(s), v, t, :], ACT.Identity,
                                              bias=gnm[0:rows(s), t:t + 1], scale=gy[0:rows(s), t:t + 1])
                    last.then_inc(c_tok.sem, 1)
                    c_tk.wait(act, s, 1)
                    c_l1.wait(act, s, -NE)
                    act.activation(tokens(tokT[:, v, 0], s), tokens(halves(ps_g[0]), s), ACT.Copy).then_inc(c_khi.sem, 1)
                elif key == "router":
                    c_top.wait(act, s, 1)
                    for t in range(tiles_of(s)):
                        last = act.activation(etop[0:rows(s), t, :], top[0:rows(s), t, :], ACT.Exp,
                                              bias=ntop[0:rows(s), t:t + 1], accum_out=esum[0:rows(s), t:t + 1])
                    last.then_inc(c_et.sem, 1)

            main_program(act, stage)
            last = STEPS - 1
            c_add.wait(act, last, NE)
            act.dma_start(super_rows(out_d, last), super_buf(acc[:, last % 2], last)).then_inc(c_out.sem, 16)
            act.wait_ge(c_out.sem, 16 * STEPS)

        @block.tensor
        def _(pe):
            pe.wait_ge(s_const, 9 + P // HD)
            pe.wait_ge(s_ctlchain, 2)
            pe.matmul(ps_g[2][0:TILES, 0:1], ones[:, 0:TILES], cs[:, 4:5], start=True, stop=True).then_inc(s_viol, 1)

            def segment_sum(u):
                for j in range(J):
                    last = pe.matmul(ps_agg[:, :], onehot[:, u, j, :], ring[:, u, j, :], start=j == 0, stop=j == J - 1)
                return last

            pe.wait_ge(s_most, 1)
            extra = pe.value_load(most[0:1, 0:1], min_val=0, max_val=MAX_EXTRA)
            with pe.If(extra > 0):
                with pe.Fori(0, extra):
                    with pe.Fori(0, TILES):
                        pe.wait_ge(s_xhot, 1)
                        pe.sem_clear(s_xhot)
                        pe.wait_ge(s_xgath, 16 * J)
                        pe.sem_clear(s_xgath)
                        segment_sum(0).then_inc(s_xsum, 1)

            def transposes_mix(j, u):
                r = rows_of(j)
                if isinstance(j, int):
                    pe.wait_ge(s_mxn[u], 16 * (j // 2 + 1))
                else:
                    pe.wait_ge(s_mxn[u], j * 8 + (16 - 8 * u))
                wait_tile(pe, s_mlo, j - 1)
                for k in range(KH):
                    last = pe.transpose(halves(ps_mt[u])[:, k, 0:r], mxn[0:r, u, k * P:(k + 1) * P], ident[0:r, 0:r])
                last.then_inc(s_mt, 1)

            def project_mix(j, u):
                r = rows_of(j)
                pe.wait_ge(s_mhi, j + 1)
                pe.wait_ge(s_mlo, j + 1)
                wait_tile(pe, s_kb, 2 * (j - 1))
                n = 0
                for wp, ap in PASSES:
                    for k in range(KH):
                        last = pe.matmul(ps_kvp[u][0:r, :], mxT[:, u, ap, k, 0:r], wkv[:, wp, k, :],
                                         start=n == 0, stop=n == len(PASSES) * KH - 1)
                        n += 1
                last.then_inc(s_kvp, 1)

            def accumulate_mix(j, u):
                r = rows_of(j)
                pe.wait_ge(s_kf, j + 1)
                pe.wait_ge(s_kb, 2 * j + 2)
                for k in range(KH):
                    last = pe.matmul(ps_kva[k][:, 0:P + 1], kf[0:r, u, k * P:(k + 1) * P], vf[0:r, u, k, 0:P + 1],
                                     start=isinstance(j, int) and j == 0, stop=isinstance(j, int) and j == TILES - 1,
                                     skip_group_check=True)
                last.then_inc(s_kva, 1)

            def mix_tile(j, u):
                if not beyond(j + 1):
                    transposes_mix(j + 1, 1 - u)
                project_mix(j, u)
                if not (isinstance(j, int) and j == 0):
                    accumulate_mix(j - 1, 1 - u)

            pe.wait_ge(s_wlo, PIECES[1])
            pe.wait_ge(s_kv1, 2)
            transposes_mix(0, 0)
            mix_program(pe, mix_tile)
            accumulate_mix(TILES - 1, (TILES - 1) % 2)
            pe.wait_ge(s_kvx, 3)
            for k in range(KH):
                last = pe.transpose(ps_g[0][:, k * P:(k + 1) * P], kvm[:, k, :], ident[:, :])
            last.then_inc(s_kvy, 1)
            pe.wait_ge(s_kvx, 4)
            pe.wait_ge(s_wo, 16)
            for k in range(KH):
                last = pe.matmul(halves(ps_g[1])[:, k, :], kvmT[:, k, :], wo[:, k, :], start=True, stop=True)
            last.then_inc(s_kvy, 1)

            pe.wait_ge(s_wlo, PIECES[-1])
            pe.wait_ge(s_wrs, 2)

            def product_T(bank_, weight, act_parts, s):
                for half in range(KH):
                    n = 0
                    for wp, ap in PASSES:
                        for k in range(KH):
                            last = pe.matmul(tokens(halves(bank_), s)[:, half], weight[:, wp, k, half * P:(half + 1) * P],
                                             tokens(act_parts[:, ap], s)[:, k], start=n == 0,
                                             stop=n == len(PASSES) * KH - 1, skip_group_check=True)
                            n += 1
                return last

            def product(bank_, pairs, s, t):
                r = rows(s)
                n = 0
                for act_parts, weight in pairs:
                    for wp, ap in PASSES:
                        for k in range(KH):
                            last = pe.matmul(halves(bank_)[0:r, t, :], act_parts[:, ap, k, t * P:t * P + r],
                                             weight[:, wp, k, :], start=n == 0,
                                             stop=n == len(pairs) * len(PASSES) * KH - 1, skip_group_check=True)
                            n += 1
                return last

            def transposes(bank_, src, s):
                r = rows(s)
                for t in range(tiles_of(s)):
                    for k in range(KH):
                        last = pe.transpose(halves(bank_)[:, k, t * P:t * P + r], src[0:r, t, k * P:(k + 1) * P],
                                            ident[0:r, 0:r])
                return last

            def stage(key, s, i, v):
                if key == "l1":
                    if i == 0:
                        c_khi.wait(pe, s, 1)
                        c_klo.wait(pe, s, 1)
                    c_g.wait(pe, s, i - 1)
                    product_T(ps_l1[i % 2], we1[:, :, i], tokT[:, v], s).then_inc(c_l1.sem, 1)
                elif key == "l2":
                    c_ghi.wait(pe, s, i + 1)
                    c_glo.wait(pe, s, i + 1)
                    c_add.wait(pe, s, i - 1)
                    for t in range(tiles_of(s)):
                        last = product(ps_l2[i % 2], [(gT[:, i % 2], we2[:, :, i])], s, t)
                    last.then_inc(c_l2.sem, 1)
                elif key == "combT":
                    c_comb.wait(pe, s, 1)
                    r = rows(s)
                    for t in range(tiles_of(s)):
                        last = pe.transpose(ps_g[2][0:NE, t * P:t * P + r], comb[0:r, v, t, :], ident[0:r, 0:r])
                    last.then_inc(c_ct.sem, 1)
                elif key == "bias2":
                    c_ctc.wait(pe, s, 1)
                    r = rows(s)
                    for t in range(tiles_of(s)):
                        last = pe.matmul(halves(ps_g[2])[0:r, t, :], combT[:, t * P:t * P + r], be2[:, :],
                                         start=True, stop=True, skip_group_check=True)
                    last.then_inc(c_b2.sem, 1)
                elif key == "trans":
                    c_xn2.wait(pe, s, 16)
                    c_khi.wait(pe, s, 0)
                    c_klo.wait(pe, s, 0)
                    transposes(ps_g[0], xn2, s).then_inc(c_tx.sem, 1)
                    c_h.wait(pe, s, tiles_of(s))
                    c_top.wait(pe, s, 0)
                    transposes(ps_g[1], h, s).then_inc(c_th.sem, 1)
                elif key == "q":
                    c_xhi.wait(pe, s, 1)
                    c_xlo.wait(pe, s, 1)
                    c_accb.wait(pe, s, 0)
                    product_T(ps_g[2], wq, xT, s).then_inc(c_q.sem, 1)
                elif key == "gin1":
                    c_hhi.wait(pe, s, 1)
                    c_hlo.wait(pe, s, 1)
                    product_T(ps_g[0], wg1, hT, s).then_inc(c_w1.sem, 1)
                elif key == "norm":
                    c_qf.wait(pe, s, 1)
                    for k in range(KH):
                        last = pe.matmul(tokens(halves(ps_g[1]), s)[:, k], ksm[:, k, :], tokens(qf, s)[:, k],
                                         start=True, stop=True, skip_group_check=True)
                    last.then_inc(c_n.sem, 1)
                elif key == "out":
                    c_rhi.wait(pe, s, 1)
                    c_rlo.wait(pe, s, 1)
                    c_qhi.wait(pe, s, 1)
                    c_qlo.wait(pe, s, 1)
                    for t in range(tiles_of(s)):
                        last = product(ps_g[2], [(rTs, wg2), (qTs, kvwo)], s, t)
                    last.then_inc(c_o.sem, 1)
                elif key == "tokT":
                    c_tok.wait(pe, s, 1)
                    c_r.wait(pe, s, 1)
                    transposes(ps_g[0], tok, s).then_inc(c_tk.sem, 1)
                elif key == "router":
                    c_khi.wait(pe, s, 1)
                    c_klo.wait(pe, s, 1)
                    c_ne.wait(pe, s, 1)
                    r = rows(s)
                    for t in range(tiles_of(s)):
                        n = 0
                        for wp, ap in PASSES:
                            for k in range(KH):
                                last = pe.matmul(ps_g[1][0:r, t * NE:(t + 1) * NE], tokT[:, v, ap, k, t * P:t * P + r],
                                                 wr[:, wp, k, :], start=n == 0, stop=n == len(PASSES) * KH - 1,
                                                 skip_group_check=True)
                                n += 1
                    last.then_inc(c_lg.sem, 1)
                elif key == "agg" and i < tiles_of(s):
                    c_h.wait(pe, s, i)
                    c_hot.wait(pe, s, i + 1)
                    pe.wait_ge(s_gath[i], s * (16 * J) + 16 * J)
                    segment_sum(i).then_inc(c_agg.sem, 1)

            main_program(pe, stage)

        @block.vector
        def _(dve):
            dve.wait_ge(s_bias, 160)
            dve.tensor_tensor(bout[:, :], bout[:, :], bout2[:, :], ALU.add).then_inc(s_bprep, 1)
            dve.wait_ge(s_bprep, 1)
            dve.memset(bout2[:, :], 0.0).then_inc(s_bprep, 1)
            dve.tensor_scalar(nbq[:, :], bq[:, :], -1.0, None, ALU.mult).then_inc(s_bprep, 1)
            dve.tensor_scalar(bq1[:, :], bq[:, :], 1.0, None, ALU.add).then_inc(s_bprep, 1)
            dve.tensor_scalar(eps1[:, :], eps1[:, :], 1.0, None, ALU.add).then_inc(s_bprep, 1)

            def rsqrt(v, y, t, inc, wait):
                inc(dve.tensor_scalar(y.bitcast(I32), v.bitcast(I32), 1, None, ALU.logical_shift_right))
                wait()
                inc(dve.tensor_scalar(y.bitcast(I32), y.bitcast(I32), -1.0, float(MAGIC), ALU.mult, ALU.add))
                for _ in range(3):
                    wait()
                    inc(dve.tensor_tensor(t, y, y, ALU.mult))
                    wait()
                    inc(dve.scalar_tensor_tensor(out=t, in0=t, scalar=-0.5, in1=v, op0=ALU.mult, op1=ALU.mult))
                    wait()
                    inc(dve.scalar_tensor_tensor(out=y, in0=t, scalar=1.5, in1=y, op0=ALU.add, op1=ALU.mult))
                wait()

            chain = [0]

            def l_inc(ins):
                ins.then_inc(s_lchain, 1)
                chain[0] += 1

            def l_wait():
                dve.wait_ge(s_lchain, chain[0])

            T = TILES

            def control_chunks():
                dve.wait_ge(s_dst, 48)
                dve.wait_ge(s_const, 9 + P // HD)
                dve.tensor_tensor(d_bad, d_next, d_cur, ALU.is_lt).then_inc(s_ctlchain, 1)
                dve.wait_ge(s_ctlchain, 1)
                dve.tensor_reduce(cs[:, 4:5], d_bad, AX_X, ALU.add).then_inc(s_ctlchain, 1)
                dve.wait_ge(s_ctlchain, 2)
                for n in range(2):
                    dve.tensor_scalar(d_bad[0:T, :], d_last, cs[0:T, n:n + 1], None, ALU.is_lt).then_inc(s_ctlchain, 1)
                    dve.wait_ge(s_ctlchain, 3 + 2 * n)
                    dve.tensor_reduce(cs[0:T, 5 + n:6 + n], d_bad[0:T, :], AX_X, ALU.add).then_inc(s_ctlchain, 1)
                    dve.wait_ge(s_ctlchain, 4 + 2 * n)
                dve.tensor_copy(row_i[0:T, :], cs[0:T, 5:7]).then_inc(s_ctlchain, 1)

            def control_edges():
                k = CTL_CHUNKS
                for n in range(2):
                    dve.wait_ge(s_row[n], 16)
                    dve.tensor_scalar(d_bad[0:T, 0:P], d_row[:, n, :], cs[0:T, n:n + 1], None, ALU.is_lt).then_inc(s_ctlchain, 1)
                    dve.wait_ge(s_ctlchain, k + 1)
                    dve.tensor_reduce(cs[0:T, 7 + n:8 + n], d_bad[0:T, 0:P], AX_X, ALU.add).then_inc(s_ctlchain, 1)
                    dve.wait_ge(s_ctlchain, k + 2)
                    k += 2
                dve.scalar_tensor_tensor(out=cs[0:T, 9:11], in0=cs[0:T, 5:7], scalar=float(P), in1=cs[0:T, 7:9],
                                         op0=ALU.mult, op1=ALU.add).then_inc(s_ctlchain, 1)
                dve.wait_ge(s_viol, 1)
                dve.tensor_scalar(cs[0:T, 11:12], ps_g[2][0:T, 0:1], 0.5, None, ALU.is_lt).then_inc(s_ctlchain, 1)
                dve.wait_ge(s_ctlchain, k + 2)
                dve.tensor_tensor(cs[0:T, 12:13], cs[0:T, 10:11], cs[0:T, 9:10], ALU.subtract).then_inc(s_ctlchain, 1)
                dve.tensor_tensor(ctl_i[0:T, 0:1], cs[0:T, 9:10], cs[0:T, 11:12], ALU.mult).then_inc(s_ctlchain, 1)
                dve.wait_ge(s_ctlchain, k + 4)
                dve.tensor_scalar(d_bad[0:T, 0:MAX_EXTRA], seg_ends, cs[0:T, 12:13], None, ALU.is_lt).then_inc(s_ctlchain, 1)
                dve.wait_ge(s_ctlchain, k + 5)
                dve.tensor_reduce(cs[0:T, 13:14], d_bad[0:T, 0:MAX_EXTRA], AX_X, ALU.add).then_inc(s_ctlchain, 1)
                dve.wait_ge(s_ctlchain, k + 6)
                dve.scalar_tensor_tensor(out=cs[0:T, 14:15], in0=cs[0:T, 13:14], scalar=float(-MAX_EXTRA), in1=cs[0:T, 11:12],
                                         op0=ALU.add, op1=ALU.mult).then_inc(s_ctlchain, 1)
                dve.wait_ge(s_ctlchain, k + 7)
                dve.tensor_scalar(ctl_i[0:T, 1:2], cs[0:T, 14:15], float(MAX_EXTRA), None, ALU.add).then_inc(s_ctlchain, 1)
                assert k + 8 == CTL_CHAIN

            def control_most():
                dve.wait_ge(s_ctl, 16)
                dve.tensor_reduce(most[0:1, 0:1], control[0:1, :, 1], AX_X, ALU.max).then_inc(s_most, 1)

            for b in range(LBATCHES + 1):
                nt = LB if b < LBATCHES else 1
                r = P if b < LBATCHES else LAST_ROWS
                dve.wait_ge(s_lx[b % 2], 16 * (b // 2 + 1))
                for t in range(nt):
                    l_inc(dve.bn_stats(lstat[0:r, t, :], lx[0:r, b % 2, t, :]))
                l_wait()
                for t in range(nt):
                    l_inc(dve.bn_aggr(lmv[0:r, t, :], lstat[0:r, t, :]))
                l_wait()
                l_inc(dve.tensor_scalar(lv[0:r, 0:nt], lmv[0:r, 0:nt, 1], LN_EPS, None, ALU.add))
                l_wait()
                rsqrt(lv[0:r, 0:nt], ly[0:r, 0:nt], lt[0:r, 0:nt], l_inc, l_wait)
                if b >= 2:
                    dve.wait_ge(s_lxn, b - 1)
                l_inc(dve.tensor_copy(lrs[0:r, b % 2, 0:nt], ly[0:r, 0:nt]))
                dve.scalar_tensor_tensor(out=lnm[0:r, b % 2, 0:nt], in0=lmv[0:r, 0:nt, 0], scalar=-1.0, in1=ly[0:r, 0:nt],
                                         op0=ALU.mult, op1=ALU.mult).then_inc(s_lrs, 1)
                if b == 0:
                    control_chunks()
                elif b == 2:
                    control_edges()
                elif b == 6:
                    control_most()
                dve.wait_ge(s_lhi, b + 1)
                dve.scalar_tensor_tensor(out=ltab[0:r, b % 2, 0:nt, 1, :], in0=lxn[0:r, b % 2, 0:nt, :],
                                         scalar=TABLE_SCALE, in1=ltab[0:r, b % 2, 0:nt, 0, :],
                                         op0=ALU.mult, op1=ALU.subtract).then_inc(s_llo, 1)
            dve.wait_ge(s_wrs, 1)
            dve.tensor_tensor(wr[:, 1], wr_f[:, :, :], wr[:, 0].bitcast(F32), ALU.subtract).then_inc(s_wrs, 1)

            def relative(u, tile):
                return dve.tensor_scalar(dst_rel[:, u, :], dst_stage[:, u, :],
                                         tile_base[:, tile:tile + 1] if isinstance(tile, int) else tile_base[:, bass.ds(tile, 1)],
                                         None, ALU.subtract)

            def onehots(u):
                return dve.tensor_tensor(onehot[:, u], iota_h[:, :].rearrange("p (o c) -> p o c", o=1).broadcast_to([P, J, P]),
                                         dst_rel[:, u, :].rearrange("p (c o) -> p c o", o=1).broadcast_to([P, J, P]), ALU.is_equal)

            def add_sum(to, base, part, r):
                return dve.scalar_tensor_tensor(out=to, in0=ps_agg[0:r, part * D:(part + 1) * D], scalar=1.0 / TABLE_SCALE,
                                                in1=base, op0=ALU.mult, op1=ALU.add)

            extra = dve.value_load(most[0:1, 0:1], min_val=0, max_val=MAX_EXTRA)
            with dve.If(extra > 0):
                with dve.Fori(0, extra):
                    with dve.Fori(0, TILES) as tile:
                        dve.wait_ge(s_xdst, 16)
                        dve.sem_clear(s_xdst)
                        relative(0, tile).then_inc(s_xchain, 1)
                        dve.wait_ge(s_xchain, 1)
                        onehots(0).then_inc(s_xhot, 1)
                        dve.wait_ge(s_xsum, 1)
                        dve.sem_clear(s_xsum)
                        dve.wait_ge(s_xbase, 16)
                        dve.sem_clear(s_xbase)
                        add_sum(xe[:, 0, :], xe[:, 0, :], 0, P).then_inc(s_xchain, 1)
                        dve.wait_ge(s_xchain, 2)
                        dve.sem_clear(s_xchain)
                        add_sum(xe[:, 0, :], xe[:, 0, :], 1, P).then_inc(s_xadd, 1)

            def split_mix(j, u):
                r = rows_of(j)
                dve.wait_ge(s_mhi, j + 1)
                dve.tensor_tensor(mxT[:, u, 1, :, 0:r], halves(ps_mt[u])[:, :, 0:r], mxT[:, u, 0, :, 0:r].bitcast(F32),
                                  ALU.subtract).then_inc(s_mlo, 1)

            def mix_tile(j, u):
                r = rows_of(j)
                if not beyond(j + 1):
                    split_mix(j + 1, 1 - u)
                dve.wait_ge(s_kvp, j + 1)
                wait_tile(dve, s_kva, j - 1)
                dve.tensor_tensor(kb[0:r, u, :], ps_kvp[u][0:r, 0:D], bkv[0:r, 0, :], ALU.add).then_inc(s_kb, 1)
                dve.tensor_tensor(vf[0:r, u, :, 0:P], halves(ps_kvp[u])[0:r, 1, :].rearrange("p (k c) -> p k c", k=KH),
                                  bkv[0:r, 1, :].rearrange("p (k c) -> p k c", k=KH), ALU.add).then_inc(s_kb, 1)
                dve.wait_ge(s_ke, j + 1)
                dve.scalar_tensor_tensor(out=kf[0:r, u, :], in0=kb[0:r, u, :], scalar=0.0, in1=kr[0:r, u, :],
                                         op0=ALU.max, op1=ALU.add).then_inc(s_kf, 1)

            split_mix(0, 0)
            mix_program(dve, mix_tile)
            dve.wait_ge(s_kva, TILES)
            for k in range(KH):
                dve.tensor_tensor(kvm[:, k, :], ps_kva[k][:, 0:P], headmask[:, :], ALU.mult)
                last = dve.tensor_copy(ksum[:, k:k + 1], ps_kva[k][:, P:P + 1])
            last.then_inc(s_kvx, 1)
            dve.wait_ge(s_kvx, 1)
            for k in range(KH):
                dve.tensor_scalar(ksm[:, k, :], headmask[:, :], ksum[:, k:k + 1], None, ALU.mult).then_inc(s_kvx, 1)
            dve.wait_ge(s_kvy, 1)
            dve.tensor_copy(kvmT[:, :, :], ps_g[0][:, 0:KH * P].rearrange("p (k c) -> p k c", k=KH)).then_inc(s_kvx, 1)
            dve.wait_ge(s_kvz, 1)
            dve.tensor_tensor(kvwo[:, 1, :, :], halves(ps_g[1]), kvwo[:, 0, :, :].bitcast(F32), ALU.subtract).then_inc(s_kvx, 1)

            gchain = Chain(s_gchain, G_CHAIN)

            def gate():
                dve.sem_inc(s_gate, 1)

            def lo_part(parts_, whole, s):
                return dve.tensor_tensor(tokens(parts_[:, 1], s), tokens(whole, s), tokens(parts_[:, 0], s).bitcast(F32), ALU.subtract)

            def stage(key, s, i, v):
                r, nt = rows(s), tiles_of(s)
                if key == "hot" and i < nt:
                    tile = s * SUPER + i
                    dve.wait_ge(s_dstl[i], s * 16 + 16)
                    relative(i, tile).then_inc(c_rel.sem, 1)
                    c_rel.wait(dve, s, i + 1)
                    c_agg.wait(dve, s, i - 1)
                    onehots(i).then_inc(c_hot.sem, 1)
                elif key == "agg" and i < nt:
                    c_xe.wait(dve, s, 1)
                    if i == 0:
                        gate()
                        with dve.If(extra > 0):
                            c_rest.wait(dve, s, 16)
                            dve.tensor_tensor(cut(xe, s), cut(xe, s), cut(h, s), ALU.add).then_inc(c_xr.sem, 1)
                            c_xr.wait(dve, s, 1)
                            gate()
                    c_th.wait(dve, s, 0)
                    c_agg.wait(dve, s, i + 1)
                    add_sum(h[0:r, i, :], xe[0:r, i, :], 0, r).then_inc(c_hp.sem, 1)
                    c_hp.wait(dve, s, i + 1)
                    add_sum(h[0:r, i, :], h[0:r, i, :], 1, r).then_inc(c_h.sem, 1)
                elif key == "l1":
                    c_ghi.wait(dve, s, i + 1)
                    lo_part(gT[:, i % 2], gact[:, i % 2], s).then_inc(c_glo.sem, 1)
                elif key == "l2":
                    c_l2.wait(dve, s, i + 1)
                    c_accb.wait(dve, s, 1) if i == 0 else c_add.wait(dve, s, i)
                    for t in range(nt):
                        last = dve.scalar_tensor_tensor(out=acc[0:r, v, t, :], in0=halves(ps_l2[i % 2])[0:r, t, :],
                                                        scalar=comb[0:r, v, t, i:i + 1], in1=acc[0:r, v, t, :],
                                                        op0=ALU.mult, op1=ALU.add)
                    last.then_inc(c_add.sem, 1)
                elif key == "bias2":
                    c_b2.wait(dve, s, 1)
                    c_acc.wait(dve, s, 1)
                    dve.tensor_tensor(cut(acc[:, v], s), cut(halves(ps_g[2]), s), cut(acc[:, v], s), ALU.add).then_inc(c_accb.sem, 1)
                elif key == "trans":
                    c_xhi.wait(dve, s, 1)
                    lo_part(xT, halves(ps_g[0]), s).then_inc(c_xlo.sem, 1)
                    c_hhi.wait(dve, s, 1)
                    lo_part(hT, halves(ps_g[1]), s).then_inc(c_hlo.sem, 1)
                elif key == "q":
                    c_qexp.wait(dve, s, 1)
                    for half in range(KH):
                        last = dve.scalar_tensor_tensor(out=tokens(qf, s)[:, half], in0=tokens(halves(ps_g[2]), s)[:, half],
                                                        scalar=bq1[:, half:half + 1], in1=tokens(ex, s)[:, half],
                                                        op0=ALU.add, op1=ALU.max)
                    last.then_inc(c_qf.sem, 1)
                elif key == "gin1":
                    c_rhi.wait(dve, s, 1)
                    lo_part(rTs, rT, s).then_inc(c_rlo.sem, 1)
                elif key == "norm":
                    c_ne.wait(dve, s, 1)
                    dve.reciprocal(tokens(nrm, s), tokens(nrm, s)).then_inc(c_nr.sem, 1)
                    c_nr.wait(dve, s, 1)
                    c_qhi.wait(dve, s, 0)
                    dve.tensor_tensor(tokens(qs, s), tokens(qf, s), tokens(nrm, s), ALU.mult).then_inc(c_qs.sem, 1)
                    c_qhi.wait(dve, s, 1)
                    lo_part(qTs, qs, s).then_inc(c_qlo.sem, 1)
                elif key == "out":
                    gchain.begin(s)
                    inc, wait = gchain.inc, lambda: gchain.wait(dve)
                    c_xs.wait(dve, s, 16)
                    dve.tensor_tensor(cut(xs, s), cut(xs, s), bout[0:r, :].rearrange("p (o c) -> p o c", o=1).broadcast_to([r, nt, D]),
                                      ALU.add).then_inc(c_xb.sem, 1)
                    c_xb.wait(dve, s, 1)
                    c_o.wait(dve, s, 1)
                    c_out.wait(dve, s, -16)
                    dve.tensor_tensor(cut(acc[:, v], s), cut(halves(ps_g[2]), s), cut(xs, s), ALU.add).then_inc(c_x1.sem, 1)
                    c_x1.wait(dve, s, 1)
                    for t in range(nt):
                        inc(dve.bn_stats(gstat[0:r, t, :], acc[0:r, v, t, :]))
                    wait()
                    gate()
                    for t in range(nt):
                        inc(dve.bn_aggr(gmv[0:r, t, :], gstat[0:r, t, :]))
                    wait()
                    inc(dve.tensor_scalar(gv[0:r, 0:nt], gmv[0:r, 0:nt, 1], LN_EPS, None, ALU.add))
                    wait()
                    c_tok.wait(dve, s, 0)
                    rsqrt(gv[0:r, 0:nt], gy[0:r, 0:nt], gt[0:r, 0:nt], inc, wait)
                    dve.scalar_tensor_tensor(out=gnm[0:r, 0:nt], in0=gmv[0:r, 0:nt, 0], scalar=-1.0, in1=gy[0:r, 0:nt],
                                             op0=ALU.mult, op1=ALU.mult).then_inc(c_ln.sem, 1)
                elif key == "tokT":
                    c_tok.wait(dve, s, 1)
                    dve.tensor_tensor(cut(acc[:, v], s), cut(acc[:, v], s), cut(tok, s), ALU.add).then_inc(c_acc.sem, 1)
                    c_khi.wait(dve, s, 1)
                    lo_part(tokT[:, v], halves(ps_g[0]), s).then_inc(c_klo.sem, 1)
                elif key == "router":
                    inc, wait = gchain.inc, lambda: gchain.wait(dve)
                    c_lg.wait(dve, s, 1)
                    gate()
                    for t in range(nt):
                        inc(dve.max(top[0:r, t, :], ps_g[1][0:r, t * NE:(t + 1) * NE]))
                    wait()
                    gate()
                    for t in range(nt):
                        inc(dve.max_index(topi[0:r, t, :], top[0:r, t, :], ps_g[1][0:r, t * NE:(t + 1) * NE]))
                    dve.tensor_scalar(ntop[0:r, 0:nt], top[0:r, 0:nt, 0], -1.0, None, ALU.mult).then_inc(c_top.sem, 1)
                    wait()
                    inc(dve.tensor_copy(topf[0:r, 0:nt, :], topi[0:r, 0:nt, 0:2]))
                    c_et.wait(dve, s, 1)
                    inc(dve.reciprocal(erec[0:r, 0:nt], esum[0:r, 0:nt]))
                    wait()

                    def over(ap, n):
                        return ap[0:r, 0:nt].rearrange("p (t o) -> p t o", o=1).broadcast_to([r, nt, n])

                    inc(dve.tensor_tensor(prob[0:r, 0:nt, :], etop[0:r, 0:nt, 0:2], over(erec, 2), ALU.mult))
                    wait()
                    inc(dve.tensor_tensor(pden[0:r, 0:nt], prob[0:r, 0:nt, 0], prob[0:r, 0:nt, 1], ALU.add))
                    wait()
                    inc(dve.tensor_scalar(pden[0:r, 0:nt], pden[0:r, 0:nt], 1e-12, None, ALU.max))
                    wait()
                    inc(dve.reciprocal(prec[0:r, 0:nt], pden[0:r, 0:nt]))
                    wait()
                    inc(dve.tensor_tensor(wtop[0:r, 0:nt, :], prob[0:r, 0:nt, :], over(prec, 2), ALU.mult))
                    for n, pick in enumerate((pick0, pick1)):
                        inc(dve.tensor_tensor(pick[0:r, 0:nt, :], iota8[0:r, :].rearrange("p (o c) -> p o c", o=1).broadcast_to([r, nt, NE]),
                                              topf[0:r, 0:nt, n:n + 1].broadcast_to([r, nt, NE]), ALU.is_equal))
                    wait()
                    for n, pick in enumerate((pick0, pick1)):
                        inc(dve.tensor_tensor(pick[0:r, 0:nt, :], pick[0:r, 0:nt, :],
                                              wtop[0:r, 0:nt, n:n + 1].broadcast_to([r, nt, NE]), ALU.mult))
                    wait()
                    c_ct.wait(dve, s, -1)
                    dve.tensor_tensor(comb[0:r, v, 0:nt, :], pick0[0:r, 0:nt, :], pick1[0:r, 0:nt, :], ALU.add).then_inc(c_comb.sem, 1)
                    assert nt < SUPER or gchain.k == G_CHAIN, gchain.k

            main_program(dve, stage)


def kernel(x, src, dst, edge_attr_16, L0_gnn_W1, L0_gnn_b1, L0_gnn_W2, L0_gnn_b2, L0_gnn_eps, L0_mix_wq, L0_mix_bq,
           L0_mix_wk, L0_mix_bk, L0_mix_wv, L0_mix_bv, L0_mix_wo, L0_mix_bo, L0_ffn_router_w, L0_ffn_w1, L0_ffn_b1,
           L0_ffn_w2, L0_ffn_b2):
    import numpy as np
    import concourse.bacc as bacc
    from concourse.bass_utils import run_bass_kernel_spmd

    def columns(v):
        return np.ascontiguousarray(np.asarray(v).reshape(-1, KH, P).transpose(2, 0, 1))

    src_p = np.zeros(EDGES, np.int32)
    src_p[:E] = np.asarray(src)
    dst_p = np.full(EDGES, NO_NODE, np.int32)
    dst_p[:E] = np.asarray(dst)
    arrays = {
        "x": np.asarray(x), "src": src_p, "dst": dst_p,
        "last_dst": np.ascontiguousarray(dst_p[:CHUNKS * P].reshape(CHUNKS, P)[:, P - 1].reshape(1, CHUNKS)),
        "wq": np.asarray(L0_mix_wq), "wk": np.asarray(L0_mix_wk), "wv": np.asarray(L0_mix_wv), "wo": np.asarray(L0_mix_wo),
        "wg1": np.asarray(L0_gnn_W1), "wg2": np.asarray(L0_gnn_W2), "we1": np.asarray(L0_ffn_w1), "we2": np.asarray(L0_ffn_w2),
        "bk": np.asarray(L0_mix_bk).reshape(1, D), "bv": np.asarray(L0_mix_bv).reshape(1, D),
        "bo": np.asarray(L0_mix_bo).reshape(1, D), "bg2": np.asarray(L0_gnn_b2).reshape(1, D),
        "eps": np.asarray(L0_gnn_eps).reshape(1, 1), "be2": np.asarray(L0_ffn_b2),
        "bq": columns(L0_mix_bq).reshape(P, KH), "bg1": columns(L0_gnn_b1).reshape(P, KH), "be1": columns(L0_ffn_b1),
        "wr": np.ascontiguousarray(np.asarray(L0_ffn_router_w).reshape(NE, KH, P).transpose(2, 1, 0)),
    }
    nc = bacc.Bacc("TRN2", target_bir_lowering=False, num_devices=1)
    aps = {k: nc.dram_tensor(f"in_{k}", list(a.shape), mybir.dt.from_np(a.dtype), kind="ExternalInput").ap()
           for k, a in arrays.items()}
    out = nc.dram_tensor("out", [N, D], F32, kind="ExternalOutput").ap()
    gps_layer(nc, aps["x"], aps["src"], aps["dst"], aps, out)
    r = run_bass_kernel_spmd(nc, [{f"in_{k}": a for k, a in arrays.items()}], core_ids=[0])
    return r.results[0]["out"]
```

```python
from contextlib import ExitStack

import concourse.bass as bass
from concourse import mybir

F32 = mybir.dt.float32
F32R = mybir.dt.float32r
F16 = mybir.dt.float16
I32 = mybir.dt.int32
U32 = mybir.dt.uint32
ALU = mybir.AluOpType
ACT = mybir.ActivationFunctionType
AX_X = mybir.AxisListType.X

P = 128
D = 256
KH = D // P
N = 6250
NE = 8
HD = 32
TILES = -(-N // P)
LAST_ROWS = N - (TILES - 1) * P
SUPER = 2
STEPS = -(-TILES // SUPER)
E = 106250
J = 18
CUTS = 3
JC = J // CUTS
SEG = J * P
MAX_EXTRA = -(-E // SEG) - 1
CHUNKS = -(-E // (P * 32)) * 32
EDGES = CHUNKS * P + (MAX_EXTRA + 1) * SEG
NO_NODE = TILES * P
TABLE_SCALE = 2048.0
LN_EPS = 1e-5
NORM_EPS = 1e-6
LB = 8
LBATCHES = (TILES - 1) // LB
MAGIC = 0x5F3759DF
G_CHAIN = 32
CTL_CHUNKS = 7
CTL_CHAIN = CTL_CHUNKS + 12
PASSES = ((0, 0), (0, 1), (1, 0))


class Count:

    def __init__(self, sem, per):
        self.sem, self.per = sem, per

    def wait(self, eng, step, k):
        value = step * self.per + k
        if isinstance(value, int) and value <= 0:
            return
        eng.wait_ge(self.sem, value)


class Chain:

    def __init__(self, sem, per):
        self.sem, self.per, self.step, self.k = sem, per, 0, 0

    def begin(self, step):
        self.step, self.k = step, 0

    def inc(self, ins):
        ins.then_inc(self.sem, 1)
        self.k += 1

    def wait(self, eng):
        eng.wait_ge(self.sem, self.step * self.per + self.k)


def rows_of(tile):
    return LAST_ROWS if isinstance(tile, int) and tile == TILES - 1 else P


def tiles_of(step):
    return TILES - SUPER * step if isinstance(step, int) and step == STEPS - 1 else SUPER


def gps_layer(nc, x_d, src_d, dst_d, w, out_d):
    with ExitStack() as ctx:
        def sb(name, shape, dt=F32):
            return ctx.enter_context(nc.sbuf_tensor(name, shape, dt))

        def sem(name):
            return ctx.enter_context(nc.semaphore(name))

        xn_d = nc.dram_tensor("xn_scratch", [N, D], F32).ap()
        table_d = nc.dram_tensor("table_scratch", [N, 2 * D], F16).ap()
        ctl_d = nc.dram_tensor("control_scratch", [TILES, 2], I32).ap()
        rest_d = nc.dram_tensor("rest_scratch", [TILES * P, D], F32).ap()

        wkv = sb("wkv", [P, 2, KH, 2 * D], F32R)
        wq = sb("wq", [P, 2, KH, D], F32R)
        wg1 = sb("wg1", [P, 2, KH, D], F32R)
        wg2 = sb("wg2", [P, 2, KH, D], F32R)
        kvwo = sb("kvwo", [P, 2, KH, D], F32R)
        we1 = sb("we1", [P, 2, NE, KH, D], F32R)
        we2 = sb("we2", [P, 2, NE, KH, D], F32R)
        wr = sb("wr", [P, 2, KH, NE], F32R)
        wo = sb("wo", [P, KH, D])
        stage_w = sb("stage_w", [P, 2, 2 * KH, D])
        bkv = sb("bkv", [P, 2, D])
        bout = sb("bout", [P, D])
        bout2 = sb("bout2", [P, D])
        bq = sb("bq", [P, KH])
        nbq = sb("nbq", [P, KH])
        bq1 = sb("bq1", [P, KH])
        bg1 = sb("bg1", [P, KH])
        be1 = sb("be1", [P, NE, KH])
        be2 = sb("be2", [NE, D])
        eps1 = sb("eps1", [P, 1])
        own_scale = sb("own_scale", [P, 1])

        ring = sb("ring", [P, 2, J, 2 * D], F16)
        onehot = sb("onehot", [P, 2, J, P], F16)
        idx_stage = sb("idx_stage", [P, 2, J], I32)
        dst_stage = sb("dst_stage", [P, 2, J], I32)
        dst_rel = sb("dst_rel", [P, 2, J], F16)
        tile_base = sb("tile_base", [P, TILES])
        iota_h = sb("iota_h", [P, P], F16)
        iota8 = sb("iota8", [P, NE])
        ident = sb("ident", [P, P])
        headmask = sb("headmask", [P, P])
        ones = sb("ones", [P, P])
        control = sb("control", [1, TILES, 2], I32)
        most = sb("most", [1, 1], I32)

        area = sb("area", [P, 7168])
        lx = area[:, 0:4096].rearrange("p (b t c) -> p b t c", b=2, t=LB)
        tokT = sb("tokT", [P, 2, 2, KH, 2 * P], F32R)
        lxn = [v.rearrange("p (t c) -> p t c", t=LB) for v in
               (area[:, 4096:6144], onehot[:, :, :, :].rearrange("p u j c -> p (u j c)")[:, 0:2 * LB * D].bitcast(F32))]

        def two(n, k=512):
            return area[:, n:n + k]

        def view(n):
            return two(n).rearrange("p (t c) -> p t c", t=2)

        rT, ex, qf, tok, qs = view(0), view(512), view(1024), view(1536), view(2048)
        h = [view(2560), view(3072)]
        xa, xn2, xs = view(3584), view(4096), view(4608)
        acc = two(5120, 1024).rearrange("p (u t c) -> p u t c", u=2, t=2)
        gact = two(6144, 1024).rearrange("p (u t c) -> p u t c", u=2, t=2)
        mxn = two(512).rearrange("p (u c) -> p u c", u=2)
        kb = two(0).rearrange("p (u c) -> p u c", u=2)
        kr = two(1024).rearrange("p (u c) -> p u c", u=2)
        kf = two(1536).rearrange("p (u c) -> p u c", u=2)
        kvm = two(2048, KH * P).rearrange("p (k c) -> p k c", k=KH)
        kvmT = two(2304, KH * P).rearrange("p (k c) -> p k c", k=KH)
        vf = two(6144, 2 * KH * (P + 2)).rearrange("p (u k c) -> p u k c", u=2, k=KH)
        ring32 = ring[:, :, :, :].rearrange("p u s c -> p (u s c)").bitcast(F32)
        d_cur = ring32[:, 0:CHUNKS].bitcast(I32)
        d_next = ring32[:, CHUNKS:2 * CHUNKS].bitcast(I32)
        d_bad = ring32[:, 2 * CHUNKS:3 * CHUNKS]
        d_last = ring32[0:TILES, 3 * CHUNKS:4 * CHUNKS].bitcast(I32)
        d_row = ring32[0:TILES, 4 * CHUNKS:4 * CHUNKS + 2 * P].bitcast(I32).rearrange("p (n c) -> p n c", n=2)
        seg_ends = ring32[0:TILES, 4 * CHUNKS + 2 * P:4 * CHUNKS + 2 * P + MAX_EXTRA]
        ltab0 = 4 * CHUNKS + 2 * P + 64
        ltab = ring32[:, ltab0:ltab0 + 2 * LB * D].bitcast(F16).rearrange("p (b t h c) -> p b t h c", b=2, t=LB, h=2)

        lstat = sb("lstat", [P, LB, 6])
        lmv = sb("lmv", [P, LB, 2])
        lv = sb("lv", [P, LB])
        ly = sb("ly", [P, LB])
        lt = sb("lt", [P, LB])
        lrs = sb("lrs", [P, 2, LB])
        lnm = sb("lnm", [P, 2, LB])
        cs = sb("cs", [P, 16])
        ctl_i = sb("ctl_i", [P, 2], I32)
        row_i = sb("row_i", [P, 2], I32)

        ksm = sb("ksm", [P, KH, P // HD])
        ksum = sb("ksum", [P, KH])

        xT = sb("xT", [P, 2, KH, 2 * P], F32R)
        mxT = xT[:, :, :, :].rearrange("p a k c -> p (a k c)").rearrange("p (u a k c) -> p u a k c", u=2, a=2, k=KH)
        hT = sb("hT", [P, 2, KH, 2 * P], F32R)
        rTs = sb("rTs", [P, 2, KH, 2 * P], F32R)
        qTs = sb("qTs", [P, 2, KH, 2 * P], F32R)
        gT = wkv[:, :, :, :].rearrange("p a k c -> p (a k c)").rearrange("p (u a k c) -> p u a k c", u=2, a=2, k=KH)
        gstat = sb("gstat", [P, SUPER, 6])
        gmv = sb("gmv", [P, SUPER, 2])
        gv = sb("gv", [P, SUPER])
        gvh = sb("gvh", [P, SUPER])
        gy = sb("gy", [P, SUPER])
        gt = sb("gt", [P, SUPER])
        gnm = sb("gnm", [P, SUPER])
        top = sb("top", [P, SUPER, 8])
        topi = sb("topi", [P, SUPER, 8], U32)
        topf = sb("topf", [P, SUPER, 2])
        ntop = sb("ntop", [P, SUPER])
        etop = sb("etop", [P, SUPER, 8])
        esum = sb("esum", [P, SUPER])
        erec = sb("erec", [P, SUPER])
        prob = sb("prob", [P, SUPER, 2])
        pden = sb("pden", [P, SUPER])
        prec = sb("prec", [P, SUPER])
        wtop = sb("wtop", [P, SUPER, 2])
        pick0 = sb("pick0", [P, SUPER, NE])
        pick1 = sb("pick1", [P, SUPER, NE])
        wr_f = sb("wr_f", [P, KH, NE])
        n8 = sb("n8", [P, SUPER, KH, P // HD])
        rn8 = sb("rn8", [P, SUPER, KH, P // HD])
        comb = sb("comb", [P, 2, SUPER, NE])
        combT = sb("combT", [NE, 2 * P])

        bank = [ctx.enter_context(nc.psum_tensor(f"bank{i}", [P, 512], F32)) for i in range(8)]
        ps_l1, ps_l2, ps_agg, ps_g = bank[0:2], bank[2:4], bank[4], bank[5:8]
        ps_out = (bank[7], bank[5])
        ps_kvp, ps_kva, ps_mt = bank[0:2], bank[2:4], bank[5:7]

        s_bias, s_wload, s_wo = sem("bias_loaded"), [sem("weights_loaded0"), sem("weights_loaded1")], sem("wo_loaded")
        s_whi, s_wlo, s_wlo2 = sem("weight_hi"), sem("weight_lo"), sem("weight_lo_late")
        s_const, s_bprep = sem("constants"), sem("biases_prepared")
        s_dst, s_ctlchain, s_viol = sem("dst_loaded"), sem("control_chain"), sem("violations_summed")
        s_ctlo, s_ctl, s_most = sem("control_stored"), sem("control_loaded"), sem("control_complete")
        s_row = [sem("chunk_rows0"), sem("chunk_rows1")]
        s_lx = [[sem(f"ln_x_loaded{b}_{half}") for half in range(2)] for b in range(2)]
        s_lchain, s_lxn, s_lhi, s_llo = sem("ln_chain"), sem("ln_xn"), sem("ln_table_hi"), sem("ln_table_lo")
        s_lrs = sem("ln_scales")
        s_lout = [sem("ln_stored0"), sem("ln_stored1")]
        s_mxn = [sem("mix_xn_loaded0"), sem("mix_xn_loaded1")]
        s_mt, s_mhi, s_mlo = sem("mix_transposed"), sem("mix_hi"), sem("mix_lo")
        s_kvp, s_kb, s_kr, s_ke = sem("kv_projected"), sem("kv_biased"), sem("k_negative_part"), sem("k_exp")
        s_kf, s_kva, s_kv1 = sem("k_features"), sem("kv_accumulated"), sem("v_ones")
        s_kvx, s_kvy = sem("kvwo_vector"), sem("kvwo_tensor")
        s_kvz = sem("kvwo_scalar")
        s_idx = [sem("indices_loaded0"), sem("indices_loaded1")]
        s_dstl = [sem("segment_dst_loaded0"), sem("segment_dst_loaded1")]
        s_gath = [sem("rows_gathered0"), sem("rows_gathered1")]
        s_grant = sem("gather_granted")
        s_table = sem("table_complete")
        s_xidx, s_xdst, s_xbase = sem("rest_indices"), sem("rest_dst"), sem("rest_loaded")
        s_xhot, s_xsum, s_xadd, s_xout = sem("rest_onehot"), sem("rest_summed"), sem("rest_added"), sem("rest_stored")
        s_xchain, s_rest = sem("rest_chain"), sem("rest_complete")
        s_xgath = [sem(f"rest_gathered{j}") for j in range(J)]
        s_wrs = sem("router_weights_split")
        s_gate = sem("gate_passed")

        def count(name, per):
            return Count(sem(name), per)

        c_rel, c_hot = count("dst_relative", 2), count("onehot_ready", 2 * CUTS)
        c_rest, c_xr = count("rest_reloaded", 16), count("rest_joined", 1)
        c_xs, c_xn2 = count("x_loaded", 16), count("xn_loaded", 16)
        c_xa, c_agg, c_h = count("own_xn_loaded", 16), count("segment_summed", 2), count("h_ready", 2)
        c_hp = count("h_first_part", 2)
        c_tx, c_th = count("xT_in_psum", 1), count("hT_in_psum", 1)
        c_xhi, c_xlo = count("xT_hi", 1), count("xT_lo", 1)
        c_hhi, c_hlo = count("hT_hi", 1), count("hT_lo", 1)
        c_q, c_qneg, c_qexp, c_qf = count("q_product", 1), count("q_negative", 1), count("q_exp", 1), count("q_features", 1)
        c_w1, c_r, c_rhi, c_rlo = count("gin1_product", 1), count("gin1_relu", 1), count("gin1_hi", 1), count("gin1_lo", 1)
        c_nx, c_nt = count("reciprocals_spread", 1), count("reciprocals_transposed", 1)
        c_n, c_ne, c_nr, c_qs = count("norm_product", 1), count("norm_eps", 1), count("norm_reciprocal", 1), count("q_normed", 1)
        c_qhi, c_qlo = count("q_hi", 1), count("q_lo", 1)
        c_o, c_xb, c_x1 = count("layer_product", SUPER), count("x_plus_bias", 1), count("residual1", SUPER)
        c_ln, c_tok, c_acc = count("ln2_scales", 1), count("tokens_normed", SUPER), count("acc_started", 1)
        c_tk, c_khi, c_klo = count("tokT_in_psum", 1), count("tokT_hi", 1), count("tokT_lo", 1)
        c_lg, c_top, c_et, c_comb = count("logits", 1), count("top_logits", 1), count("top_exp", 1), count("combine_weights", 1)
        c_out = count("out_stored", 16)
        c_ct, c_ctc, c_b2, c_accb = count("combT_in_psum", 1), count("combT_copied", 1), count("bias2_product", 1), count("acc_with_bias", 1)
        c_l1, c_g, c_ghi, c_glo = count("expert_l1", NE), count("gelu", NE), count("gelu_hi", NE), count("gelu_lo", NE)
        c_l2, c_add = count("expert_l2", NE), count("expert_added", NE)
        s_gchain = sem("ln2_router_chain")

        def rows(s):
            return P if tiles_of(s) == SUPER else LAST_ROWS

        def super_rows(dram, s):
            if tiles_of(s) == 1:
                return dram[s * SUPER * P:N, :]
            return dram[bass.ds(s * (SUPER * P), SUPER * P), :].rearrange("(t p) c -> p t c", p=P)

        def super_buf(buf, s):
            return buf[0:LAST_ROWS, 0, :] if tiles_of(s) == 1 else buf

        def cut(buf, s):
            return buf[0:rows(s), 0:tiles_of(s)]

        def tokens(buf, s):
            return buf[:, :, 0:(SUPER * P if tiles_of(s) == SUPER else LAST_ROWS)]

        def halves(b):
            return b[:, :].rearrange("p (t c) -> p t c", t=2)

        ORDER = ["trans", "split", "l1 0", "gelu 0", "hot 0 0", "combT", "combcopy", "q", "loadxn", "qexp", "l1 1",
                 "gelu 1", "bias2", "store", "accbias", "gin1", "l2 0", "norm", "relu", "recip", "l1 2", "add 0",
                 "gelu 2", "hot 0 1", "l1 3", "gelu 3", "l2 1", "spread", "l1 4", "add 1", "norm2", "qsplit",
                 "gelu 4", "l2 2", "add 2", "hot 0 2", "agg 0 0", "loadxa", "out", "ln2", "agg 0 1", "l2 3", "add 3",
                 "hot 1 0", "agg 0 2", "l2 4", "h 0", "tok", "l1 5", "tokT", "gelu 5", "toksplit", "add 4", "l1 6",
                 "hot 1 1", "hot 1 2", "gelu 6", "agg 1 0", "router", "weigh", "l2 5", "l1 7", "add 5", "agg 1 1",
                 "l2 6", "agg 1 2", "gelu 7", "add 6", "h 1", "l2 7", "add 7"]
        STAGE = {"a": ("loadxa", "hot", "agg", "h"), "p": ("loadxn",),
                 "g": ("trans", "split", "q", "qexp", "gin1", "relu", "norm", "recip", "spread", "norm2", "qsplit",
                       "out", "ln2", "tok", "tokT", "toksplit", "router", "weigh"),
                 "m": ("combT", "combcopy", "bias2", "accbias", "l1", "gelu", "l2", "add", "store")}
        STAGE = {key: stage for stage, keys in STAGE.items() for key in keys}
        AHEAD = {"a": 2, "p": 1, "g": 0, "m": -1}
        LOOP_FROM = 2
        TURNS = (STEPS - 1 - AHEAD["a"] - LOOP_FROM) // 2

        def main_program(eng, stage_fn):
            def step(n, u):
                for name in ORDER:
                    key, *arg = name.split()
                    ahead = AHEAD[STAGE[key]]
                    s = n + ahead
                    if not (isinstance(n, int) and not 0 <= s < STEPS):
                        stage_fn(key, s, [int(n) for n in arg], (u + ahead) % 2)

            for n in range(LOOP_FROM):
                step(n, n % 2)
            with eng.Fori(0, TURNS) as turn:
                for b in range(2):
                    step(turn * 2 + (LOOP_FROM + b), b)
            for n in range(LOOP_FROM + 2 * TURNS, STEPS + 1):
                step(n, n % 2)

        weights = [([w["wk"], w["wv"]], "kv"), ([w["wq"], w["wg1"]], "q1"), ([w["wg2"]], "g2")]
        weights += [([w["we1"][e], w["we2"][e]], e) for e in range(NE)]
        PIECES = [0]
        for sources, _ in weights:
            PIECES.append(PIECES[-1] + len(sources))

        EARLY_W = 7
        BESIDE = {j: [f"w {EARLY_W + j // 2} {j % 2}"] for j in range(2 * (len(weights) - EARLY_W))}
        BESIDE[3] += ["loadxa 0", "hot 0 0"]
        BESIDE[5] += ["hot 0 1"]
        BESIDE.update({9: ["agg 0 0", "hot 1 0"], 19: ["agg 0 1", "loadxa 1", "hot 1 1"], 27: ["agg 1 0"], 37: ["agg 1 1"]})
        MIX_AHEAD = 4
        MIX_LOOP = 8

        def mix_program(eng, tile_fn, weight_fn, stage_fn):
            def hook(j):
                for name in BESIDE.get(j, []):
                    key, *arg = name.split()
                    n = int(arg[0])
                    if key == "w":
                        weight_fn(n, int(arg[1]))
                    elif key == "loadxa":
                        stage_fn(key, n, [], n % 2)
                    else:
                        for part in range(CUTS):
                            stage_fn(key, n, [int(arg[1]), part], n % 2)
                        if key == "agg":
                            stage_fn("h", n, [int(arg[1])], n % 2)

            end = (TILES - 1 - MIX_AHEAD) // 2 * 2
            j = 0
            while j < TILES:
                stop = min([t + 1 for t in BESIDE if t >= j] + [end])
                if MIX_LOOP <= j < end and stop - j >= 4:
                    with eng.Fori(j // 2, stop // 2) as turn:
                        tile_fn(turn * 2, 0)
                        tile_fn(turn * 2 + 1, 1)
                    j = stop
                else:
                    tile_fn(j, j % 2)
                    j += 1
                hook(j - 1)

        def pair_program(eng, tile_fn, start=0):
            for u in range(start, 2):
                tile_fn(u, 0, u)
            with eng.Fori(1, TILES // 2) as r:
                for u in range(2):
                    tile_fn(r * 2 + u, r, u)
            for tile in range(TILES // 2 * 2, TILES):
                tile_fn(tile, tile // 2, tile % 2)

        def ln_tiles(b):
            return min(LB * (b + 1), TILES)

        def beyond(j, k=TILES):
            return isinstance(j, int) and j >= k

        def wait_tile(eng, s, value):
            if not (isinstance(value, int) and value <= 0):
                eng.wait_ge(s, value)

        def parts(n, part):
            key = weights[n][1]
            if key == "kv":
                dst = [wkv[:, part, :, 0:D], wkv[:, part, :, D:2 * D]]
            elif key == "q1":
                dst = [wq[:, part], wg1[:, part]]
            elif key == "g2":
                dst = [wg2[:, part]]
            else:
                dst = [we1[:, part, key], we2[:, part, key]]
            return [(d, stage_w[:, n % 2, i * KH:(i + 1) * KH, :]) for i, d in enumerate(dst)]

        def staged(n):
            return [(source.rearrange("(k p) n -> p k n", p=P), stage_w[:, n % 2, i * KH:(i + 1) * KH, :])
                    for i, source in enumerate(weights[n][0])]

        def loaded_pieces(n):
            return sum(PIECES[i + 1] - PIECES[i] for i in range(n % 2, n + 1, 2))

        block = ctx.enter_context(nc.Block())

        @block.sync
        def _(sp):
            def batch(dram, b):
                if b == LBATCHES:
                    return dram[b * LB * P:N, :]
                return dram[b * LB * P:(b + 1) * LB * P, :].rearrange("(t p) c -> p t c", p=P)

            def load_x(b, half):
                if b > LBATCHES:
                    return
                if b >= 2:
                    sp.wait_ge(s_lxn, LB * (b - 2) + (half + 1) * LB // 2)
                cut_ = slice(half * LB // 2, (half + 1) * LB // 2)
                if b < LBATCHES:
                    sp.dma_start(lx[:, b % 2, cut_], batch(x_d, b)[:, cut_]).then_inc(s_lx[b % 2][half], 16)
                elif half == 0:
                    sp.dma_start(lx[0:LAST_ROWS, b % 2, 0, :], batch(x_d, b)).then_inc(s_lx[b % 2][half], 16)

            def load_w(n):
                if n >= 2:
                    sp.wait_ge(s_wlo, PIECES[n - 1])
                for source, to in staged(n):
                    sp.dma_start(to, source).then_inc(s_wload[n % 2], 16)

            load_x(0, 0)
            load_x(0, 1)
            load_w(0)
            load_x(1, 0)
            load_x(1, 1)
            sp.dma_start(d_cur, dst_d[0:P * CHUNKS].rearrange("(p c) -> p c", p=P)).then_inc(s_dst, 16)
            sp.dma_start(d_next, dst_d[1:P * CHUNKS + 1].rearrange("(p c) -> p c", p=P)).then_inc(s_dst, 16)
            sp.dma_start(d_last, w["last_dst"].broadcast_to([TILES, CHUNKS])).then_inc(s_dst, 16)
            load_w(1)
            sp.dma_start(wo[:, :, :], w["wo"].rearrange("(k p) n -> p k n", p=P)).then_inc(s_wo, 16)
            for b in range(LBATCHES + 1):
                last = b == LBATCHES
                load_x(b + 2, 0)
                sp.wait_ge(s_lxn, ln_tiles(b))
                sp.dma_start(batch(xn_d, b), lxn[b % 2][0:LAST_ROWS, 0, :] if last else lxn[b % 2]
                             ).then_inc(s_lout[b % 2], 16)
                load_x(b + 2, 1)
                sp.wait_ge(s_llo, ln_tiles(b))
                rows16 = ltab[0:LAST_ROWS, b % 2, 0].rearrange("p h c -> p (h c)") if last else \
                    ltab[:, b % 2].rearrange("p t h c -> p t (h c)")
                sp.dma_start(batch(table_d, b), rows16).then_inc(s_lout[b % 2], 16)
                load_w(b + 2)
                if b == 3:
                    sp.wait_ge(s_ctlchain, CTL_CHAIN)
                    sp.dma_start(ctl_d, ctl_i[0:TILES, :]).then_inc(s_ctlo, 16)
                    sp.wait_ge(s_ctlo, 16)
                    sp.dma_start(control[:, :, :], ctl_d.rearrange("(o t) c -> o t c", o=1)).then_inc(s_ctl, 16)
            sp.wait_ge(s_most, 1)

            def start_of(tile):
                return sp.value_load(control[0:1, tile, 0:1] if isinstance(tile, int) else control[0:1, bass.ds(tile, 1), 0],
                                     min_val=0, max_val=E)

            def segment(dram, start):
                return dram[bass.ds(start, SEG)].rearrange("(p j) -> p j", p=P)

            extra = sp.value_load(most[0:1, 0:1], min_val=0, max_val=MAX_EXTRA)
            def table_complete():
                for b in range(2):
                    sp.wait_ge(s_lout[b], 32 * len(range(b, LBATCHES + 1, 2)))
                sp.sem_inc(s_table, 1)

            with sp.If(extra > 0):
                table_complete()
                with sp.Fori(0, TILES) as tile:
                    sp.dma_start(rest_d[bass.ds(tile * P, P), :], bout2[:, :]).then_inc(s_xout, 16)
                    sp.wait_ge(s_xout, 16)
                    sp.sem_clear(s_xout)
                with sp.Fori(0, extra) as k:
                    with sp.Fori(0, TILES) as tile:
                        start = start_of(tile)
                        sp.dma_start(idx_stage[:, 0, :], segment(src_d, start + (k * SEG + SEG))).then_inc(s_xidx, 16)
                        sp.dma_start(dst_stage[:, 0, :], segment(dst_d, start + (k * SEG + SEG))).then_inc(s_xdst, 16)
                        sp.dma_start(xa[:, 0, :], rest_d[bass.ds(tile * P, P), :]).then_inc(s_xbase, 16)
                        sp.wait_ge(s_xadd, 1)
                        sp.sem_clear(s_xadd)
                        sp.dma_start(rest_d[bass.ds(tile * P, P), :], xa[:, 0, :]).then_inc(s_xout, 16)
                        sp.wait_ge(s_xout, 16)
                        sp.sem_clear(s_xout)

            def indices(tile, r, u):
                start = start_of(tile)
                if not (isinstance(r, int) and r == 0):
                    sp.wait_ge(s_gath[u], r * (16 * J))
                    sp.sem_inc(s_gate, 1)
                    sp.wait_ge(c_rel.sem, tile - 1)
                    sp.sem_inc(s_gate, 1)
                sp.dma_start(idx_stage[:, u, :], segment(src_d, start)).then_inc(s_idx[u], 16)
                sp.dma_start(dst_stage[:, u, :], segment(dst_d, start)).then_inc(s_dstl[u], 16)

            sp.sem_inc(s_rest, 1)
            for tile in range(2):
                indices(tile, 0, tile)
            with sp.If(extra < 1):
                table_complete()
            pair_program(sp, indices, 2)

        @block.gpsimd
        def _(pool):
            for u in range(2):
                pool.memset(vf[:, u, :, P:P + 2], 1.0).then_inc(s_kv1, 1)
            pool.memset(ident[:, :], 0.0).then_inc(s_const, 1)
            pool.memset(headmask[:, :], 0.0).then_inc(s_const, 1)
            pool.memset(ones[:, :], 1.0).then_inc(s_const, 1)
            pool.iota(tile_base[:, :], [[P, TILES]], base=0, channel_multiplier=0,
                      allow_small_or_imprecise_dtypes=True).then_inc(s_const, 1)
            pool.iota(iota_h[:, :], [[1, P]], base=0, channel_multiplier=0,
                      allow_small_or_imprecise_dtypes=True).then_inc(s_const, 1)
            pool.iota(iota8[:, :], [[1, NE]], base=0, channel_multiplier=0,
                      allow_small_or_imprecise_dtypes=True).then_inc(s_const, 1)
            pool.iota(cs[:, 0:2], [[P, 2]], base=0, channel_multiplier=P,
                      allow_small_or_imprecise_dtypes=True).then_inc(s_const, 1)
            pool.iota(seg_ends, [[SEG, MAX_EXTRA]], base=SEG, channel_multiplier=0,
                      allow_small_or_imprecise_dtypes=True).then_inc(s_const, 1)
            pool.wait_ge(s_const, 8)
            pool.affine_select(out=ident[:, :], in_=ident[:, :], compare_op=ALU.not_equal, fill=1.0, base=0,
                               pattern=[[-1, P]], channel_multiplier=1).then_inc(s_const, 1)
            for b in range(P // HD):
                pool.wait_ge(s_const, 9 + b)
                pool.memset(headmask[b * HD:(b + 1) * HD, b * HD:(b + 1) * HD], 1.0).then_inc(s_const, 1)
            pool.wait_ge(s_const, 9 + P // HD)
            for n in range(EARLY_W):
                pool.wait_ge(s_whi, PIECES[n + 1])
                for (lo, whole), (hi, _) in zip(parts(n, 1), parts(n, 0)):
                    pool.tensor_tensor(out=lo, in0=whole, in1=hi.bitcast(F32), op=ALU.subtract).then_inc(s_wlo, 1)
                if n == 1:
                    pool.wait_ge(s_ctlchain, CTL_CHUNKS)
                    for n in range(2):
                        pool.indirect_dma_start(
                            out=d_row[:, n, :], out_offset=None, in_=dst_d[0:(CHUNKS + 1) * P].rearrange("(c p) -> c p", p=P),
                            in_offset=bass.IndirectOffsetOnAxis(ap=row_i[0:TILES, n:n + 1].bitcast(U32), axis=0),
                            bounds_check=CHUNKS, oob_is_err=False).then_inc(s_row[n], 16)
            def gather(u, j, landed):
                pool.indirect_dma_start(
                    out=ring[:, u, j, :].bitcast(F32), out_offset=None, in_=table_d.bitcast(F32),
                    in_offset=bass.IndirectOffsetOnAxis(ap=idx_stage[:, u, j:j + 1].bitcast(U32), axis=0),
                    bounds_check=N - 1, oob_is_err=False).then_inc(landed, 16)

            pool.wait_ge(s_table, 1)
            pool.wait_ge(s_most, 1)
            extra = pool.value_load(most[0:1, 0:1], min_val=0, max_val=MAX_EXTRA)
            with pool.If(extra > 0):
                with pool.Fori(0, extra):
                    with pool.Fori(0, TILES):
                        pool.wait_ge(s_xidx, 16)
                        pool.sem_clear(s_xidx)
                        for j in range(J):
                            gather(0, j, s_xgath[j])

            def gathers(tile, r, u):
                pool.wait_ge(s_idx[u], r * 16 + 16)
                if not isinstance(r, int):
                    pool.sem_inc(s_grant, 1)
                if not (isinstance(r, int) and r == 0):
                    pool.wait_ge(c_agg.sem, tile - 1)
                    if not isinstance(r, int):
                        pool.sem_inc(s_grant, 1)
                for j in range(J):
                    gather(u, j, s_gath[u])

            pair_program(pool, gathers)

        @block.scalar
        def _(act):
            act.dma_start(bkv[:, 0, :], w["bk"].broadcast_to([P, D])).then_inc(s_bias, 16)
            act.dma_start(bkv[:, 1, :], w["bv"].broadcast_to([P, D])).then_inc(s_bias, 16)
            act.dma_start(bout[:, :], w["bg2"].broadcast_to([P, D])).then_inc(s_bias, 16)
            act.dma_start(bout2[:, :], w["bo"].broadcast_to([P, D])).then_inc(s_bias, 16)
            act.dma_start(bq[:, :], w["bq"]).then_inc(s_bias, 16)
            act.dma_start(bg1[:, :], w["bg1"]).then_inc(s_bias, 16)
            act.dma_start(be1[:, :, :], w["be1"]).then_inc(s_bias, 16)
            act.dma_start(be2[:, :], w["be2"]).then_inc(s_bias, 16)
            act.dma_start(eps1[:, :], w["eps"].broadcast_to([P, 1])).then_inc(s_bias, 16)
            act.dma_start(wr_f[:, :, :], w["wr"]).then_inc(s_bias, 16)

            def load_mix(j, u):
                wait_tile(act, s_mt, j - 1)
                src = xn_d[j * P:j * P + rows_of(j), :] if isinstance(j, int) else xn_d[bass.ds(j * P, P), :]
                act.dma_start(mxn[0:rows_of(j), u, :], src).then_inc(s_mxn[u], 16)

            def weight_hi(n):
                act.wait_ge(s_wload[n % 2], 16 * loaded_pieces(n))
                for hi, whole in parts(n, 0):
                    act.activation(hi, whole, ACT.Copy).then_inc(s_whi, 1)

            def weight_beside(n, i):
                act.wait_ge(s_wload[n % 2], 16 * loaded_pieces(n))
                hi, whole = parts(n, 0)[i]
                act.activation(hi, whole, ACT.Copy).then_inc(s_whi, 1)
                if EARLY_W < n < len(weights) - 1 and i == 0:
                    act.wait_ge(s_wlo2, PIECES[n] - PIECES[EARLY_W])
                    for source, to in staged(n + 1):
                        act.dma_start(to, source).then_inc(s_wload[(n + 1) % 2], 16)

            for b in range(LBATCHES + 1):
                nt = LB if b < LBATCHES else 1
                r = P if b < LBATCHES else LAST_ROWS
                act.wait_ge(s_lrs, b + 1)
                if b >= 2:
                    act.wait_ge(s_lout[b % 2], 32 * (b // 2))
                first = LB * b
                if b == LBATCHES:
                    load_mix(0, 0)
                    load_mix(1, 1)

                def table_hi(t):
                    act.wait_ge(s_lxn, first + t + 1)
                    act.activation(ltab[0:r, b % 2, t, 0, :], lxn[b % 2][0:r, t, :], ACT.Copy,
                                   scale=TABLE_SCALE).then_inc(s_lhi, 1)

                for t in range(nt):
                    act.activation(lxn[b % 2][0:r, t, :], lx[0:r, b % 2, t, :], ACT.Identity,
                                   bias=lnm[0:r, b % 2, t:t + 1], scale=lrs[0:r, b % 2, t:t + 1]).then_inc(s_lxn, 1)
                    if t > 0:
                        table_hi(t - 1)
                table_hi(nt - 1)
                if b < EARLY_W:
                    weight_hi(b)
            act.wait_ge(s_bias, 160)
            act.activation(wr[:, 0], wr_f[:, :, :], ACT.Copy).then_inc(s_wrs, 1)

            def split_mix(j, u):
                r = rows_of(j)
                act.wait_ge(s_mt, j + 1)
                wait_tile(act, s_kvp, j - 1)
                act.activation(mxT[:, u, 0, :, 0:r], halves(ps_mt[u])[:, :, 0:r], ACT.Copy).then_inc(s_mhi, 1)

            def mix_tile(j, u):
                if not beyond(j + 2):
                    split_mix(j + 2, u)
                    if not beyond(j + MIX_AHEAD):
                        load_mix(j + MIX_AHEAD, u)
                r = rows_of(j)
                act.wait_ge(s_kb, 2 * j + 1)
                wait_tile(act, s_kf, j - 1)
                act.activation(kr[0:r, u, :], kb[0:r, u, :], ACT.Relu, scale=-1.0).then_inc(s_kr, 1)
                act.wait_ge(s_kr, j + 1)
                act.activation(kr[0:r, u, :], kr[0:r, u, :], ACT.Exp, scale=-1.0).then_inc(s_ke, 1)

            def stage(key, s, arg, v):
                i = arg[0] if arg else None
                if key == "loadxn":
                    c_tx.wait(act, s, 0)
                    act.dma_start(super_buf(xn2, s), super_rows(xn_d, s)).then_inc(c_xn2.sem, 16)
                elif key == "loadxa":
                    if isinstance(s, int) and s == 0:
                        act.wait_ge(s_table, 1)
                        act.wait_ge(s_rest, 1)
                        stage("loadxn", 0, [], 0)
                    c_h.wait(act, s, 0)
                    act.dma_start(super_buf(xa, s), super_rows(xn_d, s)).then_inc(c_xa.sem, 16)
                    with act.If(act_extra > 0):
                        c_th.wait(act, s, -1)
                        act.dma_start(super_buf(h[v], s), super_rows(rest_d, s)).then_inc(c_rest.sem, 16)
                elif key == "gelu":
                    c_l1.wait(act, s, i + 1)
                    c_glo.wait(act, s, i - 1)
                    for half in range(KH):
                        last = act.activation(tokens(gact[:, i % 2], s)[:, half], tokens(halves(ps_l1[i % 2]), s)[:, half],
                                              ACT.Gelu, bias=be1[:, i, half:half + 1])
                    last.then_inc(c_g.sem, 1)
                    c_g.wait(act, s, i + 1)
                    c_l2.wait(act, s, i - 1)
                    act.activation(tokens(gT[:, i % 2, 0], s), tokens(gact[:, i % 2], s), ACT.Copy).then_inc(c_ghi.sem, 1)
                elif key == "store" and not (isinstance(s, int) and s == 0):
                    c_add.wait(act, s, 0)
                    act.dma_start(super_rows(out_d, s - 1), super_buf(acc[:, 1 - v], s - 1)).then_inc(c_out.sem, 16)
                elif key == "combcopy":
                    c_ct.wait(act, s, 1)
                    n = SUPER * P if tiles_of(s) == SUPER else LAST_ROWS
                    act.activation(combT[:, 0:n], ps_l2[1][0:NE, 0:n], ACT.Copy).then_inc(c_ctc.sem, 1)
                elif key == "split":
                    c_x1.wait(act, s, 0)
                    act.dma_start(super_buf(xs, s), super_rows(x_d, s)).then_inc(c_xs.sem, 16)
                    c_tx.wait(act, s, 1)
                    c_q.wait(act, s, 0)
                    act.activation(tokens(xT[:, 0], s), tokens(halves(ps_g[0]), s), ACT.Copy).then_inc(c_xhi.sem, 1)
                    c_th.wait(act, s, 1)
                    c_w1.wait(act, s, 0)
                    act.activation(tokens(hT[:, 0], s), tokens(halves(ps_g[1]), s), ACT.Copy,
                                   scale=1.0 / TABLE_SCALE).then_inc(c_hhi.sem, 1)
                elif key == "qexp":
                    c_q.wait(act, s, 1)
                    c_nt.wait(act, s, 0)
                    for half in range(KH):
                        last = act.activation(tokens(ex, s)[:, half], tokens(halves(ps_g[2]), s)[:, half], ACT.Relu,
                                              bias=nbq[:, half:half + 1], scale=-1.0)
                    last.then_inc(c_qneg.sem, 1)
                    c_qneg.wait(act, s, 1)
                    act.activation(tokens(ex, s), tokens(ex, s), ACT.Exp, scale=-1.0).then_inc(c_qexp.sem, 1)
                elif key == "relu":
                    c_w1.wait(act, s, 1)
                    c_rlo.wait(act, s, 0)
                    for half in range(KH):
                        last = act.activation(tokens(rT, s)[:, half], tokens(halves(ps_g[0]), s)[:, half], ACT.Relu,
                                              bias=bg1[:, half:half + 1])
                    last.then_inc(c_r.sem, 1)
                    c_r.wait(act, s, 1)
                    c_o.wait(act, s, 0)
                    act.activation(tokens(rTs[:, 0], s), tokens(rT, s), ACT.Copy).then_inc(c_rhi.sem, 1)
                elif key == "spread":
                    c_nr.wait(act, s, 1)
                    r, nt = rows(s), tiles_of(s)
                    act.activation(ex[0:r, 0:nt].rearrange("p t (h c) -> p (t h) c", c=HD),
                                   rn8[0:r, 0:nt].rearrange("p t k h -> p (t k h)").rearrange("p (h o) -> p h o", o=1).broadcast_to(
                                       [r, nt * D // HD, HD]), ACT.Copy).then_inc(c_nx.sem, 1)
                elif key == "qsplit":
                    c_qs.wait(act, s, 1)
                    act.activation(tokens(qTs[:, 0], s), tokens(qs, s), ACT.Copy).then_inc(c_qhi.sem, 1)
                elif key == "tok":
                    c_ln.wait(act, s, 1)
                    c_acc.wait(act, s, 0)
                    for t in range(tiles_of(s)):
                        act.activation(tok[0:rows(s), t, :], acc[0:rows(s), v, t, :], ACT.Identity,
                                       bias=gnm[0:rows(s), t:t + 1], scale=gy[0:rows(s), t:t + 1]).then_inc(c_tok.sem, 1)
                elif key == "toksplit":
                    c_tk.wait(act, s, 1)
                    c_l1.wait(act, s, -NE)
                    act.activation(tokens(tokT[:, v, 0], s), tokens(halves(ps_g[0]), s), ACT.Copy).then_inc(c_khi.sem, 1)
                elif key == "weigh":
                    c_top.wait(act, s, 1)
                    for t in range(tiles_of(s)):
                        last = act.activation(etop[0:rows(s), t, :], top[0:rows(s), t, :], ACT.Exp,
                                              bias=ntop[0:rows(s), t:t + 1], accum_out=esum[0:rows(s), t:t + 1])
                    last.then_inc(c_et.sem, 1)

            act.wait_ge(s_most, 1)
            act_extra = act.value_load(most[0:1, 0:1], min_val=0, max_val=MAX_EXTRA)
            split_mix(0, 0)
            load_mix(2, 0)
            split_mix(1, 1)
            load_mix(3, 1)
            mix_program(act, mix_tile, weight_beside, stage)
            act.wait_ge(s_kvy, 2)
            act.activation(kvwo[:, 0, :, :], halves(ps_g[1]), ACT.Copy).then_inc(s_kvz, 1)

            main_program(act, stage)
            last = STEPS - 1
            c_add.wait(act, last, NE)
            act.dma_start(super_rows(out_d, last), super_buf(acc[:, last % 2], last)).then_inc(c_out.sem, 16)
            act.wait_ge(c_out.sem, 16 * STEPS)

        @block.tensor
        def _(pe):
            pe.wait_ge(s_const, 9 + P // HD)
            pe.wait_ge(s_ctlchain, 2)
            pe.matmul(ps_g[2][0:TILES, 0:1], ones[:, 0:TILES], cs[:, 4:5], start=True, stop=True).then_inc(s_viol, 1)

            def chunk_sum(u, j):
                return pe.matmul(ps_agg[:, :], onehot[:, u, j, :], ring[:, u, j, :], start=j == 0, stop=j == J - 1)

            pe.wait_ge(s_most, 1)
            extra = pe.value_load(most[0:1, 0:1], min_val=0, max_val=MAX_EXTRA)
            with pe.If(extra > 0):
                with pe.Fori(0, extra) as k:
                    with pe.Fori(0, TILES) as tile:
                        pe.wait_ge(s_xhot, 1)
                        pe.sem_clear(s_xhot)
                        for j in range(J):
                            pe.wait_ge(s_xgath[j], (k * TILES + tile) * 16 + 16)
                            last = chunk_sum(0, j)
                        last.then_inc(s_xsum, 1)

            def transposes_mix(j, u):
                r = rows_of(j)
                if isinstance(j, int):
                    pe.wait_ge(s_mxn[u], 16 * (j // 2 + 1))
                else:
                    pe.wait_ge(s_mxn[u], j * 8 + (16 - 8 * u))
                wait_tile(pe, s_mlo, j - 1)
                for k in range(KH):
                    last = pe.transpose(halves(ps_mt[u])[:, k, 0:r], mxn[0:r, u, k * P:(k + 1) * P], ident[0:r, 0:r])
                last.then_inc(s_mt, 1)

            def project_mix(j, u):
                r = rows_of(j)
                pe.wait_ge(s_mhi, j + 1)
                pe.wait_ge(s_mlo, j + 1)
                wait_tile(pe, s_kb, 2 * (j - 1))
                n = 0
                for wp, ap in PASSES:
                    for k in range(KH):
                        last = pe.matmul(ps_kvp[u][0:r, :], mxT[:, u, ap, k, 0:r], wkv[:, wp, k, :],
                                         start=n == 0, stop=n == len(PASSES) * KH - 1)
                        n += 1
                last.then_inc(s_kvp, 1)

            def accumulate_mix(j, u):
                r = rows_of(j)
                pe.wait_ge(s_kf, j + 1)
                pe.wait_ge(s_kb, 2 * j + 2)
                for k in range(KH):
                    last = pe.matmul(ps_kva[k][:, 0:P + 1], kf[0:r, u, k * P:(k + 1) * P], vf[0:r, u, k, 0:P + 1],
                                     start=isinstance(j, int) and j == 0, stop=isinstance(j, int) and j == TILES - 1,
                                     skip_group_check=True)
                last.then_inc(s_kva, 1)

            def mix_tile(j, u):
                late = isinstance(j, int) and j < 2
                if not beyond(j + 2) and not late:
                    transposes_mix(j + 2, u)
                project_mix(j, u)
                if late:
                    transposes_mix(j + 2, u)
                if not (isinstance(j, int) and j < 2):
                    accumulate_mix(j - 2, u)

            def product_T(bank_, weight, act_parts, s):
                for half in range(KH):
                    n = 0
                    for wp, ap in PASSES:
                        for k in range(KH):
                            last = pe.matmul(tokens(halves(bank_), s)[:, half], weight[:, wp, k, half * P:(half + 1) * P],
                                             tokens(act_parts[:, ap], s)[:, k], start=n == 0,
                                             stop=n == len(PASSES) * KH - 1, skip_group_check=True)
                            n += 1
                return last

            def product(bank_, pairs, s, t):
                r = rows(s)
                n = 0
                for act_parts, weight in pairs:
                    for wp, ap in PASSES:
                        for k in range(KH):
                            last = pe.matmul(halves(bank_)[0:r, t, :], act_parts[:, ap, k, t * P:t * P + r],
                                             weight[:, wp, k, :], start=n == 0,
                                             stop=n == len(pairs) * len(PASSES) * KH - 1, skip_group_check=True)
                            n += 1
                return last

            def transposes(bank_, src, s, ready=None):
                r = rows(s)
                for t in range(tiles_of(s)):
                    if ready:
                        ready.wait(pe, s, t + 1)
                    for k in range(KH):
                        last = pe.transpose(halves(bank_)[:, k, t * P:t * P + r], src[0:r, t, k * P:(k + 1) * P],
                                            ident[0:r, 0:r])
                return last

            def stage(key, s, arg, v):
                i = arg[0] if arg else None
                if key == "l1":
                    if i == 0:
                        c_khi.wait(pe, s, 1)
                        c_klo.wait(pe, s, 1)
                    c_g.wait(pe, s, i - 1)
                    product_T(ps_l1[i % 2], we1[:, :, i], tokT[:, v], s).then_inc(c_l1.sem, 1)
                elif key == "l2":
                    c_ghi.wait(pe, s, i + 1)
                    c_glo.wait(pe, s, i + 1)
                    c_accb.wait(pe, s, 1) if i == 1 else c_add.wait(pe, s, i - 1)
                    for t in range(tiles_of(s)):
                        last = product(ps_l2[i % 2], [(gT[:, i % 2], we2[:, :, i])], s, t)
                    last.then_inc(c_l2.sem, 1)
                elif key == "combT":
                    c_comb.wait(pe, s, 1)
                    c_add.wait(pe, s, 0)
                    r = rows(s)
                    for t in range(tiles_of(s)):
                        last = pe.transpose(ps_l2[1][0:NE, t * P:t * P + r], comb[0:r, v, t, :], ident[0:r, 0:r])
                    last.then_inc(c_ct.sem, 1)
                elif key == "bias2":
                    c_ctc.wait(pe, s, 1)
                    r = rows(s)
                    for t in range(tiles_of(s)):
                        last = pe.matmul(halves(ps_l2[1])[0:r, t, :], combT[:, t * P:t * P + r], be2[:, :],
                                         start=True, stop=True, skip_group_check=True)
                    last.then_inc(c_b2.sem, 1)
                elif key == "trans":
                    c_xn2.wait(pe, s, 16)
                    c_khi.wait(pe, s, 0)
                    c_klo.wait(pe, s, 0)
                    transposes(ps_g[0], xn2, s).then_inc(c_tx.sem, 1)
                    c_h.wait(pe, s, tiles_of(s))
                    c_top.wait(pe, s, 0)
                    transposes(ps_g[1], h[v], s).then_inc(c_th.sem, 1)
                elif key == "q":
                    c_xhi.wait(pe, s, 1)
                    c_xlo.wait(pe, s, 1)
                    c_x1.wait(pe, s, 0)
                    product_T(ps_g[2], wq, xT, s).then_inc(c_q.sem, 1)
                elif key == "gin1":
                    c_hhi.wait(pe, s, 1)
                    c_hlo.wait(pe, s, 1)
                    product_T(ps_g[0], wg1, hT, s).then_inc(c_w1.sem, 1)
                elif key == "norm":
                    c_qf.wait(pe, s, 1)
                    c_hhi.wait(pe, s, 1)
                    c_hlo.wait(pe, s, 1)
                    r = rows(s)
                    for t in range(tiles_of(s)):
                        for k in range(KH):
                            c = (t * KH + k) * (P // HD)
                            last = pe.matmul(ps_g[1][0:r, c:c + P // HD], qf[:, k, t * P:t * P + r], ksm[:, k, :],
                                             start=True, stop=True, skip_group_check=True)
                    last.then_inc(c_n.sem, 1)
                elif key == "norm2":
                    c_nx.wait(pe, s, 1)
                    transposes(ps_g[1], ex, s).then_inc(c_nt.sem, 1)
                elif key == "out":
                    c_rhi.wait(pe, s, 1)
                    c_rlo.wait(pe, s, 1)
                    c_qhi.wait(pe, s, 1)
                    c_qlo.wait(pe, s, 1)
                    c_qf.wait(pe, s, 1)
                    c_r.wait(pe, s, 1)
                    for t in range(tiles_of(s)):
                        product(ps_out[t], [(rTs, wg2), (qTs, kvwo)], s, t).then_inc(c_o.sem, 1)
                elif key == "tokT":
                    c_r.wait(pe, s, 1)
                    c_x1.wait(pe, s, tiles_of(s))
                    transposes(ps_g[0], tok, s, c_tok).then_inc(c_tk.sem, 1)
                elif key == "router":
                    c_khi.wait(pe, s, 1)
                    c_klo.wait(pe, s, 1)
                    c_qs.wait(pe, s, 1)
                    r = rows(s)
                    for t in range(tiles_of(s)):
                        n = 0
                        for wp, ap in PASSES:
                            for k in range(KH):
                                last = pe.matmul(ps_g[1][0:r, t * NE:(t + 1) * NE], tokT[:, v, ap, k, t * P:t * P + r],
                                                 wr[:, wp, k, :], start=n == 0, stop=n == len(PASSES) * KH - 1,
                                                 skip_group_check=True)
                                n += 1
                    last.then_inc(c_lg.sem, 1)
                elif key == "agg" and i < tiles_of(s):
                    part = arg[1]
                    if part == 0:
                        c_h.wait(pe, s, i)
                        pe.wait_ge(s_gath[i], s * (16 * J) + 16 * J)
                    c_hot.wait(pe, s, i * CUTS + part + 1)
                    for j in range(part * JC, (part + 1) * JC):
                        last = chunk_sum(i, j)
                    if part == CUTS - 1:
                        last.then_inc(c_agg.sem, 1)

            pe.wait_ge(s_wlo, PIECES[1])
            pe.wait_ge(s_kv1, 2)
            transposes_mix(0, 0)
            transposes_mix(1, 1)
            mix_program(pe, mix_tile, lambda n, i: None, stage)
            for j in range(TILES - 2, TILES):
                accumulate_mix(j, j % 2)
            pe.wait_ge(s_kvx, 3)
            for k in range(KH):
                last = pe.transpose(ps_g[0][:, k * P:(k + 1) * P], kvm[:, k, :], ident[:, :])
            last.then_inc(s_kvy, 1)
            pe.wait_ge(s_kvx, 4)
            pe.wait_ge(s_wo, 16)
            for k in range(KH):
                last = pe.matmul(halves(ps_g[1])[:, k, :], kvmT[:, k, :], wo[:, k, :], start=True, stop=True)
            last.then_inc(s_kvy, 1)

            pe.wait_ge(s_wlo, PIECES[EARLY_W])
            pe.wait_ge(s_wlo2, PIECES[-1] - PIECES[EARLY_W])
            pe.wait_ge(s_wrs, 2)
            pe.wait_ge(s_kvx, 5)
            main_program(pe, stage)

        @block.vector
        def _(dve):
            def rsqrt(v, y, t, inc, wait):
                inc(dve.tensor_scalar(y.bitcast(I32), v.bitcast(I32), 1, None, ALU.logical_shift_right))
                wait()
                inc(dve.tensor_scalar(y.bitcast(I32), y.bitcast(I32), -1.0, float(MAGIC), ALU.mult, ALU.add))
                for _ in range(3):
                    wait()
                    inc(dve.tensor_tensor(t, y, y, ALU.mult))
                    wait()
                    inc(dve.scalar_tensor_tensor(out=t, in0=t, scalar=-0.5, in1=v, op0=ALU.mult, op1=ALU.mult))
                    wait()
                    inc(dve.scalar_tensor_tensor(out=y, in0=t, scalar=1.5, in1=y, op0=ALU.add, op1=ALU.mult))
                wait()

            def small_values():
                dve.wait_ge(s_bias, 160)
                dve.tensor_tensor(bout[:, :], bout[:, :], bout2[:, :], ALU.add).then_inc(s_bprep, 1)
                dve.wait_ge(s_bprep, 1)
                dve.memset(bout2[:, :], 0.0).then_inc(s_bprep, 1)
                dve.tensor_scalar(nbq[:, :], bq[:, :], -1.0, None, ALU.mult).then_inc(s_bprep, 1)
                dve.tensor_scalar(bq1[:, :], bq[:, :], 1.0, None, ALU.add).then_inc(s_bprep, 1)
                dve.tensor_scalar(eps1[:, :], eps1[:, :], 1.0, TABLE_SCALE, ALU.add, ALU.mult).then_inc(s_bprep, 1)
                dve.wait_ge(s_bprep, 5)
                dve.tensor_copy(own_scale[:, :], eps1[:, :]).then_inc(s_bprep, 1)

            def rsqrt_tiles(v, vh, y, t, inc, wait):
                columns = range(v.shape[1])
                inc(dve.tensor_scalar(y.bitcast(I32), v.bitcast(I32), 1, None, ALU.logical_shift_right))
                wait()
                inc(dve.tensor_scalar(y.bitcast(I32), y.bitcast(I32), -1.0, float(MAGIC), ALU.mult, ALU.add))
                for _ in range(3):
                    wait()
                    for c in columns:
                        inc(dve.scalar_tensor_tensor(out=t[:, c:c + 1], in0=y[:, c:c + 1], scalar=vh[:, c:c + 1],
                                                     in1=y[:, c:c + 1], op0=ALU.mult, op1=ALU.mult))
                    wait()
                    inc(dve.scalar_tensor_tensor(out=y, in0=t, scalar=1.5, in1=y, op0=ALU.add, op1=ALU.mult))
                wait()

            chain, lo_tiles = [0], []

            def l_inc(ins):
                ins.then_inc(s_lchain, 1)
                chain[0] += 1

            def l_wait():
                if lo_tiles:
                    table_lo(*lo_tiles.pop(0))
                dve.wait_ge(s_lchain, chain[0])

            T = TILES

            def control_chunks():
                dve.wait_ge(s_dst, 48)
                dve.wait_ge(s_const, 9 + P // HD)
                dve.tensor_tensor(d_bad, d_next, d_cur, ALU.is_lt).then_inc(s_ctlchain, 1)
                dve.wait_ge(s_ctlchain, 1)
                dve.tensor_reduce(cs[:, 4:5], d_bad, AX_X, ALU.add).then_inc(s_ctlchain, 1)
                dve.wait_ge(s_ctlchain, 2)
                for n in range(2):
                    dve.tensor_scalar(d_bad[0:T, :], d_last, cs[0:T, n:n + 1], None, ALU.is_lt).then_inc(s_ctlchain, 1)
                    dve.wait_ge(s_ctlchain, 3 + 2 * n)
                    dve.tensor_reduce(cs[0:T, 5 + n:6 + n], d_bad[0:T, :], AX_X, ALU.add).then_inc(s_ctlchain, 1)
                    dve.wait_ge(s_ctlchain, 4 + 2 * n)
                dve.tensor_copy(row_i[0:T, :], cs[0:T, 5:7]).then_inc(s_ctlchain, 1)

            def control_edges():
                k = CTL_CHUNKS
                for n in range(2):
                    dve.wait_ge(s_row[n], 16)
                    dve.tensor_scalar(d_bad[0:T, 0:P], d_row[:, n, :], cs[0:T, n:n + 1], None, ALU.is_lt).then_inc(s_ctlchain, 1)
                    dve.wait_ge(s_ctlchain, k + 1)
                    dve.tensor_reduce(cs[0:T, 7 + n:8 + n], d_bad[0:T, 0:P], AX_X, ALU.add).then_inc(s_ctlchain, 1)
                    dve.wait_ge(s_ctlchain, k + 2)
                    k += 2
                dve.scalar_tensor_tensor(out=cs[0:T, 9:11], in0=cs[0:T, 5:7], scalar=float(P), in1=cs[0:T, 7:9],
                                         op0=ALU.mult, op1=ALU.add).then_inc(s_ctlchain, 1)
                dve.wait_ge(s_viol, 1)
                dve.tensor_scalar(cs[0:T, 11:12], ps_g[2][0:T, 0:1], 0.5, None, ALU.is_lt).then_inc(s_ctlchain, 1)
                dve.wait_ge(s_ctlchain, k + 2)
                dve.tensor_tensor(cs[0:T, 12:13], cs[0:T, 10:11], cs[0:T, 9:10], ALU.subtract).then_inc(s_ctlchain, 1)
                dve.tensor_tensor(ctl_i[0:T, 0:1], cs[0:T, 9:10], cs[0:T, 11:12], ALU.mult).then_inc(s_ctlchain, 1)
                dve.wait_ge(s_ctlchain, k + 4)
                dve.tensor_scalar(d_bad[0:T, 0:MAX_EXTRA], seg_ends, cs[0:T, 12:13], None, ALU.is_lt).then_inc(s_ctlchain, 1)
                dve.wait_ge(s_ctlchain, k + 5)
                dve.tensor_reduce(cs[0:T, 13:14], d_bad[0:T, 0:MAX_EXTRA], AX_X, ALU.add).then_inc(s_ctlchain, 1)
                dve.wait_ge(s_ctlchain, k + 6)
                dve.scalar_tensor_tensor(out=cs[0:T, 14:15], in0=cs[0:T, 13:14], scalar=float(-MAX_EXTRA), in1=cs[0:T, 11:12],
                                         op0=ALU.add, op1=ALU.mult).then_inc(s_ctlchain, 1)
                dve.wait_ge(s_ctlchain, k + 7)
                dve.tensor_scalar(ctl_i[0:T, 1:2], cs[0:T, 14:15], float(MAX_EXTRA), None, ALU.add).then_inc(s_ctlchain, 1)
                assert k + 8 == CTL_CHAIN

            def control_most():
                dve.wait_ge(s_ctl, 16)
                dve.tensor_reduce(most[0:1, 0:1], control[0:1, :, 1], AX_X, ALU.max).then_inc(s_most, 1)

            def batch_size(b):
                return (P, LB) if b < LBATCHES else (LAST_ROWS, 1)

            def scales(b):
                r, nt = batch_size(b)
                for t in range(nt):
                    if t % (LB // 2) == 0:
                        dve.wait_ge(s_lx[b % 2][t // (LB // 2)], 16 * (b // 2 + 1))
                    l_inc(dve.bn_stats(lstat[0:r, t, :], lx[0:r, b % 2, t, :]))
                l_wait()
                for t in range(nt):
                    l_inc(dve.bn_aggr(lmv[0:r, t, :], lstat[0:r, t, :]))
                l_wait()
                l_inc(dve.tensor_scalar(lv[0:r, 0:nt], lmv[0:r, 0:nt, 1], LN_EPS, None, ALU.add))
                l_wait()
                rsqrt(lv[0:r, 0:nt], ly[0:r, 0:nt], lt[0:r, 0:nt], l_inc, l_wait)
                if b >= 2:
                    dve.wait_ge(s_lxn, ln_tiles(b - 2))
                l_inc(dve.tensor_copy(lrs[0:r, b % 2, 0:nt], ly[0:r, 0:nt]))
                dve.scalar_tensor_tensor(out=lnm[0:r, b % 2, 0:nt], in0=lmv[0:r, 0:nt, 0], scalar=-1.0, in1=ly[0:r, 0:nt],
                                         op0=ALU.mult, op1=ALU.mult).then_inc(s_lrs, 1)

            def table_lo(b, t):
                r, _ = batch_size(b)
                dve.wait_ge(s_lhi, LB * b + t + 1)
                dve.scalar_tensor_tensor(out=ltab[0:r, b % 2, t, 1, :], in0=lxn[b % 2][0:r, t, :],
                                         scalar=TABLE_SCALE, in1=ltab[0:r, b % 2, t, 0, :],
                                         op0=ALU.mult, op1=ALU.subtract).then_inc(s_llo, 1)

            between = {0: control_chunks, 1: small_values, 2: control_edges, 4: control_most}
            scales(0)
            for b in range(LBATCHES + 1):
                lo_tiles += [(b, t) for t in range(batch_size(b)[1])]
                if b < LBATCHES:
                    scales(b + 1)
                while lo_tiles:
                    table_lo(*lo_tiles.pop(0))
                if b in between:
                    between[b]()
            dve.wait_ge(s_wrs, 1)
            dve.tensor_tensor(wr[:, 1], wr_f[:, :, :], wr[:, 0].bitcast(F32), ALU.subtract).then_inc(s_wrs, 1)

            def relative(u, tile):
                return dve.tensor_scalar(dst_rel[:, u, :], dst_stage[:, u, :],
                                         tile_base[:, tile:tile + 1] if isinstance(tile, int) else tile_base[:, bass.ds(tile, 1)],
                                         None, ALU.subtract)

            def onehots(u, c, n):
                return dve.tensor_tensor(onehot[:, u, c:c + n], iota_h[:, :].rearrange("p (o c) -> p o c", o=1).broadcast_to([P, n, P]),
                                         dst_rel[:, u, c:c + n].rearrange("p (c o) -> p c o", o=1).broadcast_to([P, n, P]), ALU.is_equal)

            def sum_part(part, r):
                return ps_agg[0:r, part * D:(part + 1) * D]

            extra = dve.value_load(most[0:1, 0:1], min_val=0, max_val=MAX_EXTRA)
            with dve.If(extra > 0):
                with dve.Fori(0, extra):
                    with dve.Fori(0, TILES) as tile:
                        dve.wait_ge(s_xdst, 16)
                        dve.sem_clear(s_xdst)
                        relative(0, tile).then_inc(s_xchain, 1)
                        dve.wait_ge(s_xchain, 1)
                        onehots(0, 0, J).then_inc(s_xhot, 1)
                        dve.wait_ge(s_xsum, 1)
                        dve.sem_clear(s_xsum)
                        dve.wait_ge(s_xbase, 16)
                        dve.sem_clear(s_xbase)
                        dve.tensor_tensor(xa[:, 0, :], sum_part(0, P), xa[:, 0, :], ALU.add).then_inc(s_xchain, 1)
                        dve.wait_ge(s_xchain, 2)
                        dve.sem_clear(s_xchain)
                        dve.tensor_tensor(xa[:, 0, :], sum_part(1, P), xa[:, 0, :], ALU.add).then_inc(s_xadd, 1)
                dve.memset(own_scale[:, :], 1.0).then_inc(s_bprep, 1)

            def weight_beside(n, i):
                dve.wait_ge(s_whi, PIECES[n] + i + 1)
                lo, whole = parts(n, 1)[i]
                dve.tensor_tensor(lo, whole, parts(n, 0)[i][0].bitcast(F32), ALU.subtract).then_inc(s_wlo2, 1)

            def split_mix(j, u):
                r = rows_of(j)
                dve.wait_ge(s_mhi, j + 1)
                dve.tensor_tensor(mxT[:, u, 1, :, 0:r], halves(ps_mt[u])[:, :, 0:r], mxT[:, u, 0, :, 0:r].bitcast(F32),
                                  ALU.subtract).then_inc(s_mlo, 1)

            def mix_tile(j, u):
                r = rows_of(j)
                dve.wait_ge(s_kvp, j + 1)
                wait_tile(dve, s_kf, j - 1)
                dve.tensor_tensor(kb[0:r, u, :], ps_kvp[u][0:r, 0:D], bkv[0:r, 0, :], ALU.add).then_inc(s_kb, 1)
                if not beyond(j + 2):
                    split_mix(j + 2, u)
                if not (isinstance(j, int) and j == 0):
                    features_mix(j - 1, 1 - u)
                wait_tile(dve, s_kva, j - 1)
                dve.tensor_tensor(vf[0:r, u, :, 0:P], halves(ps_kvp[u])[0:r, 1, :].rearrange("p (k c) -> p k c", k=KH),
                                  bkv[0:r, 1, :].rearrange("p (k c) -> p k c", k=KH), ALU.add).then_inc(s_kb, 1)

            def features_mix(j, u):
                r = rows_of(j)
                dve.wait_ge(s_ke, j + 1)
                wait_tile(dve, s_kva, j - 1)
                dve.scalar_tensor_tensor(out=kf[0:r, u, :], in0=kb[0:r, u, :], scalar=0.0, in1=kr[0:r, u, :],
                                         op0=ALU.max, op1=ALU.add).then_inc(s_kf, 1)

            gchain = Chain(s_gchain, G_CHAIN)

            def gate():
                dve.sem_inc(s_gate, 1)

            def lo_part(parts_, whole, s):
                return dve.tensor_tensor(tokens(parts_[:, 1], s), tokens(whole, s), tokens(parts_[:, 0], s).bitcast(F32), ALU.subtract)

            def stage(key, s, arg, v):
                i = arg[0] if arg else None
                r, nt = rows(s), tiles_of(s)
                if key == "hot" and i < nt:
                    tile = s * SUPER + i
                    part = arg[1]
                    if part == 0:
                        dve.wait_ge(s_dstl[i], s * 16 + 16)
                        relative(i, tile).then_inc(c_rel.sem, 1)
                        c_rel.wait(dve, s, i + 1)
                        c_agg.wait(dve, s, i - 1)
                    onehots(i, part * JC, JC).then_inc(c_hot.sem, 1)
                elif key == "h" and i < nt:
                    c_xa.wait(dve, s, 16)
                    if i == 0:
                        gate()
                        with dve.If(extra > 0):
                            c_rest.wait(dve, s, 16)
                            dve.scalar_tensor_tensor(out=cut(xa, s), in0=cut(xa, s), scalar=eps1[0:r, 0:1], in1=cut(h[v], s),
                                                     op0=ALU.mult, op1=ALU.add).then_inc(c_xr.sem, 1)
                            c_xr.wait(dve, s, 1)
                            gate()
                    c_th.wait(dve, s, -1)
                    c_agg.wait(dve, s, i + 1)
                    dve.scalar_tensor_tensor(out=h[v][0:r, i, :], in0=xa[0:r, i, :], scalar=own_scale[0:r, 0:1],
                                             in1=sum_part(0, r), op0=ALU.mult, op1=ALU.add).then_inc(c_hp.sem, 1)
                    c_hp.wait(dve, s, i + 1)
                    dve.tensor_tensor(h[v][0:r, i, :], sum_part(1, r), h[v][0:r, i, :], ALU.add).then_inc(c_h.sem, 1)
                elif key == "gelu":
                    c_ghi.wait(dve, s, i + 1)
                    lo_part(gT[:, i % 2], gact[:, i % 2], s).then_inc(c_glo.sem, 1)
                elif key == "add":
                    c_l2.wait(dve, s, i + 1)
                    c_accb.wait(dve, s, 1) if i == 0 else c_add.wait(dve, s, i)
                    for t in range(nt):
                        last = dve.scalar_tensor_tensor(out=acc[0:r, v, t, :], in0=halves(ps_l2[i % 2])[0:r, t, :],
                                                        scalar=comb[0:r, v, t, i:i + 1], in1=acc[0:r, v, t, :],
                                                        op0=ALU.mult, op1=ALU.add)
                    last.then_inc(c_add.sem, 1)
                elif key == "accbias":
                    c_b2.wait(dve, s, 1)
                    c_acc.wait(dve, s, 1)
                    dve.tensor_tensor(cut(acc[:, v], s), cut(halves(ps_l2[1]), s), cut(acc[:, v], s), ALU.add).then_inc(c_accb.sem, 1)
                elif key == "split":
                    c_xhi.wait(dve, s, 1)
                    lo_part(xT, halves(ps_g[0]), s).then_inc(c_xlo.sem, 1)
                    c_hhi.wait(dve, s, 1)
                    dve.scalar_tensor_tensor(out=tokens(hT[:, 1], s), in0=tokens(halves(ps_g[1]), s), scalar=1.0 / TABLE_SCALE,
                                             in1=tokens(hT[:, 0], s).bitcast(F32), op0=ALU.mult,
                                             op1=ALU.subtract).then_inc(c_hlo.sem, 1)
                elif key == "qexp":
                    c_qexp.wait(dve, s, 1)
                    for half in range(KH):
                        last = dve.scalar_tensor_tensor(out=tokens(qf, s)[:, half], in0=tokens(halves(ps_g[2]), s)[:, half],
                                                        scalar=bq1[:, half:half + 1], in1=tokens(ex, s)[:, half],
                                                        op0=ALU.add, op1=ALU.max)
                    last.then_inc(c_qf.sem, 1)
                elif key == "relu":
                    c_rhi.wait(dve, s, 1)
                    lo_part(rTs, rT, s).then_inc(c_rlo.sem, 1)
                elif key == "recip":
                    c_n.wait(dve, s, 1)
                    dve.tensor_scalar(n8[0:r, 0:nt], ps_g[1][0:r, 0:nt * D // HD].rearrange("p (t k h) -> p t k h", t=nt, k=KH),
                                      NORM_EPS, None, ALU.add).then_inc(c_ne.sem, 1)
                    c_ne.wait(dve, s, 1)
                    c_nx.wait(dve, s, 0)
                    dve.reciprocal(rn8[0:r, 0:nt], n8[0:r, 0:nt]).then_inc(c_nr.sem, 1)
                elif key == "qsplit":
                    c_nt.wait(dve, s, 1)
                    c_qhi.wait(dve, s, 0)
                    dve.tensor_tensor(tokens(qs, s), tokens(halves(ps_g[1]), s), tokens(qf, s), ALU.mult).then_inc(c_qs.sem, 1)
                    c_qhi.wait(dve, s, 1)
                    lo_part(qTs, qs, s).then_inc(c_qlo.sem, 1)
                elif key == "ln2":
                    gchain.begin(s)
                    inc, wait = gchain.inc, lambda: gchain.wait(dve)
                    c_xs.wait(dve, s, 16)
                    dve.tensor_tensor(cut(xs, s), cut(xs, s), bout[0:r, :].rearrange("p (o c) -> p o c", o=1).broadcast_to([r, nt, D]),
                                      ALU.add).then_inc(c_xb.sem, 1)
                    c_xb.wait(dve, s, 1)
                    c_out.wait(dve, s, -16)
                    for t in range(nt):
                        c_o.wait(dve, s, t + 1)
                        dve.tensor_tensor(acc[0:r, v, t, :], halves(ps_out[t])[0:r, t, :], xs[0:r, t, :], ALU.add).then_inc(c_x1.sem, 1)
                        c_x1.wait(dve, s, t + 1)
                        inc(dve.bn_stats(gstat[0:r, t, :], acc[0:r, v, t, :]))
                    wait()
                    gate()
                    for t in range(nt):
                        inc(dve.bn_aggr(gmv[0:r, t, :], gstat[0:r, t, :]))
                    wait()
                    inc(dve.tensor_scalar(gv[0:r, 0:nt], gmv[0:r, 0:nt, 1], LN_EPS, None, ALU.add))
                    inc(dve.tensor_scalar(gvh[0:r, 0:nt], gmv[0:r, 0:nt, 1], LN_EPS, -0.5, ALU.add, ALU.mult))
                    wait()
                    c_tok.wait(dve, s, 0)
                    rsqrt_tiles(gv[0:r, 0:nt], gvh[0:r, 0:nt], gy[0:r, 0:nt], gt[0:r, 0:nt], inc, wait)
                    dve.scalar_tensor_tensor(out=gnm[0:r, 0:nt], in0=gmv[0:r, 0:nt, 0], scalar=-1.0, in1=gy[0:r, 0:nt],
                                             op0=ALU.mult, op1=ALU.mult).then_inc(c_ln.sem, 1)
                elif key == "toksplit":
                    c_khi.wait(dve, s, 1)
                    lo_part(tokT[:, v], halves(ps_g[0]), s).then_inc(c_klo.sem, 1)
                    c_tok.wait(dve, s, nt)
                    dve.tensor_tensor(cut(acc[:, v], s), cut(acc[:, v], s), cut(tok, s), ALU.add).then_inc(c_acc.sem, 1)
                elif key == "weigh":
                    inc, wait = gchain.inc, lambda: gchain.wait(dve)
                    c_lg.wait(dve, s, 1)
                    gate()
                    for t in range(nt):
                        inc(dve.max(top[0:r, t, :], ps_g[1][0:r, t * NE:(t + 1) * NE]))
                    wait()
                    gate()
                    for t in range(nt):
                        inc(dve.max_index(topi[0:r, t, :], top[0:r, t, :], ps_g[1][0:r, t * NE:(t + 1) * NE]))
                    dve.tensor_scalar(ntop[0:r, 0:nt], top[0:r, 0:nt, 0], -1.0, None, ALU.mult).then_inc(c_top.sem, 1)
                    wait()
                    inc(dve.tensor_copy(topf[0:r, 0:nt, :], topi[0:r, 0:nt, 0:2]))
                    c_et.wait(dve, s, 1)
                    inc(dve.reciprocal(erec[0:r, 0:nt], esum[0:r, 0:nt]))
                    wait()

                    def over(ap, n):
                        return ap[0:r, 0:nt].rearrange("p (t o) -> p t o", o=1).broadcast_to([r, nt, n])

                    inc(dve.tensor_tensor(prob[0:r, 0:nt, :], etop[0:r, 0:nt, 0:2], over(erec, 2), ALU.mult))
                    wait()
                    for t in range(nt):
                        inc(dve.tensor_scalar(pden[0:r, t:t + 1], prob[0:r, t, 0:1], prob[0:r, t, 1:2], 1e-12, ALU.add, ALU.max))
                    wait()
                    inc(dve.reciprocal(prec[0:r, 0:nt], pden[0:r, 0:nt]))
                    wait()
                    inc(dve.tensor_tensor(wtop[0:r, 0:nt, :], prob[0:r, 0:nt, :], over(prec, 2), ALU.mult))
                    wait()
                    for n, pick in enumerate((pick0, pick1)):
                        for t in range(nt):
                            inc(dve.tensor_scalar(pick[0:r, t, :], iota8[0:r, :], topf[0:r, t, n:n + 1], wtop[0:r, t, n:n + 1],
                                                  ALU.is_equal, ALU.mult))
                    wait()
                    c_ct.wait(dve, s, -1)
                    dve.tensor_tensor(comb[0:r, v, 0:nt, :], pick0[0:r, 0:nt, :], pick1[0:r, 0:nt, :], ALU.add).then_inc(c_comb.sem, 1)
                    assert nt < SUPER or gchain.k == G_CHAIN, gchain.k

            split_mix(0, 0)
            split_mix(1, 1)
            mix_program(dve, mix_tile, weight_beside, stage)
            features_mix(TILES - 1, (TILES - 1) % 2)
            dve.wait_ge(s_kva, TILES)
            for k in range(KH):
                dve.tensor_tensor(kvm[:, k, :], ps_kva[k][:, 0:P], headmask[:, :], ALU.mult)
                last = dve.tensor_copy(ksum[:, k:k + 1], ps_kva[k][:, P:P + 1])
            last.then_inc(s_kvx, 1)
            dve.wait_ge(s_kvx, 1)
            for k in range(KH):
                dve.tensor_scalar(ksm[:, k, :], headmask[:, ::HD], ksum[:, k:k + 1], None, ALU.mult).then_inc(s_kvx, 1)
            dve.wait_ge(s_kvy, 1)
            dve.tensor_copy(kvmT[:, :, :], ps_g[0][:, 0:KH * P].rearrange("p (k c) -> p k c", k=KH)).then_inc(s_kvx, 1)
            dve.wait_ge(s_kvz, 1)
            dve.tensor_tensor(kvwo[:, 1, :, :], halves(ps_g[1]), kvwo[:, 0, :, :].bitcast(F32), ALU.subtract).then_inc(s_kvx, 1)

            main_program(dve, stage)


def kernel(x, src, dst, edge_attr_16, L0_gnn_W1, L0_gnn_b1, L0_gnn_W2, L0_gnn_b2, L0_gnn_eps, L0_mix_wq, L0_mix_bq,
           L0_mix_wk, L0_mix_bk, L0_mix_wv, L0_mix_bv, L0_mix_wo, L0_mix_bo, L0_ffn_router_w, L0_ffn_w1, L0_ffn_b1,
           L0_ffn_w2, L0_ffn_b2):
    import numpy as np
    import concourse.bacc as bacc
    from concourse.bass_utils import run_bass_kernel_spmd

    def columns(v):
        return np.ascontiguousarray(np.asarray(v).reshape(-1, KH, P).transpose(2, 0, 1))

    src_p = np.zeros(EDGES, np.int32)
    src_p[:E] = np.asarray(src)
    dst_p = np.full(EDGES, NO_NODE, np.int32)
    dst_p[:E] = np.asarray(dst)
    arrays = {
        "x": np.asarray(x), "src": src_p, "dst": dst_p,
        "last_dst": np.ascontiguousarray(dst_p[:CHUNKS * P].reshape(CHUNKS, P)[:, P - 1].reshape(1, CHUNKS)),
        "wq": np.asarray(L0_mix_wq), "wk": np.asarray(L0_mix_wk), "wv": np.asarray(L0_mix_wv), "wo": np.asarray(L0_mix_wo),
        "wg1": np.asarray(L0_gnn_W1), "wg2": np.asarray(L0_gnn_W2), "we1": np.asarray(L0_ffn_w1), "we2": np.asarray(L0_ffn_w2),
        "bk": np.asarray(L0_mix_bk).reshape(1, D), "bv": np.asarray(L0_mix_bv).reshape(1, D),
        "bo": np.asarray(L0_mix_bo).reshape(1, D), "bg2": np.asarray(L0_gnn_b2).reshape(1, D),
        "eps": np.asarray(L0_gnn_eps).reshape(1, 1), "be2": np.asarray(L0_ffn_b2),
        "bq": columns(L0_mix_bq).reshape(P, KH), "bg1": columns(L0_gnn_b1).reshape(P, KH), "be1": columns(L0_ffn_b1),
        "wr": np.ascontiguousarray(np.asarray(L0_ffn_router_w).reshape(NE, KH, P).transpose(2, 1, 0)),
    }
    nc = bacc.Bacc("TRN2", target_bir_lowering=False, num_devices=1)
    aps = {k: nc.dram_tensor(f"in_{k}", list(a.shape), mybir.dt.from_np(a.dtype), kind="ExternalInput").ap()
           for k, a in arrays.items()}
    out = nc.dram_tensor("out", [N, D], F32, kind="ExternalOutput").ap()
    gps_layer(nc, aps["x"], aps["src"], aps["dst"], aps, out)
    r = run_bass_kernel_spmd(nc, [{f"in_{k}": a for k, a in arrays.items()}], core_ids=[0])
    return r.results[0]["out"]
```
